# Optimizing a Trainium2 kernel written in Bass

```python
import numpy as np
import jax
import jax.numpy as jnp

def _softmax(x, axis=-1):
    return jax.nn.softmax(x, axis=axis)

def _gelu(x):
    return jax.nn.gelu(x, approximate=True)

def _silu(x):
    return jax.nn.silu(x)

def _sigmoid(x):
    return jax.nn.sigmoid(x)

def _layernorm(x, axis=-1, eps=1e-05):
    m = jnp.mean(x, axis=axis, keepdims=True)
    v = jnp.var(x, axis=axis, keepdims=True)
    return (x - m) / jnp.sqrt(v + eps)

def _scatter_add(tgt, idx, src, axis=0):
    return tgt.at[idx].add(src)

def _segment_sum(src, seg, n):
    return jax.ops.segment_sum(src, seg, n)
kernel_name = 'mk_flamingo_gated_d2_seqx_r8_16743d'

def setup_inputs(seed: int=0):
    np.random.seed(seed)
    _w = jnp.asarray

    def _rec_inputs():
        import jax
        import jax.numpy as jnp
        _rk = jax.random.key(seed)
        x = -0.0002928 + 1 * jax.random.normal(jax.random.fold_in(_rk, 1), (64, 64, 128), jnp.float32)
        _lenS = 64 - jax.random.randint(jax.random.fold_in(_rk, 7), (64,), 0, max(1, 64 // 4) + 1, jnp.int32)
        _lenS2 = 64 - jax.random.randint(jax.random.fold_in(_rk, 8), (64,), 0, max(1, 64 // 4) + 1, jnp.int32)
        _ctx_1024P = jax.random.normal(jax.random.fold_in(_rk, 11), (64, 16, 128), jnp.float32)
        _ctx_1024c = jax.random.dirichlet(jax.random.fold_in(_rk, 511), 0.3 * jnp.ones((16,), jnp.float32), (64, 64))
        _ctx_1024t = jnp.einsum('bsk,bkd->bsd', _ctx_1024c, _ctx_1024P)
        _ctx_1024t = _ctx_1024t * jax.lax.rsqrt(jnp.mean(jnp.square(_ctx_1024t)) + 1e-12) * 0.953939
        ctx_1024 = -1.39393e-06 + 0.999914 * (_ctx_1024t + 0.3 * jax.random.normal(jax.random.fold_in(_rk, 611), (64, 64, 128), jnp.float32))
        _g = jax.random.normal(jax.random.fold_in(_rk, 9001), (2, 2), jnp.float32)
        _g = jnp.sign(_g) * jnp.maximum(jnp.abs(_g), 1.0) + (_g == 0) * 1.0
        g_xattn = _g[0]
        g_ffn = _g[1]
        return (x, ctx_1024, g_xattn, g_ffn)
    x, ctx_1024, g_xattn, g_ffn = _rec_inputs()

    def _L0_xattn_setup():
        import jax, jax.numpy as jnp
        import numpy as np
        import math
        EMBED_DIM = 128
        NUM_HEADS = 16
        HEAD_DIM = EMBED_DIM // NUM_HEADS
        BLOCK = 64
        SPARSITY = 0.05
        BATCH = 2
        SEQ = 256

        def _block_pattern(seq_len, block_size, sparsity_ratio, is_causal):
            nb = seq_len // block_size
            total = nb * nb
            keep = int(total * (1.0 - sparsity_ratio))
            idx = [(i, i) for i in range(nb)]
            band = max(1, int(math.sqrt(keep - nb) / 2))
            for i in range(nb):
                for o in range(1, band + 1):
                    if i + o < nb:
                        idx.append((i, i + o))
                        if not is_causal:
                            idx.append((i + o, i))
                    if not is_causal and i - o >= 0:
                        idx.append((i, i - o))
            for skip in (2, 4, 8, 16):
                if len(idx) >= keep:
                    break
                for i in range(0, nb - skip, skip):
                    if len(idx) < keep:
                        idx.append((i, i + skip))
                        if not is_causal and len(idx) < keep:
                            idx.append((i + skip, i))
            uniq = sorted(set(idx))
            if is_causal:
                uniq = [(r, c) for r, c in uniq if r >= c]
            uniq = uniq[:keep]
            rows = np.array([r for r, c in uniq], dtype=np.int32)
            cols = np.array([c for r, c in uniq], dtype=np.int32)
            return (rows, cols)
        ROWS, COLS = _block_pattern(SEQ, BLOCK, SPARSITY, is_causal=False)
        rng = jax.random.key(seed)
        ks = jax.random.split(rng, 7)
        wscale = EMBED_DIM ** (-0.5)
        return {'query': jax.random.normal(ks[0], (BATCH, SEQ, EMBED_DIM), jnp.float32), 'key': jax.random.normal(ks[1], (BATCH, SEQ, EMBED_DIM), jnp.float32), 'value': jax.random.normal(ks[2], (BATCH, SEQ, EMBED_DIM), jnp.float32), 'Wq': jax.random.normal(ks[3], (EMBED_DIM, EMBED_DIM), jnp.float32) * wscale, 'Wk': jax.random.normal(ks[4], (EMBED_DIM, EMBED_DIM), jnp.float32) * wscale, 'Wv': jax.random.normal(ks[5], (EMBED_DIM, EMBED_DIM), jnp.float32) * wscale, 'Wo': jax.random.normal(ks[6], (EMBED_DIM, EMBED_DIM), jnp.float32) * wscale}
    _L0_xattn_all = _L0_xattn_setup()
    _L0_xattn_in = {k: v for k, v in _L0_xattn_all.items() if k in ('Wq', 'Wk', 'Wv', 'Wo')}
    del _L0_xattn_all

    def _L0_ffn_setup():
        import jax, jax.numpy as jnp
        import numpy as np
        B, S, D, H, L, E, K = (4, 128, 128, 16, 2, 8, 2)
        DFF = 4 * D

        def _ln(x, w, b):
            m = x.mean(-1, keepdims=True)
            v = x.var(-1, keepdims=True)
            return (x - m) / jnp.sqrt(v + 1e-05) * w + b

        def _attn(x, wq, wk, wv, wo, bq, bk, bv, bo):
            Bb, T, C = x.shape
            hd = C // H
            q = (x @ wq + bq).reshape(Bb, T, H, hd).transpose(0, 2, 1, 3)
            k = (x @ wk + bk).reshape(Bb, T, H, hd).transpose(0, 2, 1, 3)
            v = (x @ wv + bv).reshape(Bb, T, H, hd).transpose(0, 2, 1, 3)
            att = jnp.einsum('bhqd,bhkd->bhqk', q, k) * hd ** (-0.5)
            causal = jnp.tril(jnp.ones((T, T), bool))
            att = jnp.where(causal, att, -jnp.inf)
            att = jax.nn.softmax(att, axis=-1)
            y = jnp.einsum('bhqk,bhkd->bhqd', att, v).transpose(0, 2, 1, 3).reshape(Bb, T, C)
            return y @ wo + bo

        def _ffn(h, w1, b1, w2, b2):
            return jax.nn.gelu(h @ w1 + b1, approximate=False) @ w2 + b2

        def _combine_weights(logits):
            vals, idx = jax.lax.top_k(logits, K)
            w = jax.nn.softmax(vals, axis=-1)
            onehot = (idx[..., None] == jnp.arange(E)).astype(w.dtype)
            return jnp.sum(w[..., None] * onehot, axis=-2)

        def _token_moe(h, gw, gb, w1, b1, w2, b2):
            cw = _combine_weights(h @ gw + gb)
            out = jnp.zeros_like(h)
            for e in range(E):
                out = out + _ffn(h, w1[e], b1[e], w2[e], b2[e]) * cw[..., e:e + 1]
            return out

        def _seq_moe(h, gw, gb, w1, b1, w2, b2):
            cw = _combine_weights(h.mean(axis=1) @ gw + gb)
            out = jnp.zeros_like(h)
            for e in range(E):
                out = out + _ffn(h, w1[e], b1[e], w2[e], b2[e]) * cw[:, e, None, None]
            return out
        key = jax.random.key(seed)
        ks = jax.random.split(key, 9)
        n = lambda k, shp: jax.random.normal(k, shp, dtype=jnp.float32) * 0.02
        return {'x': jax.random.normal(ks[0], (B, S, D), dtype=jnp.float32), 'ln1_w': jnp.ones((L, D), jnp.float32), 'ln1_b': jnp.zeros((L, D), jnp.float32), 'ln2_w': jnp.ones((L, D), jnp.float32), 'ln2_b': jnp.zeros((L, D), jnp.float32), 'wq': n(ks[1], (L, D, D)), 'wk': n(ks[2], (L, D, D)), 'wv': n(ks[3], (L, D, D)), 'wo': n(ks[4], (L, D, D)), 'bq': jnp.zeros((L, D), jnp.float32), 'bk': jnp.zeros((L, D), jnp.float32), 'bv': jnp.zeros((L, D), jnp.float32), 'bo': jnp.zeros((L, D), jnp.float32), 'gate_w': n(ks[5], (L, D, E)), 'gate_b': jnp.zeros((L, E), jnp.float32), 'e_w1': n(ks[6], (L, E, D, DFF)), 'e_b1': jnp.zeros((L, E, DFF), jnp.float32), 'e_w2': n(ks[7], (L, E, DFF, D)), 'e_b2': jnp.zeros((L, E, D), jnp.float32)}
    _L0_ffn_all = _L0_ffn_setup()
    _L0_ffn_in = {k: v for k, v in _L0_ffn_all.items() if k in ('ln1_w', 'ln1_b', 'ln2_w', 'ln2_b', 'wq', 'wk', 'wv', 'wo', 'bq', 'bk', 'bv', 'bo', 'gate_w', 'gate_b', 'e_w1', 'e_b1', 'e_w2', 'e_b2')}
    del _L0_ffn_all

    def _L1_xattn_setup():
        import jax, jax.numpy as jnp
        import numpy as np
        DIM = 128
        HEADS = 8
        HEAD_DIM = DIM // HEADS
        TAU = HEAD_DIM ** 0.5
        BS, SEQ = (1, 256)
        key = jax.random.key(seed)
        kq, kk, kv, kb = jax.random.split(key, 4)
        q = jax.random.normal(kq, (BS, SEQ, DIM), jnp.float32)
        k = jax.random.normal(kk, (BS, SEQ, DIM), jnp.float32)
        v = jax.random.normal(kv, (BS, SEQ, DIM), jnp.float32)
        Wi_w = jnp.zeros((HEADS, 3 * DIM), jnp.float32)
        Wi_b = 0.1 * jax.random.normal(kb, (HEADS,), jnp.float32)
        Wf_w = jnp.zeros((HEADS, 3 * DIM), jnp.float32)
        Wf_b = jnp.linspace(3.0, 6.0, HEADS, dtype=jnp.float32)
        gn_w = jnp.ones((DIM,), jnp.float32)
        gn_b = jnp.zeros((DIM,), jnp.float32)
        return {'q': q, 'k': k, 'v': v, 'Wi_w': Wi_w, 'Wi_b': Wi_b, 'Wf_w': Wf_w, 'Wf_b': Wf_b, 'gn_w': gn_w, 'gn_b': gn_b}
    _L1_xattn_all = _L1_xattn_setup()
    _L1_xattn_in = {k: v for k, v in _L1_xattn_all.items() if k in ('Wi_w', 'Wi_b', 'Wf_w', 'Wf_b', 'gn_w', 'gn_b')}
    del _L1_xattn_all

    def _L1_ffn_setup():
        import jax, jax.numpy as jnp
        import numpy as np
        EPS = 1e-05
        key = jax.random.key(seed)
        kx, kw, kb = jax.random.split(key, 3)
        B, S, K, N = (8, 1024, 128, 128)
        x = jax.random.normal(kx, (B, S, K), dtype=jnp.float32)
        W = jax.random.normal(kw, (N, K), dtype=jnp.float32) * 0.02
        weight_scale = jnp.maximum(jnp.max(jnp.abs(W), axis=1, keepdims=True) / 127.0, EPS)
        weight_int8 = jnp.clip(jnp.round(W / weight_scale), -128, 127).astype(jnp.int8)
        bias = jax.random.normal(kb, (N,), dtype=jnp.float32) * 0.01
        return {'x': x, 'weight_int8': weight_int8, 'weight_scale': weight_scale, 'bias': bias}
    _L1_ffn_all = _L1_ffn_setup()
    _L1_ffn_in = {k: v for k, v in _L1_ffn_all.items() if k in ('weight_int8', 'weight_scale', 'bias')}
    del _L1_ffn_all
    return {'x': x, 'ctx_1024': ctx_1024, 'g_xattn': g_xattn, 'g_ffn': g_ffn, 'L0_xattn_Wq': _L0_xattn_in['Wq'], 'L0_xattn_Wk': _L0_xattn_in['Wk'], 'L0_xattn_Wv': _L0_xattn_in['Wv'], 'L0_xattn_Wo': _L0_xattn_in['Wo'], 'L0_ffn_ln1_w': _L0_ffn_in['ln1_w'], 'L0_ffn_ln1_b': _L0_ffn_in['ln1_b'], 'L0_ffn_ln2_w': _L0_ffn_in['ln2_w'], 'L0_ffn_ln2_b': _L0_ffn_in['ln2_b'], 'L0_ffn_wq': _L0_ffn_in['wq'], 'L0_ffn_wk': _L0_ffn_in['wk'], 'L0_ffn_wv': _L0_ffn_in['wv'], 'L0_ffn_wo': _L0_ffn_in['wo'], 'L0_ffn_bq': _L0_ffn_in['bq'], 'L0_ffn_bk': _L0_ffn_in['bk'], 'L0_ffn_bv': _L0_ffn_in['bv'], 'L0_ffn_bo': _L0_ffn_in['bo'], 'L0_ffn_gate_w': _L0_ffn_in['gate_w'], 'L0_ffn_gate_b': _L0_ffn_in['gate_b'], 'L0_ffn_e_w1': _L0_ffn_in['e_w1'], 'L0_ffn_e_b1': _L0_ffn_in['e_b1'], 'L0_ffn_e_w2': _L0_ffn_in['e_w2'], 'L0_ffn_e_b2': _L0_ffn_in['e_b2'], 'L1_xattn_Wi_w': _L1_xattn_in['Wi_w'], 'L1_xattn_Wi_b': _L1_xattn_in['Wi_b'], 'L1_xattn_Wf_w': _L1_xattn_in['Wf_w'], 'L1_xattn_Wf_b': _L1_xattn_in['Wf_b'], 'L1_xattn_gn_w': _L1_xattn_in['gn_w'], 'L1_xattn_gn_b': _L1_xattn_in['gn_b'], 'L1_ffn_weight_int8': _L1_ffn_in['weight_int8'], 'L1_ffn_weight_scale': _L1_ffn_in['weight_scale'], 'L1_ffn_bias': _L1_ffn_in['bias']}

def reference(x, ctx_1024, g_xattn, g_ffn, L0_xattn_Wq, L0_xattn_Wk, L0_xattn_Wv, L0_xattn_Wo, L0_ffn_ln1_w, L0_ffn_ln1_b, L0_ffn_ln2_w, L0_ffn_ln2_b, L0_ffn_wq, L0_ffn_wk, L0_ffn_wv, L0_ffn_wo, L0_ffn_bq, L0_ffn_bk, L0_ffn_bv, L0_ffn_bo, L0_ffn_gate_w, L0_ffn_gate_b, L0_ffn_e_w1, L0_ffn_e_b1, L0_ffn_e_w2, L0_ffn_e_b2, L1_xattn_Wi_w, L1_xattn_Wi_b, L1_xattn_Wf_w, L1_xattn_Wf_b, L1_xattn_gn_w, L1_xattn_gn_b, L1_ffn_weight_int8, L1_ffn_weight_scale, L1_ffn_bias):
    import jax
    import jax.numpy as jnp

    def _L0_xattn_ref(query, key, value, Wq, Wk, Wv, Wo):
        import jax, jax.numpy as jnp
        import numpy as np
        import math
        EMBED_DIM = 128
        NUM_HEADS = 16
        HEAD_DIM = EMBED_DIM // NUM_HEADS
        BLOCK = 64
        SPARSITY = 0.05
        BATCH = 2
        SEQ = 256

        def _block_pattern(seq_len, block_size, sparsity_ratio, is_causal):
            nb = seq_len // block_size
            total = nb * nb
            keep = int(total * (1.0 - sparsity_ratio))
            idx = [(i, i) for i in range(nb)]
            band = max(1, int(math.sqrt(keep - nb) / 2))
            for i in range(nb):
                for o in range(1, band + 1):
                    if i + o < nb:
                        idx.append((i, i + o))
                        if not is_causal:
                            idx.append((i + o, i))
                    if not is_causal and i - o >= 0:
                        idx.append((i, i - o))
            for skip in (2, 4, 8, 16):
                if len(idx) >= keep:
                    break
                for i in range(0, nb - skip, skip):
                    if len(idx) < keep:
                        idx.append((i, i + skip))
                        if not is_causal and len(idx) < keep:
                            idx.append((i + skip, i))
            uniq = sorted(set(idx))
            if is_causal:
                uniq = [(r, c) for r, c in uniq if r >= c]
            uniq = uniq[:keep]
            rows = np.array([r for r, c in uniq], dtype=np.int32)
            cols = np.array([c for r, c in uniq], dtype=np.int32)
            return (rows, cols)
        ROWS, COLS = _block_pattern(SEQ, BLOCK, SPARSITY, is_causal=False)
        B, S, E = query.shape
        nb = S // BLOCK
        scale = HEAD_DIM ** (-0.5)

        def proj_blocks(x, W):
            h = (x @ W.T).reshape(B, S, NUM_HEADS, HEAD_DIM).transpose(0, 2, 1, 3)
            return h.reshape(B, NUM_HEADS, nb, BLOCK, HEAD_DIM)
        qb = proj_blocks(query, Wq)
        kb = proj_blocks(key, Wk)
        vb = proj_blocks(value, Wv)
        rows = jnp.asarray(ROWS)
        cols = jnp.asarray(COLS)
        qg = qb[:, :, rows]
        kg = kb[:, :, cols]
        vg = vb[:, :, cols]
        scores = jnp.einsum('bhpqd,bhpkd->bhpqk', qg, kg) * scale
        attn = jax.nn.softmax(scores, axis=-1)
        ob = jnp.einsum('bhpqk,bhpkd->bhpqd', attn, vg)
        acc = jax.ops.segment_sum(ob.transpose(2, 0, 1, 3, 4), rows, num_segments=nb)
        out = acc.transpose(1, 2, 0, 3, 4).reshape(B, NUM_HEADS, S, HEAD_DIM)
        out = out.transpose(0, 2, 1, 3).reshape(B, S, E)
        return out @ Wo.T

    def _L0_ffn_ref(x, ln1_w, ln1_b, ln2_w, ln2_b, wq, wk, wv, wo, bq, bk, bv, bo, gate_w, gate_b, e_w1, e_b1, e_w2, e_b2):
        import jax, jax.numpy as jnp
        import numpy as np
        B, S, D, H, L, E, K = (4, 128, 128, 16, 2, 8, 2)
        DFF = 4 * D

        def _ln(x, w, b):
            m = x.mean(-1, keepdims=True)
            v = x.var(-1, keepdims=True)
            return (x - m) / jnp.sqrt(v + 1e-05) * w + b

        def _attn(x, wq, wk, wv, wo, bq, bk, bv, bo):
            Bb, T, C = x.shape
            hd = C // H
            q = (x @ wq + bq).reshape(Bb, T, H, hd).transpose(0, 2, 1, 3)
            k = (x @ wk + bk).reshape(Bb, T, H, hd).transpose(0, 2, 1, 3)
            v = (x @ wv + bv).reshape(Bb, T, H, hd).transpose(0, 2, 1, 3)
            att = jnp.einsum('bhqd,bhkd->bhqk', q, k) * hd ** (-0.5)
            causal = jnp.tril(jnp.ones((T, T), bool))
            att = jnp.where(causal, att, -jnp.inf)
            att = jax.nn.softmax(att, axis=-1)
            y = jnp.einsum('bhqk,bhkd->bhqd', att, v).transpose(0, 2, 1, 3).reshape(Bb, T, C)
            return y @ wo + bo

        def _ffn(h, w1, b1, w2, b2):
            return jax.nn.gelu(h @ w1 + b1, approximate=False) @ w2 + b2

        def _combine_weights(logits):
            vals, idx = jax.lax.top_k(logits, K)
            w = jax.nn.softmax(vals, axis=-1)
            onehot = (idx[..., None] == jnp.arange(E)).astype(w.dtype)
            return jnp.sum(w[..., None] * onehot, axis=-2)

        def _token_moe(h, gw, gb, w1, b1, w2, b2):
            cw = _combine_weights(h @ gw + gb)
            out = jnp.zeros_like(h)
            for e in range(E):
                out = out + _ffn(h, w1[e], b1[e], w2[e], b2[e]) * cw[..., e:e + 1]
            return out

        def _seq_moe(h, gw, gb, w1, b1, w2, b2):
            cw = _combine_weights(h.mean(axis=1) @ gw + gb)
            out = jnp.zeros_like(h)
            for e in range(E):
                out = out + _ffn(h, w1[e], b1[e], w2[e], b2[e]) * cw[:, e, None, None]
            return out
        for l in range(L):
            x = x + _attn(_ln(x, ln1_w[l], ln1_b[l]), wq[l], wk[l], wv[l], wo[l], bq[l], bk[l], bv[l], bo[l])
            h = _ln(x, ln2_w[l], ln2_b[l])
            moe = _token_moe if l % 2 == 0 else _seq_moe
            x = x + moe(h, gate_w[l], gate_b[l], e_w1[l], e_b1[l], e_w2[l], e_b2[l])
        return x

    def _L1_xattn_ref(q, k, v, Wi_w, Wi_b, Wf_w, Wf_b, gn_w, gn_b):
        import jax, jax.numpy as jnp
        import numpy as np
        DIM = 128
        HEADS = 8
        HEAD_DIM = DIM // HEADS
        TAU = HEAD_DIM ** 0.5
        BS, SEQ = (1, 256)
        bs, seq, dim = q.shape
        gate_in = jnp.concatenate([q, k, v], axis=-1)
        itilde = jnp.einsum('bsd,hd->bhs', gate_in, Wi_w) + Wi_b[None, :, None]
        ftilde = jnp.einsum('bsd,hd->bhs', gate_in, Wf_w) + Wf_b[None, :, None]
        csum = jnp.cumsum(jax.nn.log_sigmoid(ftilde), axis=-1)
        Fmat = csum[..., :, None] - csum[..., None, :]
        mask = jnp.tril(jnp.ones((seq, seq), dtype=bool))
        F_act = jnp.where(mask, Fmat, -jnp.inf)
        Dtilde = F_act + itilde[..., None, :]
        max_d = jnp.max(Dtilde, axis=-1, keepdims=True)
        D = jnp.exp(Dtilde - max_d)
        qh = q.reshape(bs, seq, HEADS, HEAD_DIM).transpose(0, 2, 1, 3)
        kh = k.reshape(bs, seq, HEADS, HEAD_DIM).transpose(0, 2, 1, 3)
        vh = v.reshape(bs, seq, HEADS, HEAD_DIM).transpose(0, 2, 1, 3)
        Ctilde = jnp.einsum('bhid,bhjd->bhij', qh, kh) * D / TAU
        maxit = jnp.maximum(jnp.abs(jnp.sum(Ctilde, axis=-1, keepdims=True)), jnp.exp(-max_d))
        Htilde = jnp.einsum('bhij,bhjd->bhid', Ctilde, vh) / (maxit + 1e-06)
        x = Htilde.transpose(0, 2, 1, 3).reshape(bs * seq, HEADS, HEAD_DIM)
        mean = jnp.mean(x, axis=-1, keepdims=True)
        var = jnp.var(x, axis=-1, keepdims=True)
        xn = (x - mean) / jnp.sqrt(var + 1e-05)
        out = xn.reshape(bs * seq, DIM) * gn_w + gn_b
        return out.reshape(bs, seq, DIM)

    def _L1_ffn_ref(x, weight_int8, weight_scale, bias):
        import jax, jax.numpy as jnp
        import numpy as np
        EPS = 1e-05
        B, S, K = x.shape
        x2 = x.reshape(-1, K)
        x_scale = jnp.maximum(jnp.abs(x2).max() / 127.0, EPS)
        x_int8 = jnp.clip(jnp.round(x2 / x_scale), -128, 127).astype(jnp.int8)
        acc_i32 = jax.lax.dot_general(x_int8, weight_int8.T, dimension_numbers=(((1,), (0,)), ((), ())), preferred_element_type=jnp.int32)
        out = acc_i32.astype(jnp.float32) * x_scale * weight_scale.T
        out = out + bias
        return out.reshape(B, S, -1)
    x = x + jnp.tanh(g_xattn[0]) * _L0_xattn_ref(_layernorm(x, axis=-1), ctx_1024, ctx_1024, L0_xattn_Wq, L0_xattn_Wk, L0_xattn_Wv, L0_xattn_Wo)
    x = x + jnp.tanh(g_ffn[0]) * _L0_ffn_ref(_layernorm(x, axis=-1), L0_ffn_ln1_w, L0_ffn_ln1_b, L0_ffn_ln2_w, L0_ffn_ln2_b, L0_ffn_wq, L0_ffn_wk, L0_ffn_wv, L0_ffn_wo, L0_ffn_bq, L0_ffn_bk, L0_ffn_bv, L0_ffn_bo, L0_ffn_gate_w, L0_ffn_gate_b, L0_ffn_e_w1, L0_ffn_e_b1, L0_ffn_e_w2, L0_ffn_e_b2)
    x = x + jnp.tanh(g_xattn[1]) * _L1_xattn_ref(_layernorm(x, axis=-1), ctx_1024, ctx_1024, L1_xattn_Wi_w, L1_xattn_Wi_b, L1_xattn_Wf_w, L1_xattn_Wf_b, L1_xattn_gn_w, L1_xattn_gn_b)
    x = x + jnp.tanh(g_ffn[1]) * _L1_ffn_ref(_layernorm(x, axis=-1), L1_ffn_weight_int8, L1_ffn_weight_scale, L1_ffn_bias)
    return x

_drawn_inputs = setup_inputs


def setup_inputs(seed=0):
    import zlib

    import numpy as np

    out = dict(_drawn_inputs(seed))
    spreads = {'g_ffn': (-1.0, 0.6),
     'L0_ffn_ln1_w': (1.0, 0.2),
     'L0_ffn_ln1_b': (0.0, 0.293),
     'L0_ffn_ln2_w': (1.0, 0.2),
     'L0_ffn_ln2_b': (0.0, 0.1),
     'L0_ffn_bq': (0.0, 0.8),
     'L0_ffn_bk': (0.0, 2.0),
     'L0_ffn_bv': (0.0, 0.1),
     'L0_ffn_bo': (0.0, 0.1),
     'L0_ffn_gate_b': (0.0, 0.1),
     'L0_ffn_e_b1': (0.0, 0.1),
     'L0_ffn_e_b2': (0.0, 0.1),
     'L1_xattn_Wi_w': (0.0, 0.1),
     'L1_xattn_Wf_w': (0.0, 0.1),
     'L1_xattn_gn_w': (1.0, 0.2),
     'L1_xattn_gn_b': (0.0, 0.1)}
    factors = {'L0_ffn_wq': 8.0, 'L0_ffn_wk': 8.0, 'L1_xattn_Wi_b': 61.618, 'L1_ffn_bias': 7.14}
    for name, (base, spread) in spreads.items():
        noise = np.random.default_rng([zlib.crc32(name.encode()), seed]).standard_normal(out[name].shape)
        drawn = base * np.exp(spread * noise) if base else spread * noise
        out[name] = jnp.asarray(drawn.astype(out[name].dtype))
    for name, factor in factors.items():
        out[name] = (out[name] * factor).astype(out[name].dtype)
    return out
```

```python
from contextlib import ExitStack

import concourse.bass as bass
from concourse import mybir

P = 128
NSEQ, SEQ, D = 64, 64, 128
TOK = NSEQ * SEQ
NT = TOK // P
SPT = P // SEQ
HEADS, HD = 16, 8
MH, MHD = 8, 16
NE, DFF = 8, 512
CH = DFF // P
BLK = 512
NB = TOK // BLK
SUB = BLK // P
LAYERS = 2
EPS = 1e-5
NEG = -1e30
MAGIC = 12582912.0
ROW0_PAIRS = 3.0

F32 = mybir.dt.float32
BF16 = mybir.dt.bfloat16
I8 = mybir.dt.int8
U32 = mybir.dt.uint32
I32 = mybir.dt.int32
ALU = mybir.AluOpType
ACT = mybir.ActivationFunctionType
AXX = mybir.AxisListType.X


def seen(eng, sem, value):
    if isinstance(value, int) and value <= 0:
        return
    eng.wait_ge(sem, value)


def capped(value, most):
    return min(value, most) if isinstance(value, int) else value


def arrived(t, par, each):
    return (t - par) * (each // 2) + each


def pipeline(eng, steps, n=NT):
    last = max(lag for lag, _ in steps)
    head = (last + 2) // 2 * 2
    for i in range(head):
        for lag, fn in steps:
            if i - lag >= 0:
                fn(i - lag, (i - lag) % 2)
    with eng.Fori(head // 2, n // 2, 1) as pair:
        i0 = pair * 2
        for u in range(2):
            for lag, fn in steps:
                fn(i0 + (u - lag), (u - lag) % 2)
    for i in range(n, n + last):
        for lag, fn in steps:
            if i - lag < n:
                fn(i - lag, (i - lag) % 2)


def build(nc, A, out):
    with ExitStack() as ctx:
        def sb(name, shape, dt=F32):
            return ctx.enter_context(nc.sbuf_tensor(name, shape, dt))

        def psum(name, cols):
            return ctx.enter_context(nc.psum_tensor(name, [P, cols], F32))

        def sem(name):
            return ctx.enter_context(nc.semaphore(name))

        def tile(buf, t):
            return buf[:, bass.ds(t * P, P)]

        x_res = sb("x_res", [P, NT * D])
        inner = sb("inner", [P, NT * D])
        h_t = sb("h_t", [P, TOK])
        w1 = sb("w1", [P, NE, DFF])
        w2 = sb("w2", [P, NE, CH, D])
        wraw = sb("wraw", [P, 4, D])
        wx = sb("wx", [P, 4, D])
        wself = sb("wself", [P, LAYERS, 4, D])
        gatew = sb("gatew", [P, LAYERS, NE])
        vecs = sb("vecs", [78, D])
        vec_t = sb("vec_t", [P, 78])
        wg_raw = sb("wg_raw", [2 * MH, 3, D])
        wg_t = sb("wg_t", [P, 3, 2 * MH])
        w8 = sb("w8", [P, D // 4], I32)
        w8f = sb("w8f", [P, D])
        w8t = sb("w8t", [P, D], BF16)
        rows = sb("rows", [1, 1024])
        rowb = sb("rowb", [P, 5 * D + 16])
        tg = sb("tg", [P, 4])
        coef = sb("coef", [P, 4])
        b2src = sb("b2src", [3, NE, D])
        b2a = sb("b2a", [3, NE, D])
        b2hi = sb("b2hi", [3, NE, D], BF16)
        b2mid = sb("b2mid", [3, NE, D], BF16)
        b2lo = sb("b2lo", [3, NE, D], BF16)
        b2rows = sb("b2rows", [3, NE, SUB, D], BF16)
        ident = sb("ident", [P, P])
        identb = sb("identb", [P, P], BF16)
        ones_row = sb("ones_row", [1, P])
        ones3 = sb("ones3", [3, P], BF16)
        kmask = sb("kmask", [P, 8, P])
        kmask4 = sb("kmask4", [P, 4, P])
        vmask = sb("vmask", [P, SPT * HEADS, HD])
        vmask16 = sb("vmask16", [P, SPT * MH, MHD])
        causal = sb("causal", [P, 8, SEQ], BF16)
        block_ones = sb("block_ones", [P, P])
        block_tri = sb("block_tri", [P, P])
        delta = sb("delta", [P, MH, SEQ])
        row3 = sb("row3", [3, 3])
        mhalf = sb("mhalf", [P, 16])
        iota8 = sb("iota8", [P, NT, NE])
        pair_sel = sb("pair_sel", [NSEQ, P])
        pair_int = sb("pair_int", [NSEQ, P], I32)
        seq_tile = sb("seq_tile", [NSEQ, NT, NE])
        stats = sb("stats", [P, 2, 6])
        mv = sb("mv", [P, 2, 2])
        vare = sb("vare", [P, 2])
        rstd = sb("rstd", [P, 2])
        xn = sb("xn", [P, 2, D])
        xts = sb("xts", [P, 2, P])
        cts = sb("cts", [P, 2, P])
        ctx_in = sb("ctx_in", [P, 2, D])
        ctx_dup = sb("ctx_dup", [P, 2, SPT, D])
        qts = sb("qts", [P, 2, P])
        kts = sb("kts", [P, 2, P])
        kbd = sb("kbd", [P, 2, 8, P])
        vbd = sb("vbd", [P, 2, SPT, HEADS, HD + 1])
        vbd16 = sb("vbd16", [P, 2, SPT, MH, MHD + 1])
        rowmax = sb("rowmax", [P, 2, HEADS])
        work = sb("work", [P, 2 * CH * BLK])
        shifted = work[:, 0:2048].rearrange("p (b n) -> p b n", b=2)
        probs = work[:, 2048:4096].rearrange("p (b n) -> p b n", b=2)
        gel = work[:, :].rearrange("p (b c n) -> p b c n", b=2, c=CH)
        probs_t = sb("probs_t", [P, 2, 1024])
        recip = sb("recip", [P, 2, HEADS])
        y = sb("y", [P, 2, D])
        yts = sb("yts", [P, 2, P])
        logits = sb("logits", [P, NT, NE])
        cand = sb("cand", [P, NT, NE])
        first = sb("first", [P, NT])
        best1 = sb("best1", [P, NT])
        best2 = sb("best2", [P, NT])
        e21 = sb("e21", [P, NT])
        tw1 = sb("tw1", [P, NT])
        tw2 = sb("tw2", [P, NT])
        oneh = sb("oneh", [P, NT, NE])
        cw = sb("cw", [P, NT, NE])
        hmean = sb("hmean", [P, NSEQ])
        cwrep = sb("cwrep", [NSEQ, NT, NE])
        gates = sb("gates", [P, 2, 16])
        gtmp = sb("gtmp", [P, 2, 8])
        gexp = sb("gexp", [P, 2, 8])
        gln = sb("gln", [P, 2, 8])
        lsig = sb("lsig", [P, 2, 8])
        csum = sb("csum", [P, 2, 8])
        avec = sb("avec", [P, 2, 8])
        adiag = shifted[:, :, 512:1024].rearrange("p b (h k) -> p b h k", k=SEQ)
        negmd = sb("negmd", [P, 2, 8])
        emd = sb("emd", [P, 2, 8])
        rs = sb("rs", [P, 2, 8])
        rs2 = sb("rs2", [P, 2, 8])
        rs3 = sb("rs3", [P, 2, 8])
        gsum = sb("gsum", [P, 2, 8])
        gvar = sb("gvar", [P, 2, 8])
        gve = sb("gve", [P, 2, 8])
        grstd = sb("grstd", [P, 2, 8])
        ysq = sb("ysq", [P, 2, D])
        yc = sb("yc", [P, 2, D])
        yn = sb("yn", [P, 2, D])
        ctil = sb("ctil", [P, 2, 512])
        amax = sb("amax", [P, 1])
        amrow = sb("amrow", [1, P])
        am1 = sb("am1", [1, 2])
        xscale = sb("xscale", [P, 2])
        qa = sb("qa", [P, 2, D])
        qb = sb("qb", [P, 2, D])
        q8 = sb("q8", [P, 2, D], BF16)
        q8t = sb("q8t", [P, 2, P], BF16)
        o1 = sb("o1", [P, 2, D])
        o2 = sb("o2", [P, 2, D])
        o3 = sb("o3", [P, 2, D])

        ps_s = psum("ps_s", 1024)
        ps_t = psum("ps_t", 1024)
        ps_o = psum("ps_o", 512)
        ps_x = psum("ps_x", 512)
        ps_a = psum("ps_a", 512)
        ps_v = psum("ps_v", 512)
        ps_s3 = ps_s[:, :].rearrange("p (r n) -> p r n", r=2)

        names = """x_loaded weights_loaded ffn_w_loaded ffn_w_free pool_const ident_ready setup_t setup_copied dve_setup
        bn_done stats_ready vare_ready rstd_ready xn_ready xt_ready xts_ready ctx_used
        proj_ready qk_ready kbd_ready vbd_ready scores_ready max_ready shifted_ready probs_ready
        pt_ready pts_ready o_ready recip_ready y_ready yt_ready yts_ready outp_ready x_updated
        ht_stored logits_ps logits_sb route_link route_exp route_done hmean_ready seqlog_ready seq_cw cw_ps
        hid_ready gelu_ready yexp_ready acc_ready gates_ps gates_sb nabs_ready gexp_ready gln_ready lsig_ready
        csum_ps csum_sb avec_ready adiag_ready a_ready d_ready ctil_ready negmd_ready emd_ready
        vb16_ready rs_link gn_link gve_ready grstd_ready yn_ready yb_ready fin_link amax_ready amrow_ps
        amrow_done scale_ps scale_ready q8_ready q8t_ps q8t_ready acc8_ready o1_ready o2_ready o3_ready
        ctx0_loaded ctx1_loaded dup0_loaded dup1_loaded out0_stored out1_stored out_left"""
        S = {n: sem(n) for n in names.split()}
        ctx_loaded = [S["ctx0_loaded"], S["ctx1_loaded"]]
        dup_loaded = [S["dup0_loaded"], S["dup1_loaded"]]
        out_stored = [S["out0_stored"], S["out1_stored"]]

        CROSS, NORM0, SELF0, PRE0, SELF1, PRE1, MLSTM, NORM1 = (k * NT for k in range(8))
        ATT = {"x": 0, 0: NT, 1: 2 * NT, "m": 3 * NT}
        TB = {"x": 0, 0: NT, "p0": 2 * NT, 1: 3 * NT, "p1": 4 * NT, "m": 5 * NT}
        UPD = {"x": 0, 0: NT, 1: 2 * NT, "add": 3 * NT, "m": 3 * NT + 1}

        x_v = A["x"].rearrange("(t s) i d -> (s i) t d", s=SPT)
        ctx_v = A["ctx_1024"].rearrange("(t s) i d -> t (s i) d", s=SPT)
        ctxd_v = A["ctx_1024"].rearrange("(t s) i d -> t i s d", s=SPT)
        out_v = out.rearrange("(t s) i d -> t (s i) d", s=SPT)

        CONSTS = []
        block = ctx.enter_context(nc.Block())

        ROUTE_EXP = 12
        ROUTE_LINKS = (ROUTE_EXP + 5, ROUTE_EXP + 6)
        B2_LINKS = 7 + SUB
        GN_LINKS = 11

        def ROUTE_AT(l, k):
            return sum(ROUTE_LINKS[:l]) + k

        q8ps = ps_x[:, :].bitcast(BF16)[:, 0:P]

        def vec(kind, l):
            c = 2 * kind + l
            return vec_t[:, c:c + 1]

        def b1col(l, e, c):
            k = 14 + (l * NE + e) * CH + c
            return vec_t[:, k:k + 1]

        R_GNW, R_GNB, R_WS, R_B1, R_GB1, R_G = 0, D, 2 * D, 3 * D, 4 * D, 4 * D + 8
        R_BO, R_GI, R_GB0 = 4 * D + 16, 6 * D + 16, 6 * D + 32
        row_loads = [("L1_xattn_gn_w", R_GNW), ("L1_xattn_gn_b", R_GNB), ("L1_ffn_weight_scale", R_WS),
                     ("L1_ffn_bias", R_B1), ("g_xattn", R_G), ("g_ffn", R_G + 2), ("L1_xattn_Wi_b", R_GI),
                     ("L1_xattn_Wf_b", R_GI + 8)]
        small_loads = []
        for name, at in row_loads:
            ap = A[name]
            n = 1
            for s_ in ap.shape:
                n *= s_
            flat = ap.rearrange("a b -> (b a)") if len(ap.shape) == 2 else ap
            small_loads.append((rows[0:1, at:at + n], flat.rearrange("(a n) -> a n", a=1)))
        small_loads.append((rows[0:1, R_GB1:R_GB1 + 8], A["L0_ffn_gate_b"][1:2, :]))
        small_loads.append((rows[0:1, R_GB0:R_GB0 + 8], A["L0_ffn_gate_b"][0:1, :]))
        for l in range(LAYERS):
            small_loads.append((rows[0:1, R_BO + l * D:R_BO + (l + 1) * D], A["L0_ffn_bo"][l:l + 1, :]))
        for k, name in enumerate(("ln1_w", "ln1_b", "ln2_w", "ln2_b", "bq", "bk", "bv")):
            small_loads.append((vecs[2 * k:2 * k + 2, :], A["L0_ffn_" + name]))
        small_loads.append((vecs[14:78, :], A["L0_ffn_e_b1"].rearrange("l e (c p) -> (l e c) p", p=P)))
        for k, name in enumerate(("Wq", "Wk", "Wv", "Wo")):
            small_loads.append((wraw[:, k, :], A["L0_xattn_" + name]))
            for l in range(LAYERS):
                small_loads.append((wself[:, l, k, :], A["L0_ffn_" + name.lower()][l, :, :]))
        for l in range(LAYERS):
            small_loads.append((gatew[:, l, :], A["L0_ffn_gate_w"][l, :, :]))
        small_loads.append((wg_raw[0:MH, :, :], A["L1_xattn_Wi_w"].rearrange("h (k d) -> h k d", k=3)))
        small_loads.append((wg_raw[MH:2 * MH, :, :], A["L1_xattn_Wf_w"].rearrange("h (k d) -> h k d", k=3)))
        small_loads.append((w8[:, :], A["L1_ffn_weight_int8"]))
        N_WLOADS = len(small_loads)

        @block.sync
        def _(sp):
            sp.dma_start(x_res[:, :].rearrange("p (t d) -> p t d", d=D), x_v).then_inc(S["x_loaded"], 16)
            for dst, src in small_loads[:N_WLOADS // 2]:
                sp.dma_start(dst, src).then_inc(S["weights_loaded"], 16)

            def ctx_load(base):
                def fn(t, par):
                    if base:
                        seen(sp, S["vb16_ready"], t - 1)
                    else:
                        seen(sp, S["ctx_used"], t - 1)
                    sp.dma_start(ctx_in[:, par, :], ctx_v[bass.ds(t, 1), :, :].rearrange("a p d -> p (a d)")
                                 ).then_inc(ctx_loaded[par], 16)
                    if base:
                        for g in range(2):
                            sp.dma_start(ctx_dup[g * SEQ:(g + 1) * SEQ, par, :, :],
                                         ctxd_v[bass.ds(t, 1), :, :, :].rearrange("a i s d -> i (a s) d")
                                         ).then_inc(dup_loaded[par], 16)
                return fn

            def expert_load(l):
                if l:
                    sp.wait_ge(S["yexp_ready"], NB * NE)
                sp.dma_start(w1[:, :, :], A["L0_ffn_e_w1"][l, :, :, :].rearrange("e d f -> d e f")
                             ).then_inc(S["ffn_w_loaded"], 16)
                sp.dma_start(w2[:, :, :, :], A["L0_ffn_e_w2"][l, :, :, :].rearrange("e (c p) d -> p e c d", p=P)
                             ).then_inc(S["ffn_w_loaded"], 16)
                for r in range(3):
                    sp.dma_start(b2src[r:r + 1, :, :], A["L0_ffn_e_b2"][l:l + 1, :, :]
                                 ).then_inc(S["ffn_w_loaded"], 16)

            pipeline(sp, [(0, ctx_load(0))])
            expert_load(0)
            expert_load(1)
            pipeline(sp, [(0, ctx_load(NT))])

            def store(t, par):
                sp.wait_ge(S["o3_ready"], t + 1)
                sp.dma_start(out_v[bass.ds(t, 1), :, :].rearrange("a p d -> p (a d)"), o3[:, par, :]
                             ).then_inc(out_stored[par], 16)
            pipeline(sp, [(0, store)])
            for par in range(2):
                sp.wait_ge(out_stored[par], 16 * (NT // 2))

        @block.gpsimd
        def _(pool):
            n = [0]

            def fresh(ins):
                n[0] += 1
                ins.then_inc(S["pool_const"], 1)
                pool.wait_ge(S["pool_const"], n[0])

            def select(ap, pattern, base, mult, cmp=ALU.is_ge, fill=0.0):
                fresh(pool.affine_select(out=ap, in_=ap, compare_op=cmp, fill=fill, base=base,
                                         pattern=pattern, channel_multiplier=mult))

            fresh(pool.memset(ident[:, :], 0.0))
            select(ident[:, :], [[-1, P]], 0, 1, ALU.not_equal, 1.0)
            fresh(pool.memset(identb[:, :], 0.0))
            select(identb[:, :], [[-1, P]], 0, 1, ALU.not_equal, 1.0)
            fresh(pool.memset(ones_row[:, :], 1.0))
            fresh(pool.memset(ones3[:, :], 1.0))
            fresh(pool.memset(mhalf[:, :], -0.5))
            for buf, hh, hd in ((kmask, 8, HD), (kmask4, 4, MHD)):
                for half in range(2):
                    part = buf[half * 64:(half + 1) * 64, :, :]
                    fresh(pool.memset(part, 1.0))
                    select(part, [[-hd, hh], [0, P]], 0, 1)
                    select(part, [[hd, hh], [0, P]], hd - 1, -1)
            for buf, hd in ((vmask, HD), (vmask16, MHD)):
                v = buf[:, :, :].rearrange("p (n g) d -> p n g d", g=2)
                fresh(pool.memset(buf[:, :, :], 0.0))
                for half in range(2):
                    fresh(pool.memset(v[half * 64:(half + 1) * 64, :, half, :], 1.0))
            fresh(pool.memset(vbd[:, :, :, :, :], 1.0))
            fresh(pool.memset(vbd16[:, :, :, :, :], 1.0))
            for buf, nh, hd in ((vbd, HEADS, HD), (vbd16, MH, MHD)):
                for half in range(2):
                    for par in range(2):
                        v = buf[half * 64:(half + 1) * 64, par, :, :, hd:hd + 1].rearrange(
                            "p s (n g) o -> p s n g o", g=2)[:, :, :, 1 - half, :]
                        fresh(pool.memset(v, 0.0))
            fresh(pool.memset(causal[:, :, :], 0.0))
            for half in range(2):
                part = causal[half * 64:(half + 1) * 64, :, :]
                select(part, [[0, 8], [-1, SEQ]], 0, 1, ALU.is_ge, NEG)
            fresh(pool.memset(block_ones[:, :], 0.0))
            fresh(pool.memset(block_tri[:, :], 0.0))
            fresh(pool.memset(delta[:, :, :], 0.0))
            for half in range(2):
                a, b = half * 64, (half + 1) * 64
                fresh(pool.memset(block_ones[a:b, a:b], 1.0))
                fresh(pool.memset(block_tri[a:b, a:b], 1.0))
                select(block_tri[a:b, a:b], [[1, 64]], 0, -1)
                select(delta[a:b, :, :], [[0, MH], [-1, SEQ]], 0, 1, ALU.not_equal, 1.0)
            fresh(pool.memset(row3[:, :], 0.0))
            select(row3[:, :], [[-1, 3]], 0, 1, ALU.not_equal, 1.0)
            fresh(pool.iota(iota8[:, :, :], pattern=[[0, NT], [1, NE]], base=0, channel_multiplier=0,
                            allow_small_or_imprecise_dtypes=True))
            fresh(pool.iota(pair_int[:, :], pattern=[[1, SPT], [0, SEQ]], base=1, channel_multiplier=1))
            fresh(pool.memset(seq_tile[:, :, :], 1.0))
            select(seq_tile[:, :, :], [[-2, NT], [0, NE]], 0, 1)
            select(seq_tile[:, :, :], [[2, NT], [0, NE]], 1, -1)
            CONSTS.append(n[0])

            def rstd_step(base):
                def fn(t, par):
                    pool.wait_ge(S["vare_ready"], base + t + 1)
                    pool.tensor_tensor(rstd[:, par:par + 1], vare[:, par:par + 1], mhalf[:, 0:1], ALU.pow
                                       ).then_inc(S["rstd_ready"], 1)
                return fn

            def kbd_step(base):
                def fn(t, par):
                    pool.wait_ge(S["qk_ready"], base + t + 1)
                    seen(pool, S["scores_ready"], base + t - 1)
                    pool.tensor_tensor(kbd[:, par, :, :], kts[:, par:par + 1, :].to_broadcast([P, 8, P]),
                                       kmask[:, :, :], ALU.mult).then_inc(S["kbd_ready"], 1)
                return fn

            def ht_step(base):
                def fn(t, par):
                    pool.wait_ge(S["xts_ready"], TB[base] + t + 1)
                    pool.tensor_copy(tile(h_t, t), xts[:, par, :]).then_inc(S["ht_stored"], 1)
                return fn

            pipeline(pool, [(0, rstd_step(CROSS)), (2, kbd_step(ATT["x"]))])
            pipeline(pool, [(0, rstd_step(NORM0))])
            for l in range(LAYERS):
                pipeline(pool, [(0, rstd_step((SELF0, SELF1)[l])), (2, kbd_step(ATT[l]))])
                if l:
                    pool.wait_ge(S["yexp_ready"], NB * NE)
                pipeline(pool, [(0, rstd_step((PRE0, PRE1)[l])), (1, ht_step(f"p{l}"))])

            def kbd16_step(t, par):
                pool.wait_ge(S["xts_ready"], TB["m"] + t + 1)
                seen(pool, S["scores_ready"], ATT["m"] + t - 1)
                pool.tensor_tensor(kbd[:, par, 0:4, :], cts[:, par:par + 1, :].to_broadcast([P, 4, P]),
                                   kmask4[:, :, :], ALU.mult).then_inc(S["kbd_ready"], 1)

            def vbd16_step(t, par):
                pool.wait_ge(dup_loaded[par], arrived(t, par, 32))
                seen(pool, S["o_ready"], ATT["m"] + t - 1)
                pool.tensor_tensor(vbd16[:, par, :, :, 0:MHD].rearrange("p s h d -> p (s h) d"),
                                   ctx_dup[:, par, :, :].rearrange("p s (h d) -> p (s h) d", d=MHD),
                                   vmask16[:, :, :], ALU.mult).then_inc(S["vb16_ready"], 1)

            def adiag_step(t, par):
                pool.wait_ge(S["avec_ready"], t + 1)
                seen(pool, S["a_ready"], t - 1)
                pool.tensor_tensor(adiag[:, par, :, :], avec[:, par, :].unsqueeze(2).to_broadcast([P, MH, SEQ]),
                                   delta[:, :, :], ALU.mult).then_inc(S["adiag_ready"], 1)

            def grstd_step(t, par):
                pool.wait_ge(S["gve_ready"], t + 1)
                pool.tensor_tensor(grstd[:, par, :], gve[:, par, :], mhalf[:, 0:MH], ALU.pow
                                   ).then_inc(S["grstd_ready"], 1)

            def ybias_step(t, par):
                pool.wait_ge(S["yn_ready"], t + 1)
                seen(pool, S["x_updated"], UPD["m"] + t - 1)
                pool.tensor_tensor(ysq[:, par, :], yn[:, par, :], rowb[:, R_GNB:R_GNB + D], ALU.add
                                   ).then_inc(S["yb_ready"], 1)

            pipeline(pool, [(0, rstd_step(MLSTM)), (2, adiag_step), (1, kbd16_step), (2, vbd16_step),
                            (4, grstd_step), (4, ybias_step)])
            pipeline(pool, [(0, rstd_step(NORM1))])

            def o2_step(t, par):
                pool.wait_ge(S["o1_ready"], t + 1)
                seen(pool, S["o3_ready"], t - 1)
                pool.tensor_tensor(o2[:, par, :], o1[:, par, :], rowb[:, R_B1:R_B1 + D], ALU.add
                                   ).then_inc(S["o2_ready"], 1)
            pipeline(pool, [(0, o2_step)])

        @block.scalar
        def _(act):
            for dst, src in small_loads[N_WLOADS // 2:]:
                act.dma_start(dst, src).then_inc(S["weights_loaded"], 16)
            k = [0]

            def copied(dst, src):
                k[0] += 1
                act.wait_ge(S["setup_t"], k[0])
                nc.scalar.copy(dst, src).then_inc(S["setup_copied"], 1)
            copied(wx[:, :, :].rearrange("p a d -> p (a d)"), ps_s[:, 0:4 * D])
            copied(vec_t[:, :], ps_t[:, 0:78])
            copied(wg_t[:, :, :].rearrange("p a d -> p (a d)"), ps_o[:, 0:48])
            copied(rowb[:, 0:512], ps_a[:, 0:512])
            copied(rowb[:, 512:524], ps_v[:, 0:12])
            copied(w8t[:, :], ps_x[:, 0:P])
            act.wait_ge(S["setup_copied"], 5)
            nc.scalar.activation(tg[:, :], rowb[:, R_G:R_G + 4], ACT.Tanh).then_inc(S["setup_copied"], 1)

            def evac_t(base, l, vk, both):
                def fn(t, par):
                    act.wait_ge(S["xt_ready"], TB[base] + t + 1)
                    if base in ("x", 0, 1):
                        seen(act, S["proj_ready"], ATT[base] + t - 1)
                    elif base == "m":
                        seen(act, S["scores_ready"], ATT["m"] + t - 1)
                        seen(act, S["gates_ps"], t - 1)
                        seen(act, S["kbd_ready"], ATT["m"] + t - 1)
                    else:
                        seen(act, S["ht_stored"], int(base[1]) * NT + t - 1)
                        if base == "p0":
                            seen(act, S["logits_ps"], t - 1)
                    if vk is None:
                        i = nc.scalar.copy(xts[:, par, :], ps_x[:, 0:P])
                    else:
                        i = nc.scalar.activation(xts[:, par, :], ps_x[:, 0:P], ACT.Identity,
                                                 bias=vec(vk + 1, l), scale=vec(vk, l))
                    if both:
                        i = nc.scalar.copy(cts[:, par, :], ps_x[:, P:2 * P])
                    i.then_inc(S["xts_ready"], 1)
                return fn

            def evac_qk(base, l):
                def fn(t, par):
                    act.wait_ge(S["proj_ready"], ATT[base] + t + 1)
                    seen(act, S["scores_ready"], ATT[base] + t - 1)
                    seen(act, S["kbd_ready"], ATT[base] + t - 1)
                    if l is None:
                        nc.scalar.copy(qts[:, par, :], ps_a[:, 0:P])
                        i = nc.scalar.copy(kts[:, par, :], ps_a[:, P:2 * P])
                    else:
                        nc.scalar.activation(qts[:, par, :], ps_a[:, 0:P], ACT.Identity, bias=vec(4, l))
                        i = nc.scalar.activation(kts[:, par, :], ps_a[:, P:2 * P], ACT.Identity, bias=vec(5, l))
                    i.then_inc(S["qk_ready"], 1)
                return fn

            def exp_step(base):
                def fn(t, par):
                    act.wait_ge(S["shifted_ready"], ATT[base] + t + 1)
                    seen(act, S["pt_ready"], ATT[base] + t - 1)
                    nc.scalar.activation(probs[:, par, :], shifted[:, par, :], ACT.Exp, scale=HD ** -0.5
                                         ).then_inc(S["probs_ready"], 1)
                return fn

            def evac_pt(base, width):
                def fn(t, par):
                    act.wait_ge(S["pt_ready"], ATT[base] + t + 1)
                    seen(act, S["o_ready"], ATT[base] + t - 1)
                    nc.scalar.copy(probs_t[:, par, 0:width], ps_t[:, 0:width]).then_inc(S["pts_ready"], 1)
                return fn

            def evac_yt(base, l):
                def fn(t, par):
                    act.wait_ge(S["yt_ready"], ATT[base] + t + 1)
                    seen(act, S["outp_ready"], ATT[base] + t - 1)
                    if l is None:
                        i = nc.scalar.copy(yts[:, par, :], ps_a[:, 0:P])
                    else:
                        i = nc.scalar.activation(yts[:, par, :], ps_a[:, 0:P], ACT.Identity, bias=vec(6, l))
                    i.then_inc(S["yts_ready"], 1)
                return fn

            def attention(base, l):
                pipeline(act, [(4, evac_pt(base, 1024)), (2, evac_qk(base, l)), (3, exp_step(base)),
                               (1, evac_t(base, l, None if l is None else 0, l is None)), (5, evac_yt(base, l))])

            def gelu_block(l):
                def fn(b, par):
                    for e in range(NE):
                        for c in range(CH):
                            k = c + 1 + e * CH
                            act.wait_ge(S["hid_ready"], l * NB * NE * CH + b * (NE * CH) + k)
                            if c == 0:
                                seen(act, S["yexp_ready"], l * NB * NE + b * NE + (e - 1))
                            nc.scalar.activation(gel[:, e % 2, c, :], (ps_s, ps_t)[c // 2][:, (c % 2) * BLK:(c % 2 + 1) * BLK],
                                                 ACT.Gelu, bias=b1col(l, e, c)).then_inc(S["gelu_ready"], 1)
                return fn

            attention("x", None)
            for l in range(LAYERS):
                attention(l, l)
                pipeline(act, [(1, evac_t(f"p{l}", l, 2, False))])
                act.wait_ge(S["route_link"], ROUTE_AT(l, ROUTE_EXP))
                nr = (P, NSEQ)[l]
                nt = (NT, 1)[l]
                nc.scalar.activation(e21[0:nr, 0:nt], e21[0:nr, 0:nt], ACT.Exp).then_inc(S["route_exp"], 1)
                fn = gelu_block(l)
                fn(0, 0)
                with act.Fori(1, NB, 1) as b:
                    fn(b, 0)

            def gate_exp(t, par):
                act.wait_ge(S["nabs_ready"], t + 1)
                nc.scalar.activation(gexp[:, par, :], gtmp[:, par, :], ACT.Exp).then_inc(S["gexp_ready"], 1)
                act.wait_ge(S["gexp_ready"], t + 1)
                nc.scalar.activation(gln[:, par, :], gexp[:, par, :], ACT.Ln, bias=1.0).then_inc(S["gln_ready"], 1)

            def decay_exp(t, par):
                act.wait_ge(S["shifted_ready"], ATT["m"] + t + 1)
                seen(act, S["ctil_ready"], t - 1)
                nc.scalar.activation(probs[:, par, 0:512], shifted[:, par, 0:512], ACT.Exp).then_inc(S["d_ready"], 1)
                act.wait_ge(S["negmd_ready"], t + 1)
                seen(act, S["yn_ready"], t - 1)
                nc.scalar.activation(emd[:, par, :], negmd[:, par, :], ACT.Exp).then_inc(S["emd_ready"], 1)

            pipeline(act, [(4, evac_pt("m", 512)), (1, evac_t("m", None, None, True)), (2, gate_exp), (3, decay_exp)])

            act.wait_ge(S["amrow_ps"], 1)
            nc.scalar.copy(amrow[:, :], ps_a[0:1, 0:P]).then_inc(S["amrow_done"], 1)

            def evac_q8(t, par):
                act.wait_ge(S["q8t_ps"], t + 1)
                seen(act, S["acc8_ready"], t - 1)
                nc.scalar.copy(q8t[:, par, :], q8ps[:, :]).then_inc(S["q8t_ready"], 1)
            pipeline(act, [(1, evac_q8)])

        @block.tensor
        def _(pe):
            pe.wait_ge(S["pool_const"], CONSTS[0])
            pe.wait_ge(S["weights_loaded"], 16 * N_WLOADS)

            def mm(o, a, b, start=True, stop=True):
                return nc.tensor.matmul(o, a, b, start=start, stop=stop, skip_group_check=True)

            for k in range(4):
                i = nc.tensor.transpose(ps_s[:, k * D:(k + 1) * D], wraw[:, k, :], ident[:, :])
            i.then_inc(S["setup_t"], 1)
            nc.tensor.transpose(ps_t[:, 0:78], vecs[:, :], ident[0:78, 0:78]).then_inc(S["setup_t"], 1)
            for k in range(3):
                i = nc.tensor.transpose(ps_o[:, k * 16:(k + 1) * 16], wg_raw[:, k, :], ident[0:16, 0:16])
            i.then_inc(S["setup_t"], 1)
            mm(ps_a[:, 0:512], ones_row[:, :], rows[:, 0:512]).then_inc(S["setup_t"], 1)
            mm(ps_v[:, 0:12], ones_row[:, :], rows[:, 512:524]).then_inc(S["setup_t"], 1)
            pe.wait_ge(S["dve_setup"], 1)
            nc.tensor.transpose(ps_x[:, 0:P], w8f[:, :], ident[:, :]).then_inc(S["setup_t"], 1)
            pe.wait_ge(S["setup_copied"], 7)

            def ctx_transpose(base, before):
                def fn(t, par):
                    seen(pe, S["xts_ready"], TB[base] + t)
                    pe.wait_ge(ctx_loaded[par], (8 * NT if base == "m" else 0) + arrived(t, par, 16))
                    if not isinstance(t, int):
                        before(t)
                    nc.tensor.transpose(ps_x[:, P:2 * P], ctx_in[:, par, :], ident[:, :]).then_inc(S["ctx_used"], 1)
                return fn

            def transposes(base, nbase):
                def fn(t, par):
                    pe.wait_ge(S["xn_ready"], nbase + t + 1)
                    seen(pe, S["xts_ready"], TB[base] + t)
                    nc.tensor.transpose(ps_x[:, 0:P], xn[:, par, :], ident[:, :]).then_inc(S["xt_ready"], 1)
                return fn

            def project(base, l):
                w = (lambda k: wx[:, k, :]) if l is None else (lambda k: wself[:, l, k, :])

                def fn(t, par):
                    kv = cts if l is None else xts
                    pe.wait_ge(S["xts_ready"], TB[base] + t + 1)
                    seen(pe, S["yts_ready"], ATT[base] + t - 3)
                    seen(pe, S["qk_ready"], ATT[base] + t)
                    mm(ps_a[:, 0:P], w(0), xts[:, par, :])
                    mm(ps_a[:, P:2 * P], w(1), kv[:, par, :])
                    seen(pe, S["x_updated"], UPD[base] + t - 3)
                    seen(pe, S["vbd_ready"], ATT[base] + t)
                    for s in range(SPT):
                        for g in range(2):
                            i = mm(ps_v[g * SEQ:(g + 1) * SEQ, s * D:(s + 1) * D],
                                   kv[:, par, s * SEQ:(s + 1) * SEQ], w(2))
                    i.then_inc(S["proj_ready"], 1)
                return fn

            def scores_need(base, t):
                pe.wait_ge(S["qk_ready"], ATT[base] + t + 1)
                pe.wait_ge(S["kbd_ready"], ATT[base] + t + 1)
                seen(pe, S["shifted_ready"], ATT[base] + t)

            def scores(base, masked):
                def fn(t, par):
                    if masked or isinstance(t, int):
                        scores_need(base, t)
                    if masked:
                        for r in range(2):
                            mm(ps_s3[:, r, :], identb[:, :], causal[:, :, :].rearrange("p a b -> p (a b)"),
                               True, False)
                    for s in range(SPT):
                        for r in range(2):
                            i = mm(ps_s3[s * 64:(s + 1) * 64, r, :],
                                   qts[r * 64:(r + 1) * 64, par, s * SEQ:(s + 1) * SEQ],
                                   kbd[r * 64:(r + 1) * 64, par, :, s * SEQ:(s + 1) * SEQ], not masked, True)
                    i.then_inc(S["scores_ready"], 1)
                return fn

            def transpose_probs(base, n, src):
                def fn(t, par):
                    if base == "m":
                        pe.wait_ge(S["ctil_ready"], t + 1)
                    else:
                        pe.wait_ge(S["probs_ready"], ATT[base] + t + 1)
                    seen(pe, S["pts_ready"], ATT[base] + t)
                    for j in range(n):
                        i = nc.tensor.transpose(ps_t[:, j * P:(j + 1) * P], src[:, par, j * P:(j + 1) * P], ident[:, :])
                    i.then_inc(S["pt_ready"], 1)
                return fn

            def weigh(base, buf, nh, hd):
                def fn(t, par):
                    pe.wait_ge(S["pts_ready"], ATT[base] + t + 1)
                    if base == "m":
                        pe.wait_ge(S["vb16_ready"], t + 1)
                        seen(pe, S["y_ready"], ATT[base] + t)
                    else:
                        pe.wait_ge(S["vbd_ready"], ATT[base] + t + 1)
                        seen(pe, S["y_ready"], ATT[base] + t)
                    o = ps_o[:, 0:SPT * nh * (hd + 1)].rearrange("p (s n) -> p s n", s=SPT)
                    for j in range(nh // 2):
                        a = 2 * j * (hd + 1)
                        i = mm(o[:, :, a:a + 2 * (hd + 1)], probs_t[:, par, j * P:(j + 1) * P],
                               buf[:, par, :, 2 * j:2 * j + 2, :].rearrange("p s h d -> p s (h d)"))
                    i.then_inc(S["o_ready"], 1)
                return fn

            def transpose_y(base):
                def fn(t, par):
                    pe.wait_ge(S["y_ready"], ATT[base] + t + 1)
                    pe.wait_ge(S["qk_ready"], ATT[base] + capped(t + 4, NT))
                    seen(pe, S["yts_ready"], ATT[base] + t)
                    nc.tensor.transpose(ps_a[:, 0:P], y[:, par, :], ident[:, :]).then_inc(S["yt_ready"], 1)
                return fn

            def out_project(base, l):
                def fn(t, par):
                    pe.wait_ge(S["yts_ready"], ATT[base] + t + 1)
                    pe.wait_ge(S["vbd_ready"], ATT[base] + capped(t + 4, NT))
                    seen(pe, S["x_updated"], UPD[base] + t)
                    if l is None:
                        i = mm(ps_v[:, 0:D], yts[:, par, :], wx[:, 3, :])
                    else:
                        mm(ps_v[:, 0:D], yts[:, par, :], wself[:, l, 3, :], True, False)
                        i = mm(ps_v[:, 0:D], ones_row[:, :], rows[:, R_BO + l * D:R_BO + (l + 1) * D], False, True)
                    i.then_inc(S["outp_ready"], 1)
                return fn

            def attention(base, l, nbase):
                early = [] if l is not None else [(1, ctx_transpose(base, lambda t: scores_need(base, t - 2)))]
                pipeline(pe, early + [(3, scores(base, l is not None)), (4, transpose_probs(base, HEADS // 2, probs)),
                                      (2, project(base, l)), (1, transposes(base, nbase)),
                                      (4, weigh(base, vbd, HEADS, HD)), (5, transpose_y(base)),
                                      (5, out_project(base, l))])

            def logits_step(t, par):
                pe.wait_ge(S["xts_ready"], TB["p0"] + t + 1)
                seen(pe, S["logits_sb"], t)
                mm(ps_a[:, 0:NE], xts[:, par, :], gatew[:, 0, :], True, False)
                mm(ps_a[:, 0:NE], ones_row[:, :], rows[:, R_GB0:R_GB0 + NE], False, True
                   ).then_inc(S["logits_ps"], 1)

            def expert_block(l):
                def hidden(b, e):
                    for c in range(CH):
                        seen(pe, S["gelu_ready"], l * NB * NE * CH + b * (NE * CH) + (e - 1) * CH + c + 1)
                        mm((ps_s, ps_t)[c // 2][:, (c % 2) * BLK:(c % 2 + 1) * BLK], w1[:, e, c * P:(c + 1) * P],
                           h_t[:, bass.ds(b * BLK, BLK)]).then_inc(S["hid_ready"], 1)

                def second(b, e):
                    bank = (ps_o, ps_v)[e % 2]
                    seen(pe, S["acc_ready"], l * NB * NE + b * NE + (e - 1))
                    mm(bank[:, :], ones3[:, :], b2rows[:, e, :, :].rearrange("p s d -> p (s d)"), True, False)
                    for c in range(CH):
                        pe.wait_ge(S["gelu_ready"], l * NB * NE * CH + b * (NE * CH) + e * CH + c + 1)
                        for s in range(SUB):
                            i = mm(bank[:, s * D:(s + 1) * D], gel[:, e % 2, c, s * P:(s + 1) * P],
                                   w2[:, e, c, :], False, c == CH - 1)
                    i.then_inc(S["yexp_ready"], 1)

                def fn(b, par):
                    hidden(b, 0)
                    for e in range(NE):
                        if e + 1 < NE:
                            hidden(b, e + 1)
                        second(b, e)
                return fn

            attention("x", None, CROSS)
            for l in range(LAYERS):
                attention(l, l, (SELF0, SELF1)[l])
                steps = [(1, transposes(f"p{l}", (PRE0, PRE1)[l]))]
                if l == 0:
                    steps.append((1, logits_step))
                pipeline(pe, steps)
                if l == 1:
                    pe.wait_ge(S["hmean_ready"], 1)
                    mm(ps_a[0:NSEQ, 0:NE], hmean[:, :], gatew[:, 1, :]).then_inc(S["seqlog_ready"], 1)
                    pe.wait_ge(S["seq_cw"], 1)
                    mm(ps_a[:, 0:NT * NE], pair_sel[:, :], cwrep[:, :, :].rearrange("q t e -> q (t e)")
                       ).then_inc(S["cw_ps"], 1)
                pe.wait_ge(S["ffn_w_loaded"], 16 * 5 * (l + 1))
                pe.wait_ge(S["route_done"], l + 1)
                pe.wait_ge(S["ht_stored"], NT * (l + 1))
                fn = expert_block(l)
                fn(0, 0)
                with pe.Fori(1, NB, 1) as b:
                    fn(b, 0)
                pe.wait_ge(S["acc_ready"], (l + 1) * NB * NE)

            def gates_step(t, par):
                pe.wait_ge(S["xts_ready"], TB["m"] + t + 1)
                seen(pe, S["csum_sb"], t)
                for k, a in enumerate((xts, cts, cts)):
                    mm(ps_a[:, 0:16], a[:, par, :], wg_t[:, k, :], k == 0, False)
                mm(ps_a[:, 0:16], ones_row[:, :], rows[:, R_GI:R_GI + 16], False, True).then_inc(S["gates_ps"], 1)

            def csum_step(t, par):
                pe.wait_ge(S["lsig_ready"], t + 1)
                mm(ps_a[:, 16:24], block_tri[:, :], lsig[:, par, :]).then_inc(S["csum_ps"], 1)

            def decay_step(t, par):
                pe.wait_ge(S["adiag_ready"], t + 1)
                seen(pe, S["shifted_ready"], ATT["m"] + t)
                mm(ps_t[:, 512:1024], identb[:, :], causal[:, :, :].rearrange("p a b -> p (a b)"), True, False)
                mm(ps_t[:, 512:1024], block_ones[:, :], adiag[:, par, :, :].rearrange("p a b -> p (a b)"),
                   False, True).then_inc(S["a_ready"], 1)

            def scores16_need(t):
                pe.wait_ge(S["kbd_ready"], ATT["m"] + t + 1)
                seen(pe, S["ctil_ready"], t)

            def scores16(t, par):
                if isinstance(t, int):
                    scores16_need(t)
                for s in range(SPT):
                    for r in range(2):
                        i = mm(ps_s3[s * 64:(s + 1) * 64, r, 0:4 * SEQ],
                               xts[r * 64:(r + 1) * 64, par, s * SEQ:(s + 1) * SEQ],
                               kbd[r * 64:(r + 1) * 64, par, 0:4, s * SEQ:(s + 1) * SEQ])
                i.then_inc(S["scores_ready"], 1)

            pipeline(pe, [(3, decay_step), (1, ctx_transpose("m", lambda t: scores16_need(t - 2))), (3, scores16),
                          (1, transposes("m", MLSTM)),
                          (4, weigh("m", vbd16, MH, MHD)), (2, csum_step), (1, gates_step),
                          (3, transpose_probs("m", MH // 2, ctil))])

            pe.wait_ge(S["amax_ready"], 1)
            nc.tensor.transpose(ps_a[0:1, 0:P], amax[:, :], ident[:, :]).then_inc(S["amrow_ps"], 1)
            pe.wait_ge(S["scale_ready"], 1)
            mm(ps_v[:, 0:1], ones_row[:, :], am1[:, 0:1]).then_inc(S["scale_ps"], 1)

            def q8_transpose(t, par):
                pe.wait_ge(S["q8_ready"], t + 1)
                seen(pe, S["q8t_ready"], t)
                nc.tensor.transpose(q8ps[:, :], q8[:, par, :], identb[:, :]).then_inc(S["q8t_ps"], 1)

            def q8_product(t, par):
                pe.wait_ge(S["q8t_ready"], t + 1)
                seen(pe, S["o1_ready"], t)
                mm(ps_o[:, 0:D], q8t[:, par, :], w8t[:, :]).then_inc(S["acc8_ready"], 1)
            pipeline(pe, [(1, q8_transpose), (2, q8_product)])

        @block.vector
        def _(dve):
            V = nc.vector
            dve.wait_ge(S["weights_loaded"], 16 * N_WLOADS)
            V.tensor_copy(w8f[:, :], w8[:, :].bitcast(I8)).then_inc(S["dve_setup"], 1)
            dve.wait_ge(S["setup_copied"], 7)
            V.tensor_scalar(coef[:, 0:1], tg[:, 0:1], ROW0_PAIRS, None, ALU.mult).then_inc(S["dve_setup"], 1)
            V.tensor_scalar(rowb[:, 0:2 * D], rowb[:, 0:2 * D], tg[:, 1:2], None, ALU.mult).then_inc(S["dve_setup"], 1)
            dve.wait_ge(S["dve_setup"], 3)
            dve.wait_ge(S["x_loaded"], 16)
            dve.wait_ge(S["pool_const"], CONSTS[0])
            V.tensor_scalar(pair_int[:, :], pair_int[:, :], 1, None, ALU.bitwise_and).then_inc(S["dve_setup"], 1)
            dve.wait_ge(S["dve_setup"], 4)
            V.tensor_copy(pair_sel[:, :], pair_int[:, :]).then_inc(S["dve_setup"], 1)

            def sums_step(src):
                def fn(t, par):
                    V.bn_stats(stats[:, par, :], tile(src, t)).then_inc(S["bn_done"], 1)
                return fn

            def stats_step(base):
                def fn(t, par):
                    if isinstance(t, int):
                        dve.wait_ge(S["bn_done"], base + t + 1)
                    V.bn_aggr(mv[:, par, :], stats[:, par, :]).then_inc(S["stats_ready"], 1)
                    dve.wait_ge(S["stats_ready"], base + t + 1)
                    V.tensor_scalar(vare[:, par:par + 1], mv[:, par, 1:2], EPS, None, ALU.add
                                    ).then_inc(S["vare_ready"], 1)
                return fn

            def norm_step(src, base, tb):
                def fn(t, par):
                    dve.wait_ge(S["bn_done"], base + capped(t + 2, NT))
                    dve.wait_ge(S["rstd_ready"], base + t + 1)
                    seen(dve, S["xt_ready"], TB[tb] + t - 1)
                    V.tensor_scalar(xn[:, par, :], tile(src, t), mv[:, par, 0:1], rstd[:, par:par + 1],
                                    ALU.subtract, ALU.mult).then_inc(S["xn_ready"], 1)
                return fn

            def vbd_step(base):
                def fn(t, par):
                    dve.wait_ge(S["proj_ready"], ATT[base] + t + 1)
                    seen(dve, S["o_ready"], ATT[base] + t - 1)
                    V.tensor_tensor(vbd[:, par, :, :, 0:HD].rearrange("p s h d -> p (s h) d"),
                                    ps_v[:, 0:2 * D].rearrange("p (n d) -> p n d", d=HD), vmask[:, :, :],
                                    ALU.mult).then_inc(S["vbd_ready"], 1)
                return fn

            def shift_step(base):
                def fn(t, par):
                    dve.wait_ge(S["scores_ready"], ATT[base] + t + 1)
                    s3 = ps_s[:, :].rearrange("p (h k) -> p h k", k=SEQ)
                    V.tensor_reduce(rowmax[:, par, :], s3, AXX, ALU.max).then_inc(S["max_ready"], 1)
                    dve.wait_ge(S["max_ready"], ATT[base] + t + 1)
                    seen(dve, S["probs_ready"], ATT[base] + t - 1)
                    V.tensor_tensor(shifted[:, par, :].rearrange("p (h k) -> p h k", k=SEQ), s3,
                                    rowmax[:, par, :].unsqueeze(2).to_broadcast([P, HEADS, SEQ]), ALU.subtract
                                    ).then_inc(S["shifted_ready"], 1)
                return fn

            def y_step(base):
                def fn(t, par):
                    dve.wait_ge(S["o_ready"], ATT[base] + t + 1)
                    seen(dve, S["yt_ready"], ATT[base] + t - 1)
                    o = ps_o[:, 0:SPT * HEADS * (HD + 1)].rearrange("p (s h d) -> p s h d", s=SPT, h=HEADS)
                    for s in range(SPT):
                        r = slice(64 * s, 64 * s + 64)
                        i = V.reciprocal(recip[r, par, :].unsqueeze(2), o[r, s, :, HD:HD + 1])
                    i.then_inc(S["recip_ready"], 1)
                    dve.wait_ge(S["recip_ready"], ATT[base] + t + 1)
                    for s in range(SPT):
                        r = slice(64 * s, 64 * s + 64)
                        i = V.tensor_tensor(y[r, par, :].rearrange("p (h d) -> p h d", d=HD), o[r, s, :, 0:HD],
                                            recip[r, par, :].unsqueeze(2).to_broadcast([64, HEADS, HD]), ALU.mult)
                    i.then_inc(S["y_ready"], 1)
                return fn

            def add_step(base, dst, scale):
                def fn(t, par):
                    dve.wait_ge(S["outp_ready"], ATT[base] + t + 1)
                    V.scalar_tensor_tensor(tile(dst, t), ps_v[:, 0:D], scale, tile(dst, t), ALU.mult, ALU.add
                                           ).then_inc(S["x_updated"], 1)
                return fn

            def attention(base, src, nbase, scale):
                pipeline(dve, [(0, sums_step(src)), (1, norm_step(src, nbase, base)), (0, stats_step(nbase)), (3, shift_step(base)),
                               (4, y_step(base)), (2, vbd_step(base)), (5, add_step(base, src, scale))])

            def plain_norm(src, dst, base, upd):
                def fn(t, par):
                    dve.wait_ge(S["bn_done"], base + capped(t + 2, NT))
                    dve.wait_ge(S["rstd_ready"], base + t + 1)
                    V.tensor_scalar(tile(dst, t), tile(src, t), mv[:, par, 0:1], rstd[:, par:par + 1],
                                    ALU.subtract, ALU.mult).then_inc(S["xn_ready"], 1)
                dve.wait_ge(S["x_updated"], upd)
                pipeline(dve, [(0, sums_step(src)), (1, fn), (0, stats_step(base))])
                dve.wait_ge(S["xn_ready"], base + NT)

            def best_two(rows_, n, l):
                k = [ROUTE_AT(l, 0)]

                def link(i):
                    k[0] += 1
                    i.then_inc(S["route_link"], 1)
                    dve.wait_ge(S["route_link"], k[0])
                r = slice(0, rows_)
                lg, c1, c2 = logits[r, 0:n, :], cw[r, 0:n, :], oneh[r, 0:n, :]

                def wide(v):
                    return v[r, 0:n].unsqueeze(2).to_broadcast([rows_, n, NE])

                def first_best(best, hot):
                    link(V.tensor_reduce(best[r, 0:n], lg, AXX, ALU.max))
                    link(V.tensor_tensor(hot, lg, wide(best), ALU.is_equal))
                    link(V.scalar_tensor_tensor(cand[r, 0:n, :], hot, -float(NE), iota8[r, 0:n, :], ALU.mult, ALU.add))
                    link(V.tensor_reduce(first[r, 0:n], cand[r, 0:n, :], AXX, ALU.min))
                    link(V.tensor_tensor(hot, cand[r, 0:n, :], wide(first), ALU.is_equal))

                first_best(best1, c1)
                link(V.scalar_tensor_tensor(lg, c1, NEG, lg, ALU.mult, ALU.add))
                first_best(best2, c2)
                link(V.tensor_tensor(e21[r, 0:n], best2[r, 0:n], best1[r, 0:n], ALU.subtract))
                dve.wait_ge(S["route_exp"], l + 1)
                link(V.tensor_scalar(tw2[r, 0:n], e21[r, 0:n], 1.0, None, ALU.add))
                link(V.reciprocal(tw1[r, 0:n], tw2[r, 0:n]))
                link(V.tensor_tensor(tw2[r, 0:n], e21[r, 0:n], tw1[r, 0:n], ALU.mult))
                link(V.tensor_tensor(c1, c1, wide(tw1), ALU.mult))
                link(V.tensor_tensor(c2, c2, wide(tw2), ALU.mult))
                i = V.tensor_tensor(c1, c1, c2, ALU.add)
                if l == 0:
                    i.then_inc(S["route_done"], 1)
                else:
                    link(i)
                assert k[0] == ROUTE_AT(l, ROUTE_LINKS[l])

            def top_step(t, par):
                dve.wait_ge(S["logits_ps"], t + 1)
                V.tensor_copy(logits[:, bass.ds(t, 1), :], ps_a[:, 0:NE].unsqueeze(1)).then_inc(S["logits_sb"], 1)

            def split_b2(l):
                k = [B2_LINKS * l]

                def link(i):
                    k[0] += 1
                    i.then_inc(S["rs_link"], 1)
                    dve.wait_ge(S["rs_link"], k[0])
                dve.wait_ge(S["ffn_w_loaded"], 16 * 5 * (l + 1))
                link(V.tensor_copy(b2hi[:, :, :], b2src[:, :, :]))
                link(V.tensor_tensor(b2a[:, :, :], b2src[:, :, :], b2hi[:, :, :], ALU.subtract))
                link(V.tensor_copy(b2mid[:, :, :], b2a[:, :, :]))
                link(V.tensor_tensor(b2lo[:, :, :], b2a[:, :, :], b2mid[:, :, :], ALU.subtract))
                link(V.tensor_scalar(b2a[:, :, :], b2hi[:, :, :], row3[:, 0:1], None, ALU.mult))
                link(V.scalar_tensor_tensor(b2a[:, :, :], b2mid[:, :, :], row3[:, 1:2], b2a[:, :, :], ALU.mult, ALU.add))
                link(V.scalar_tensor_tensor(b2a[:, :, :], b2lo[:, :, :], row3[:, 2:3], b2a[:, :, :], ALU.mult, ALU.add))
                for s in range(SUB):
                    link(V.tensor_copy(b2rows[:, :, s, :], b2a[:, :, :]))
                assert k[0] == B2_LINKS * (l + 1)

            def weigh_experts(l):
                def fn(b, par):
                    for e in range(NE):
                        bank = (ps_o, ps_v)[e % 2]
                        dve.wait_ge(S["yexp_ready"], l * NB * NE + b * NE + (e + 1))
                        seen(dve, S["acc_ready"], l * NB * NE + b * NE + e)
                        for s in range(SUB):
                            t = b * SUB + s
                            i = V.scalar_tensor_tensor(tile(inner, t), bank[:, s * D:(s + 1) * D],
                                                       cw[:, bass.ds(t, 1), e], tile(inner, t), ALU.mult, ALU.add)
                        i.then_inc(S["acc_ready"], 1)
                return fn

            attention("x", x_res, CROSS, coef[:, 0:1])
            plain_norm(x_res, inner, NORM0, UPD["x"] + NT)
            for l in range(LAYERS):
                attention(l, inner, (SELF0, SELF1)[l], 1.0)
                dve.wait_ge(S["x_updated"], UPD[l] + NT)
                nb_ = (PRE0, PRE1)[l]
                steps = [(0, sums_step(inner)), (1, norm_step(inner, nb_, f"p{l}")), (0, stats_step(nb_))]
                if l == 0:
                    steps.append((1, top_step))
                pipeline(dve, steps)
                if l == 0:
                    dve.wait_ge(S["logits_sb"], NT)
                    split_b2(0)
                    best_two(P, NT, 0)
                    dve.wait_ge(S["route_done"], 1)
                else:
                    dve.wait_ge(S["ht_stored"], 2 * NT)
                    V.tensor_reduce(hmean[:, :], h_t[:, :].rearrange("p (q i) -> p q i", i=SEQ), AXX, ALU.add
                                    ).then_inc(S["hmean_ready"], 1)
                    dve.wait_ge(S["seqlog_ready"], 1)
                    V.scalar_tensor_tensor(logits[0:NSEQ, 0, :], ps_a[0:NSEQ, 0:NE], 1.0 / SEQ,
                                           rowb[0:NSEQ, R_GB1:R_GB1 + NE], ALU.mult, ALU.add).then_inc(S["logits_sb"], 1)
                    dve.wait_ge(S["logits_sb"], NT + 1)
                    best_two(NSEQ, 1, 1)
                    V.tensor_tensor(cwrep[:, :, :], seq_tile[:, :, :], cw[0:NSEQ, 0:1, :].to_broadcast([NSEQ, NT, NE]),
                                    ALU.mult).then_inc(S["seq_cw"], 1)
                    split_b2(1)
                    dve.wait_ge(S["cw_ps"], 1)
                    V.tensor_copy(cw[:, :, :].rearrange("p t e -> p (t e)"), ps_a[:, 0:NT * NE]
                                  ).then_inc(S["route_done"], 1)
                    dve.wait_ge(S["route_done"], 2)
                fn = weigh_experts(l)
                fn(0, 0)
                with dve.Fori(1, NB, 1) as b:
                    fn(b, 0)
                dve.wait_ge(S["acc_ready"], (l + 1) * NB * NE)

            V.scalar_tensor_tensor(x_res[:, :], inner[:, :], tg[:, 2:3], x_res[:, :], ALU.mult, ALU.add
                                   ).then_inc(S["x_updated"], 1)
            dve.wait_ge(S["x_updated"], UPD["m"])

            def gates_copy(t, par):
                dve.wait_ge(S["gates_ps"], t + 1)
                V.tensor_copy(gates[:, par, :], ps_a[:, 0:16]).then_inc(S["gates_sb"], 1)
                dve.wait_ge(S["gates_sb"], t + 1)
                seen(dve, S["gexp_ready"], t - 1)
                V.scalar_tensor_tensor(gtmp[:, par, :], gates[:, par, 8:16], -1.0, gates[:, par, 8:16], ALU.mult,
                                       ALU.min).then_inc(S["nabs_ready"], 1)

            def lsig_step(t, par):
                dve.wait_ge(S["gln_ready"], t + 1)
                seen(dve, S["csum_ps"], t - 1)
                V.scalar_tensor_tensor(lsig[:, par, :], gates[:, par, 8:16], 0.0, gln[:, par, :], ALU.min, ALU.subtract
                                       ).then_inc(S["lsig_ready"], 1)

            def avec_step(t, par):
                dve.wait_ge(S["csum_ps"], t + 1)
                V.tensor_copy(csum[:, par, :], ps_a[:, 16:24]).then_inc(S["csum_sb"], 1)
                dve.wait_ge(S["csum_sb"], t + 1)
                seen(dve, S["adiag_ready"], t - 1)
                V.tensor_tensor(avec[:, par, :], gates[:, par, 0:8], csum[:, par, :], ALU.subtract
                                ).then_inc(S["avec_ready"], 1)

            def decay_shift(t, par):
                dve.wait_ge(S["a_ready"], t + 1)
                a3 = ps_t[:, 512:1024].rearrange("p (h k) -> p h k", k=SEQ)
                V.tensor_reduce(rowmax[:, par, 0:MH], a3, AXX, ALU.max).then_inc(S["max_ready"], 1)
                dve.wait_ge(S["max_ready"], ATT["m"] + t + 1)
                seen(dve, S["d_ready"], t - 1)
                V.tensor_tensor(shifted[:, par, 0:512].rearrange("p (h k) -> p h k", k=SEQ), a3,
                                rowmax[:, par, 0:MH].unsqueeze(2).to_broadcast([P, MH, SEQ]), ALU.subtract
                                ).then_inc(S["shifted_ready"], 1)
                seen(dve, S["emd_ready"], t - 1)
                V.scalar_tensor_tensor(negmd[:, par, :], csum[:, par, :], -1.0, rowmax[:, par, 0:MH], ALU.mult,
                                       ALU.subtract).then_inc(S["negmd_ready"], 1)

            def ctil_step(t, par):
                dve.wait_ge(S["d_ready"], t + 1)
                dve.wait_ge(S["scores_ready"], ATT["m"] + t + 1)
                seen(dve, S["pt_ready"], ATT["m"] + t - 1)
                V.tensor_tensor(ctil[:, par, :].rearrange("p (r n) -> p r n", r=2), ps_s3[:, :, 0:4 * SEQ],
                                probs[:, par, 0:512].rearrange("p (r n) -> p r n", r=2), ALU.mult
                                ).then_inc(S["ctil_ready"], 1)

            def h_step(t, par):
                k = [0]

                def link(i):
                    k[0] += 1
                    i.then_inc(S["gn_link"], 1)
                    dve.wait_ge(S["gn_link"], GN_LINKS * t + k[0])
                dve.wait_ge(S["o_ready"], ATT["m"] + t + 1)
                o = ps_o[:, 0:SPT * MH * (MHD + 1)].rearrange("p (s h d) -> p s h d", s=SPT, h=MH)
                halves = [slice(0, 64), slice(64, 128)]
                for s, r in enumerate(halves):
                    i = V.tensor_scalar(rs[r, par, :].unsqueeze(2), o[r, s, :, MHD:MHD + 1], 0.25, None, ALU.mult)
                link(i)
                link(V.scalar_tensor_tensor(rs[:, par, :], rs[:, par, :], -1.0, rs[:, par, :], ALU.mult, ALU.max))
                dve.wait_ge(S["emd_ready"], t + 1)
                link(V.tensor_tensor(rs2[:, par, :], rs[:, par, :], emd[:, par, :], ALU.max))
                link(V.tensor_scalar(rs2[:, par, :], rs2[:, par, :], 1e-6, 4.0, ALU.add, ALU.mult))
                link(V.reciprocal(rs3[:, par, :], rs2[:, par, :]))
                for s, r in enumerate(halves):
                    i = V.tensor_tensor(y[r, par, :].rearrange("p (h d) -> p h d", d=MHD), o[r, s, :, 0:MHD],
                                        rs3[r, par, :].unsqueeze(2).to_broadcast([64, MH, MHD]), ALU.mult)
                i.then_inc(S["y_ready"], 1)
                dve.wait_ge(S["y_ready"], ATT["m"] + t + 1)
                y3 = y[:, par, :].rearrange("p (h d) -> p h d", d=MHD)
                yc3 = yc[:, par, :].rearrange("p (h d) -> p h d", d=MHD)
                q3 = qa[:, par, :].rearrange("p (h d) -> p h d", d=MHD)
                link(V.tensor_reduce(gsum[:, par, :], y3, AXX, ALU.add))
                link(V.tensor_scalar(gsum[:, par, :], gsum[:, par, :], 1.0 / MHD, None, ALU.mult))
                link(V.tensor_tensor(yc3, y3, gsum[:, par, :].unsqueeze(2).to_broadcast([P, MH, MHD]), ALU.subtract))
                link(V.tensor_tensor(q3, yc3, yc3, ALU.mult))
                link(V.tensor_reduce(gvar[:, par, :], q3, AXX, ALU.add))
                V.tensor_scalar(gve[:, par, :], gvar[:, par, :], 1.0 / MHD, EPS, ALU.mult, ALU.add
                                ).then_inc(S["gve_ready"], 1)
                dve.wait_ge(S["grstd_ready"], t + 1)
                link(V.tensor_tensor(yc3, yc3, grstd[:, par, :].unsqueeze(2).to_broadcast([P, MH, MHD]), ALU.mult))
                V.tensor_tensor(yn[:, par, :], yc[:, par, :], rowb[:, R_GNW:R_GNW + D], ALU.mult
                                ).then_inc(S["yn_ready"], 1)
                assert k[0] == GN_LINKS
                dve.wait_ge(S["yb_ready"], t + 1)
                V.tensor_tensor(tile(x_res, t), tile(x_res, t), ysq[:, par, :], ALU.add).then_inc(S["x_updated"], 1)

            pipeline(dve, [(0, sums_step(x_res)), (1, norm_step(x_res, MLSTM, "m")), (0, stats_step(MLSTM)), (3, decay_shift),
                           (2, lsig_step), (3, ctil_step), (2, avec_step), (1, gates_copy), (4, h_step)])

            plain_norm(x_res, inner, NORM1, UPD["m"] + NT)
            V.tensor_reduce(xscale[:, 0:1], inner[:, :], AXX, ALU.min).then_inc(S["fin_link"], 1)
            V.tensor_reduce(xscale[:, 1:2], inner[:, :], AXX, ALU.max).then_inc(S["fin_link"], 1)
            dve.wait_ge(S["fin_link"], 2)
            V.scalar_tensor_tensor(amax[:, :], xscale[:, 0:1], -1.0, xscale[:, 1:2], ALU.mult, ALU.max
                                   ).then_inc(S["amax_ready"], 1)
            dve.wait_ge(S["amrow_done"], 1)
            V.tensor_reduce(am1[:, 1:2], amrow[:, :], AXX, ALU.max).then_inc(S["fin_link"], 1)
            dve.wait_ge(S["fin_link"], 3)
            V.tensor_scalar(am1[:, 0:1], am1[:, 1:2], 1.0 / 127.0, EPS, ALU.mult, ALU.max).then_inc(S["scale_ready"], 1)
            dve.wait_ge(S["scale_ps"], 1)
            V.tensor_copy(xscale[:, 0:1], ps_v[:, 0:1]).then_inc(S["fin_link"], 1)
            dve.wait_ge(S["fin_link"], 4)
            V.reciprocal(xscale[:, 1:2], xscale[:, 0:1]).then_inc(S["fin_link"], 1)
            dve.wait_ge(S["fin_link"], 5)

            def quantise(t, par):
                V.tensor_scalar(qa[:, par, :], tile(inner, t), xscale[:, 1:2], -128.0, ALU.mult, ALU.max
                                ).then_inc(S["fin_link"], 1)
                dve.wait_ge(S["fin_link"], 5 + 2 * t + 1)
                V.tensor_scalar(qb[:, par, :], qa[:, par, :], 127.0, MAGIC, ALU.min, ALU.add).then_inc(S["fin_link"], 1)
                dve.wait_ge(S["fin_link"], 5 + 2 * t + 2)
                seen(dve, S["q8t_ps"], t - 1)
                V.tensor_scalar(q8[:, par, :], qb[:, par, :], MAGIC, None, ALU.subtract).then_inc(S["q8_ready"], 1)

            def dequantise(t, par):
                dve.wait_ge(S["acc8_ready"], t + 1)
                seen(dve, S["o2_ready"], t - 1)
                V.scalar_tensor_tensor(o1[:, par, :], ps_o[:, 0:D], xscale[:, 0:1], rowb[:, R_WS:R_WS + D], ALU.mult,
                                       ALU.mult).then_inc(S["o1_ready"], 1)

            def finish(t, par):
                dve.wait_ge(S["o2_ready"], t + 1)
                seen(dve, out_stored[par], arrived(t, par, 16) - 16)
                V.scalar_tensor_tensor(o3[:, par, :], o2[:, par, :], tg[:, 3:4], tile(x_res, t), ALU.mult, ALU.add
                                       ).then_inc(S["o3_ready"], 1)
            pipeline(dve, [(0, quantise), (2, dequantise), (3, finish)])


_INS = ['x', 'ctx_1024', 'g_xattn', 'g_ffn', 'L0_xattn_Wq', 'L0_xattn_Wk', 'L0_xattn_Wv', 'L0_xattn_Wo',
        'L0_ffn_ln1_w', 'L0_ffn_ln1_b', 'L0_ffn_ln2_w', 'L0_ffn_ln2_b', 'L0_ffn_wq', 'L0_ffn_wk', 'L0_ffn_wv',
        'L0_ffn_wo', 'L0_ffn_bq', 'L0_ffn_bk', 'L0_ffn_bv', 'L0_ffn_bo', 'L0_ffn_gate_w', 'L0_ffn_gate_b',
        'L0_ffn_e_w1', 'L0_ffn_e_b1', 'L0_ffn_e_w2', 'L0_ffn_e_b2', 'L1_xattn_Wi_w', 'L1_xattn_Wi_b',
        'L1_xattn_Wf_w', 'L1_xattn_Wf_b', 'L1_xattn_gn_w', 'L1_xattn_gn_b', 'L1_ffn_weight_int8',
        'L1_ffn_weight_scale', 'L1_ffn_bias']


def kernel(**inputs):
    import numpy as _np
    import concourse.bacc as _bacc
    from concourse import mybir as _mybir
    from concourse.bass_utils import run_bass_kernel_spmd as _run

    nc = _bacc.Bacc("TRN2", target_bir_lowering=False, num_devices=1)
    arrays, args = {}, {}
    for name in _INS:
        a = _np.ascontiguousarray(inputs[name])
        if a.dtype == _np.int8:
            a = a.view(_np.int32)
        arrays[f"in_{name}_dram"] = a
        args[name] = nc.dram_tensor(f"in_{name}_dram", a.shape, _mybir.dt.from_np(a.dtype), kind="ExternalInput").ap()
    out = nc.dram_tensor("out_0_dram", (NSEQ, SEQ, D), _mybir.dt.float32, kind="ExternalOutput").ap()
    build(nc, args, out)
    r = _run(nc, [arrays], core_ids=[0])
    return r.results[0]["out_0_dram"]
```

```python
from contextlib import ExitStack

import concourse.bass as bass
from concourse import mybir

P = 128
NSEQ, SEQ, D = 64, 64, 128
TOK = NSEQ * SEQ
NT = TOK // P
SPT = P // SEQ
HEADS, HD = 16, 8
MH, MHD = 8, 16
NE, DFF = 8, 512
CH = DFF // P
BLK = 512
NB = TOK // BLK
SUB = BLK // P
LAYERS = 2
L_SCORES, L_WEIGH, L_OUT = 4, 5, 6
VBUFS = 4
ITEMS = 2 * NSEQ
NPAIR = (ITEMS + NE) // 2
PLACES = 2 * NPAIR
EPS = 1e-5
NEG = -1e30
MAGIC = 12582912.0
ROW0_PAIRS = 3.0

F32 = mybir.dt.float32
BF16 = mybir.dt.bfloat16
I8 = mybir.dt.int8
U32 = mybir.dt.uint32
I32 = mybir.dt.int32
ALU = mybir.AluOpType
ACT = mybir.ActivationFunctionType
AXX = mybir.AxisListType.X


def seen(eng, sem, value):
    if isinstance(value, int) and value <= 0:
        return
    eng.wait_ge(sem, value)


def capped(value, most):
    return min(value, most) if isinstance(value, int) else value


def arrived(t, par, each):
    return (t - par) * (each // 2) + each


def pipeline(eng, steps, n=NT, unroll=4):
    last = max(step[0] for step in steps)
    head = (last + unroll) // unroll * unroll

    def call(step, t, k):
        step[1](t, k % 2, *(k % buffers for buffers in step[2:]))
    for i in range(head):
        for step in steps:
            if i >= step[0]:
                call(step, i - step[0], i - step[0])
    with eng.Fori(head // unroll, n // unroll, 1) as turn:
        i0 = turn * unroll
        for u in range(unroll):
            for step in steps:
                call(step, i0 + (u - step[0]), u - step[0])
    for i in range(n, n + last):
        for step in steps:
            if i - step[0] < n:
                call(step, i - step[0], i - step[0])


def build(nc, A, out):
    with ExitStack() as ctx:
        def sb(name, shape, dt=F32):
            return ctx.enter_context(nc.sbuf_tensor(name, shape, dt))

        def psum(name, cols):
            return ctx.enter_context(nc.psum_tensor(name, [P, cols], F32))

        def sem(name):
            return ctx.enter_context(nc.semaphore(name))

        def tile(buf, t):
            return buf[:, bass.ds(t * P, P)]

        x_res = sb("x_res", [P, NT * D])
        inner = sb("inner", [P, NT * D])
        h_t = sb("h_t", [P, TOK])
        w12 = sb("w12", [P, 2 * NE * DFF])
        w1 = w12[:, 0:NE * DFF].rearrange("p (e n) -> p e n", e=NE)
        w2 = w12[:, NE * DFF:2 * NE * DFF].rearrange("p (e c d) -> p e c d", e=NE, c=CH)
        o_all = w12[:, 0:NT * MH * (MHD + 1)].rearrange("p (t h d) -> p t h d", t=NT, h=MH)
        wraw = sb("wraw", [P, 4, D])
        wx = sb("wx", [P, 4, D])
        wself = sb("wself", [P, LAYERS, 4, D])
        gatew = sb("gatew", [P, LAYERS, NE])
        vecs = sb("vecs", [78, D])
        vec_t = sb("vec_t", [P, 78])
        wg_raw = sb("wg_raw", [2 * MH, 3, D])
        wg_t = sb("wg_t", [P, 3, 2 * MH])
        w8 = sb("w8", [P, D // 4], I32)
        w8f = sb("w8f", [P, D])
        w8t = sb("w8t", [P, D], BF16)
        rows = sb("rows", [1, 1024])
        rowb = sb("rowb", [P, 5 * D + 16])
        tg = sb("tg", [P, 4])
        coef = sb("coef", [P, 4])
        b2src = sb("b2src", [3, NE, D])
        b2a = sb("b2a", [3, NE, D])
        b2hi = sb("b2hi", [3, NE, D], BF16)
        b2mid = sb("b2mid", [3, NE, D], BF16)
        b2lo = sb("b2lo", [3, NE, D], BF16)
        b2rows = sb("b2rows", [3, NE, SUB, D], BF16)
        ident = sb("ident", [P, P])
        identb = sb("identb", [P, P], BF16)
        ones_row = sb("ones_row", [1, P])
        ones3 = sb("ones3", [3, P], BF16)
        kmask = sb("kmask", [P, 8, SEQ])
        kmask4 = sb("kmask4", [P, 4, P])
        vmask = sb("vmask", [P, SPT * HEADS, HD])
        vmask16 = sb("vmask16", [P, SPT * MH, MHD])
        causal = sb("causal", [P, 8, SEQ], BF16)
        block_ones = sb("block_ones", [P, P])
        block_tri = sb("block_tri", [P, P])
        delta = sb("delta", [P, MH, SEQ])
        row3 = sb("row3", [3, 3])
        mhalf = sb("mhalf", [P, NT])
        iota8 = sb("iota8", [P, NT, NE])
        before = sb("before", [NSEQ, NSEQ])
        ones_seq = sb("ones_seq", [NSEQ, P])
        place_no = sb("place_no", [NSEQ, PLACES])
        pair_no = sb("pair_no", [1, NPAIR, NE])
        seq_col = sb("seq_col", [NSEQ, 1])
        b2w = sb("b2w", [NE, D])
        stats = sb("stats", [P, NT, 6])
        mean = sb("mean", [P, NT])
        half_gap = sb("half_gap", [P, NT])
        var = sb("var", [P, NT])
        vare = sb("vare", [P, NT])
        rstd = sb("rstd", [P, NT])
        xn = sb("xn", [P, 2, D])
        xts = sb("xts", [P, 2, P])
        cts = sb("cts", [P, 2, P])
        ctx_in = sb("ctx_in", [P, 2, D])
        ctx_dup = sb("ctx_dup", [P, 2, SPT, D])
        kvt = sb("kvt", [P, 2, SPT, 2, SEQ])
        qbd = sb("qbd", [P, 2, 2, P])
        kts = sb("kts", [P, 2, 2, SEQ])
        vecs2 = sb("vecs2", [8, P])
        vec2_t = sb("vec2_t", [P, 8])
        kbd = sb("kbd", [P, 2, 8, P])
        vbd = sb("vbd", [P, VBUFS, SPT, HEADS, HD + 1])
        vbd16 = sb("vbd16", [P, 2, SPT, MH, MHD + 1])
        rowmax = sb("rowmax", [P, 2, HEADS])
        work = sb("work", [P, 2 * CH * BLK])
        shifted = work[:, 0:2048].rearrange("p (b n) -> p b n", b=2)
        probs = work[:, 2048:4096].rearrange("p (b n) -> p b n", b=2)
        gel = work[:, :].rearrange("p (b c n) -> p b c n", b=2, c=CH)
        w1s = work[:, 0:2 * DFF].rearrange("p (b n) -> p b n", b=2)
        w2s = work[:, 2 * DFF:4 * DFF].rearrange("p (b n) -> p b n", b=2)
        gels = work[:, 4 * DFF:6 * DFF].rearrange("p (b n) -> p b n", b=2)
        hs = work[:, 6 * DFF:6 * DFF + 2 * P].rearrange("p (b n) -> p b n", b=2)
        probs_t = sb("probs_t", [P, 2, 1024])
        recip = sb("recip", [P, 2, HEADS])
        y = sb("y", [P, 2, D])
        yts = sb("yts", [P, 2, P])
        logits = sb("logits", [P, NT, NE])
        cand = sb("cand", [P, NT, NE])
        first = sb("first", [P, NT])
        best1 = sb("best1", [P, NT])
        best2 = sb("best2", [P, NT])
        e21 = sb("e21", [P, NT])
        tw1 = sb("tw1", [P, NT])
        tw2 = sb("tw2", [P, NT])
        oneh = sb("oneh", [P, NT, NE])
        cw = sb("cw", [P, NT, NE])
        hmean = sb("hmean", [P, NSEQ])
        chosen = sb("chosen", [NSEQ, 2, NE])
        counts = sb("counts", [NSEQ, NE])
        tiles_of = sb("tiles_of", [P, NE])
        upto_a = sb("upto_a", [P, 2 * NE])
        upto_b = sb("upto_b", [P, 2 * NE])
        place_base = sb("place_base", [NSEQ, NE])
        chosen_place = sb("chosen_place", [NSEQ, 2, NE])
        place = sb("place", [NSEQ, 2])
        at_place = sb("at_place", [NSEQ, 2, 2, PLACES])
        past = sb("past", [1, NPAIR, NE])
        expert_f = sb("expert_f", [1, NPAIR])
        expert_of = sb("expert_of", [1, NPAIR], I32)
        col_of = sb("col_of", [1, PLACES], I32)
        place_w = sb("place_w", [P, PLACES])
        cw_t = sb("cw_t", [NE, NSEQ])
        b1s = sb("b1s", [P, 2, CH])
        gates = sb("gates", [P, NT, 2 * MH])
        gtmp = oneh
        lsig = logits
        csum = sb("csum", [P, NT, MH])
        avec = cw
        maxes = cand
        adiag = shifted[:, :, 512:1024].rearrange("p b (h k) -> p b h k", k=SEQ)
        ctil = probs[:, :, 512:1024]
        amax = sb("amax", [P, 1])
        amrow = sb("amrow", [1, P])
        am1 = sb("am1", [1, 2])
        xscale = sb("xscale", [P, 2])
        qa = xn
        qb = work[:, 0 * D:2 * D].rearrange("p (b n) -> p b n", b=2)
        q8 = sb("q8", [P, 2, D], BF16)
        q8t = sb("q8t", [P, 2, P], BF16)
        o1 = work[:, 2 * D:4 * D].rearrange("p (b n) -> p b n", b=2)
        o2 = work[:, 4 * D:6 * D].rearrange("p (b n) -> p b n", b=2)
        o3 = work[:, 6 * D:8 * D].rearrange("p (b n) -> p b n", b=2)

        ps_s = psum("ps_s", 1024)
        ps_t = psum("ps_t", 1024)
        ps_o = psum("ps_o", 512)
        ps_x = psum("ps_x", 512)
        ps_a = psum("ps_a", 512)
        ps_v = psum("ps_v", 512)
        ps_s3 = ps_s[:, :].rearrange("p (r n) -> p r n", r=2)

        names = """x_loaded weights_loaded ffn_w_loaded ffn_w_free pool_const ident_ready setup_t setup_copied dve_setup
        bn_done stat_link vare_ready rstd_ready xn_ready xt_ready xts_ready ctx_used
        proj_ready qk_ready kbd_ready vbd_ready scores_ready max_ready shifted_ready probs_ready
        pt_ready pts_ready o_ready recip_ready y_ready yt_ready yts_ready outp_ready x_updated
        ht_stored logits_ps logits_sb route_link route_exp route_done hmean_ready seqlog_ready
        place_ps place_link tables_ready w1s_ready w2s_ready hs_ready pair_hid pair_gelu pair_out pair_added
        rows_ps rows_added
        hid_ready gelu_ready yexp_ready acc_ready gates_ps gates_sb xct_stored gate_link gexp_ready gln_ready
        csum_ps avec_ready adiag_ready a_ready d_ready ctil_ready qcopy_ready o_stored negmd_ready emd_ready
        vb16_ready rs_link gn_link square_ready gve_ready grstd_ready fin_link amax_ready amrow_ps
        amrow_done scale_ps scale_ready q8_ready q8t_ps q8t_ready acc8_ready o1_ready o2_ready o3_ready
        ctx0_loaded ctx1_loaded dup0_loaded dup1_loaded out0_stored out1_stored out_left"""
        S = {n: sem(n) for n in names.split()}
        ctx_loaded = [S["ctx0_loaded"], S["ctx1_loaded"]]
        dup_loaded = [S["dup0_loaded"], S["dup1_loaded"]]
        out_stored = [S["out0_stored"], S["out1_stored"]]

        CROSS, NORM0, SELF0, PRE0, SELF1, PRE1, MLSTM, NORM1 = (k * NT for k in range(8))
        ATT = {"x": 0, 0: NT, 1: 2 * NT, "m": 3 * NT}
        TB = {"x": 0, 0: NT, "p0": 2 * NT, 1: 3 * NT, "p1": 4 * NT, "m": 5 * NT}
        UPD = {"x": 0, 0: NT, 1: 2 * NT, "m": 3 * NT}

        x_v = A["x"].rearrange("(t s) i d -> (s i) t d", s=SPT)
        ctx_v = A["ctx_1024"].rearrange("(t s) i d -> t (s i) d", s=SPT)
        ctxd_v = A["ctx_1024"].rearrange("(t s) i d -> t i s d", s=SPT)
        out_v = out.rearrange("(t s) i d -> t (s i) d", s=SPT)

        CONSTS = []
        block = ctx.enter_context(nc.Block())

        ROUTE_EXP = 12
        ROUTE_COUNTS = ROUTE_EXP + 3
        ROUTE_LINKS = (ROUTE_EXP + 5, ROUTE_COUNTS + 6)
        B2_LINKS = 7 + SUB
        STAT_LINKS = 6
        PLACE_TABLES = 14
        GN_CENTRED = 7

        def ROUTE_AT(l, k):
            return sum(ROUTE_LINKS[:l]) + k

        q8ps = ps_x[:, :].bitcast(BF16)[:, 0:P]

        def vec(kind, l):
            c = 2 * kind + l
            return vec_t[:, c:c + 1]

        def b1col(l, e, c):
            k = 14 + (l * NE + e) * CH + c
            return vec_t[:, k:k + 1]

        def qkbias(kind, l, r, rows_):
            c = kind * 4 + l * 2 + r
            return vec2_t[rows_, c:c + 1]

        R_GNW, R_GNB, R_WS, R_B1, R_GB1, R_G = 0, D, 2 * D, 3 * D, 4 * D, 4 * D + 8
        R_BO, R_GI, R_GB0 = 4 * D + 16, 6 * D + 16, 6 * D + 32
        row_loads = [("L1_xattn_gn_w", R_GNW), ("L1_xattn_gn_b", R_GNB), ("L1_ffn_weight_scale", R_WS),
                     ("L1_ffn_bias", R_B1), ("g_xattn", R_G), ("g_ffn", R_G + 2), ("L1_xattn_Wi_b", R_GI),
                     ("L1_xattn_Wf_b", R_GI + 8)]
        small_loads = []
        for name, at in row_loads:
            ap = A[name]
            n = 1
            for s_ in ap.shape:
                n *= s_
            flat = ap.rearrange("a b -> (b a)") if len(ap.shape) == 2 else ap
            small_loads.append((rows[0:1, at:at + n], flat.rearrange("(a n) -> a n", a=1)))
        small_loads.append((rows[0:1, R_GB1:R_GB1 + 8], A["L0_ffn_gate_b"][1:2, :]))
        small_loads.append((rows[0:1, R_GB0:R_GB0 + 8], A["L0_ffn_gate_b"][0:1, :]))
        for l in range(LAYERS):
            small_loads.append((rows[0:1, R_BO + l * D:R_BO + (l + 1) * D], A["L0_ffn_bo"][l:l + 1, :]))
        for k, name in enumerate(("ln1_w", "ln1_b", "ln2_w", "ln2_b", "bq", "bk", "bv")):
            small_loads.append((vecs[2 * k:2 * k + 2, :], A["L0_ffn_" + name]))
        for k, name in enumerate(("bq", "bk")):
            for half in range(2):
                small_loads.append((vecs2[4 * k:4 * k + 4, half * 64:(half + 1) * 64],
                                    A["L0_ffn_" + name].rearrange("l (r c) -> (l r) c", r=2)))
        small_loads.append((vecs[14:78, :], A["L0_ffn_e_b1"].rearrange("l e (c p) -> (l e c) p", p=P)))
        for k, name in enumerate(("Wq", "Wk", "Wv", "Wo")):
            small_loads.append((wraw[:, k, :], A["L0_xattn_" + name]))
            for l in range(LAYERS):
                small_loads.append((wself[:, l, k, :], A["L0_ffn_" + name.lower()][l, :, :]))
        for l in range(LAYERS):
            small_loads.append((gatew[:, l, :], A["L0_ffn_gate_w"][l, :, :]))
        small_loads.append((wg_raw[0:MH, :, :], A["L1_xattn_Wi_w"].rearrange("h (k d) -> h k d", k=3)))
        small_loads.append((wg_raw[MH:2 * MH, :, :], A["L1_xattn_Wf_w"].rearrange("h (k d) -> h k d", k=3)))
        small_loads.append((w8[:, :], A["L1_ffn_weight_int8"]))
        small_loads.append((b2w[:, :], A["L0_ffn_e_b2"][1, :, :]))
        N_WLOADS = len(small_loads)

        @block.sync
        def _(sp):
            sp.dma_start(x_res[:, :].rearrange("p (t d) -> p t d", d=D), x_v).then_inc(S["x_loaded"], 16)
            for dst, src in small_loads[:N_WLOADS // 2]:
                sp.dma_start(dst, src).then_inc(S["weights_loaded"], 16)

            def ctx_load(base):
                def fn(t, par):
                    seen(sp, S["ctx_used"], base + t - 1)
                    sp.dma_start(ctx_in[:, par, :], ctx_v[bass.ds(t, 1), :, :].rearrange("a p d -> p (a d)")
                                 ).then_inc(ctx_loaded[par], 16)
                return fn

            def dup_load(t, par):
                seen(sp, S["vb16_ready"], t - 1)
                for g in range(2):
                    sp.dma_start(ctx_dup[g * SEQ:(g + 1) * SEQ, par, :, :],
                                 ctxd_v[bass.ds(t, 1), :, :, :].rearrange("a i s d -> i (a s) d")
                                 ).then_inc(dup_loaded[par], 16)

            def expert_load(l):
                if l:
                    sp.wait_ge(S["yexp_ready"], NB * NE)
                sp.dma_start(w1[:, :, :], A["L0_ffn_e_w1"][l, :, :, :].rearrange("e d f -> d e f")
                             ).then_inc(S["ffn_w_loaded"], 16)
                sp.dma_start(w2[:, :, :, :], A["L0_ffn_e_w2"][l, :, :, :].rearrange("e (c p) d -> p e c d", p=P)
                             ).then_inc(S["ffn_w_loaded"], 16)
                for r in range(0 if l else 3):
                    sp.dma_start(b2src[r:r + 1, :, :], A["L0_ffn_e_b2"][0:1, :, :]
                                 ).then_inc(S["ffn_w_loaded"], 16)

            pipeline(sp, [(0, ctx_load(0))])
            expert_load(0)
            expert_load(1)
            pipeline(sp, [(0, ctx_load(NT))])
            pipeline(sp, [(0, dup_load)])

            def store(t, par):
                sp.wait_ge(S["o3_ready"], t + 1)
                sp.dma_start(out_v[bass.ds(t, 1), :, :].rearrange("a p d -> p (a d)"), o3[:, par, :]
                             ).then_inc(out_stored[par], 16)
            pipeline(sp, [(0, store)])
            for par in range(2):
                sp.wait_ge(out_stored[par], 16 * (NT // 2))

        @block.gpsimd
        def _(pool):
            n = [0]

            def fresh(ins):
                n[0] += 1
                ins.then_inc(S["pool_const"], 1)
                pool.wait_ge(S["pool_const"], n[0])

            def select(ap, pattern, base, mult, cmp=ALU.is_ge, fill=0.0):
                fresh(pool.affine_select(out=ap, in_=ap, compare_op=cmp, fill=fill, base=base,
                                         pattern=pattern, channel_multiplier=mult))

            fresh(pool.memset(ident[:, :], 0.0))
            select(ident[:, :], [[-1, P]], 0, 1, ALU.not_equal, 1.0)
            fresh(pool.memset(identb[:, :], 0.0))
            select(identb[:, :], [[-1, P]], 0, 1, ALU.not_equal, 1.0)
            fresh(pool.memset(ones_row[:, :], 1.0))
            fresh(pool.memset(ones3[:, :], 1.0))
            fresh(pool.memset(mhalf[:, :], -0.5))
            for buf, hh, hd, width in ((kmask, 8, HD, SEQ), (kmask4, 4, MHD, P)):
                for half in range(2):
                    part = buf[half * 64:(half + 1) * 64, :, :]
                    fresh(pool.memset(part, 1.0))
                    select(part, [[-hd, hh], [0, width]], 0, 1)
                    select(part, [[hd, hh], [0, width]], hd - 1, -1)
            for buf, hd in ((vmask, HD), (vmask16, MHD)):
                v = buf[:, :, :].rearrange("p (n g) d -> p n g d", g=2)
                fresh(pool.memset(buf[:, :, :], 0.0))
                for half in range(2):
                    fresh(pool.memset(v[half * 64:(half + 1) * 64, :, half, :], 1.0))
            fresh(pool.memset(vbd[:, :, :, :, :], 1.0))
            fresh(pool.memset(qbd[:, :, :, :], 0.0))
            fresh(pool.memset(vbd16[:, :, :, :, :], 1.0))
            for buf, nh, hd in ((vbd, HEADS, HD), (vbd16, MH, MHD)):
                for half in range(2):
                    for par in range(buf.shape[1]):
                        v = buf[half * 64:(half + 1) * 64, par, :, :, hd:hd + 1].rearrange(
                            "p s (n g) o -> p s n g o", g=2)[:, :, :, 1 - half, :]
                        fresh(pool.memset(v, 0.0))
            fresh(pool.memset(causal[:, :, :], 0.0))
            for half in range(2):
                part = causal[half * 64:(half + 1) * 64, :, :]
                select(part, [[0, 8], [-1, SEQ]], 0, 1, ALU.is_ge, NEG)
            fresh(pool.memset(block_ones[:, :], 0.0))
            fresh(pool.memset(block_tri[:, :], 0.0))
            fresh(pool.memset(delta[:, :, :], 0.0))
            for half in range(2):
                a, b = half * 64, (half + 1) * 64
                fresh(pool.memset(block_ones[a:b, a:b], 1.0))
                fresh(pool.memset(block_tri[a:b, a:b], 1.0))
                select(block_tri[a:b, a:b], [[1, 64]], 0, -1)
                select(delta[a:b, :, :], [[0, MH], [-1, SEQ]], 0, 1, ALU.not_equal, 1.0)
            fresh(pool.memset(row3[:, :], 0.0))
            select(row3[:, :], [[-1, 3]], 0, 1, ALU.not_equal, 1.0)
            fresh(pool.iota(iota8[:, :, :], pattern=[[0, NT], [1, NE]], base=0, channel_multiplier=0,
                            allow_small_or_imprecise_dtypes=True))
            fresh(pool.memset(before[:, :], 1.0))
            select(before[:, :], [[1, NSEQ]], -1, -1)
            fresh(pool.memset(ones_seq[:, :], 1.0))
            fresh(pool.iota(place_no[:, :], pattern=[[1, PLACES]], base=0, channel_multiplier=0,
                            allow_small_or_imprecise_dtypes=True))
            fresh(pool.iota(pair_no[:, :, :], pattern=[[1, NPAIR], [0, NE]], base=0, channel_multiplier=0,
                            allow_small_or_imprecise_dtypes=True))
            fresh(pool.iota(seq_col[:, :], pattern=[[0, 1]], base=0, channel_multiplier=SEQ,
                            allow_small_or_imprecise_dtypes=True))
            fresh(pool.memset(upto_a[:, :], 0.0))
            fresh(pool.memset(upto_b[:, :], 0.0))
            CONSTS.append(n[0])

            def row_rstd(k):
                pool.wait_ge(S["vare_ready"], k + 1)
                pool.tensor_tensor(rstd[:, :], vare[:, :], mhalf[:, :], ALU.pow).then_inc(S["rstd_ready"], 1)

            def kbd_step(base):
                def fn(t, par):
                    pool.wait_ge(S["qk_ready"], base + t + 1)
                    seen(pool, S["scores_ready"], base + t - 1)
                    for r in range(2):
                        i = pool.tensor_tensor(kbd[:, par, r * 4:(r + 1) * 4, :].rearrange("p a (b k) -> p (a b) k", k=SEQ),
                                               kts[:, par, r:r + 1, :].to_broadcast([P, 8, SEQ]),
                                               kmask[:, :, :], ALU.mult)
                    i.then_inc(S["kbd_ready"], 1)
                return fn

            def ht_step(base):
                def fn(t, par):
                    pool.wait_ge(S["xts_ready"], TB[base] + t + 1)
                    pool.tensor_copy(tile(h_t, t), xts[:, par, :]).then_inc(S["ht_stored"], 1)
                return fn

            row_rstd(0)
            pipeline(pool, [(2, kbd_step(ATT["x"]))])
            row_rstd(1)
            for l in range(LAYERS):
                row_rstd(2 + 2 * l)
                pipeline(pool, [(2, kbd_step(ATT[l]))])
                row_rstd(3 + 2 * l)
                if l:
                    pool.wait_ge(S["yexp_ready"], NB * NE)
                pipeline(pool, [(1, ht_step(f"p{l}"))])

            def second_weights(t, par):
                seen(pool, S["pair_out"], t - 1)
                e = pool.value_load(expert_of[0:1, bass.ds(t, 1)], min_val=0, max_val=NE - 1)
                pool.tensor_copy(w2s[:, par, :].unsqueeze(1), w2[:, bass.ds(e, 1), :, :].rearrange("p e c d -> p e (c d)")
                                 ).then_inc(S["w2s_ready"], 1)
            pool.wait_ge(S["ffn_w_loaded"], 16 * 7)
            pool.wait_ge(S["tables_ready"], 1)
            pipeline(pool, [(0, second_weights)], NPAIR)

            def store_xct(t, par):
                pool.wait_ge(S["xts_ready"], TB["m"] + t + 1)
                pool.tensor_copy(tile(h_t, t), xts[:, par, :])
                pool.tensor_copy(tile(inner, t), cts[:, par, :]).then_inc(S["xct_stored"], 1)

            def kbd16_step(t, par):
                seen(pool, S["scores_ready"], ATT["m"] + t - 1)
                pool.tensor_tensor(kbd[:, par, 0:4, :], tile(inner, t).unsqueeze(1).to_broadcast([P, 4, P]),
                                   kmask4[:, :, :], ALU.mult).then_inc(S["kbd_ready"], 1)

            def vbd16_step(t, par):
                pool.wait_ge(dup_loaded[par], arrived(t, par, 32))
                seen(pool, S["o_ready"], ATT["m"] + t - 1)
                pool.tensor_tensor(vbd16[:, par, :, :, 0:MHD].rearrange("p s h d -> p (s h) d"),
                                   ctx_dup[:, par, :, :].rearrange("p s (h d) -> p (s h) d", d=MHD),
                                   vmask16[:, :, :], ALU.mult).then_inc(S["vb16_ready"], 1)

            def adiag_step(t, par):
                seen(pool, S["a_ready"], t - 1)
                pool.tensor_tensor(adiag[:, par, :, :],
                                   avec[:, bass.ds(t, 1), :].rearrange("p a h -> p (a h)").unsqueeze(2).to_broadcast([P, MH, SEQ]),
                                   delta[:, :, :], ALU.mult).then_inc(S["adiag_ready"], 1)

            row_rstd(6)
            pipeline(pool, [(2, store_xct)])
            pool.wait_ge(S["xct_stored"], NT)
            pool.wait_ge(S["avec_ready"], 1)
            pipeline(pool, [(6, vbd16_step), (2, kbd16_step), (0, adiag_step)])
            pool.wait_ge(S["gve_ready"], 1)
            for k in range(MH):
                i = pool.tensor_tensor(gtmp[:, :, k], lsig[:, :, k], mhalf[:, :], ALU.pow)
            i.then_inc(S["grstd_ready"], 1)
            row_rstd(7)

            def o2_step(t, par):
                pool.wait_ge(S["o1_ready"], t + 1)
                seen(pool, S["o3_ready"], t - 1)
                pool.tensor_tensor(o2[:, par, :], o1[:, par, :], rowb[:, R_B1:R_B1 + D], ALU.add
                                   ).then_inc(S["o2_ready"], 1)
            pipeline(pool, [(0, o2_step)])

        @block.scalar
        def _(act):
            for dst, src in small_loads[N_WLOADS // 2:]:
                act.dma_start(dst, src).then_inc(S["weights_loaded"], 16)
            k = [0]

            def copied(dst, src):
                k[0] += 1
                act.wait_ge(S["setup_t"], k[0])
                nc.scalar.copy(dst, src).then_inc(S["setup_copied"], 1)
            copied(wx[:, :, :].rearrange("p a d -> p (a d)"), ps_s[:, 0:4 * D])
            copied(vec_t[:, :], ps_t[:, 0:78])
            copied(vec2_t[:, :], ps_t[:, 512:520])
            copied(wg_t[:, :, :].rearrange("p a d -> p (a d)"), ps_o[:, 0:48])
            copied(rowb[:, 0:512], ps_a[:, 0:512])
            copied(rowb[:, 512:524], ps_v[:, 0:12])
            copied(w8t[:, :], ps_x[:, 0:P])
            act.wait_ge(S["setup_copied"], 6)
            nc.scalar.activation(tg[:, :], rowb[:, R_G:R_G + 4], ACT.Tanh).then_inc(S["setup_copied"], 1)

            def evac_t(base, l, vk, both):
                def fn(t, par):
                    act.wait_ge(S["xt_ready"], TB[base] + t + 1)
                    if base in ("x", 0, 1):
                        seen(act, S["proj_ready"], ATT[base] + t - 1)
                    elif base == "m":
                        seen(act, S["gates_ps"], t - 1)
                        seen(act, S["xct_stored"], t - 1)
                    else:
                        seen(act, S["ht_stored"], int(base[1]) * NT + t - 1)
                        if base == "p0":
                            seen(act, S["logits_ps"], t - 1)
                    if base in (0, 1):
                        src = ps_x[:, 0:P].rearrange("p (s k) -> p s k", s=SPT)
                        for g in range(2):
                            i = nc.scalar.activation(kvt[:, par, :, g, :], src, ACT.Identity, bias=vec(vk + 1, l),
                                                     scale=vec(vk, l))
                    elif vk is None:
                        i = nc.scalar.copy(xts[:, par, :], ps_x[:, 0:P])
                    else:
                        i = nc.scalar.activation(xts[:, par, :], ps_x[:, 0:P], ACT.Identity,
                                                 bias=vec(vk + 1, l), scale=vec(vk, l))
                    if base == "x":
                        src = ps_x[:, P:2 * P].rearrange("p (s k) -> p s k", s=SPT)
                        for g in range(2):
                            i = nc.scalar.copy(kvt[:, par, :, g, :], src)
                    elif both:
                        i = nc.scalar.copy(cts[:, par, :], ps_x[:, P:2 * P])
                    i.then_inc(S["xts_ready"], 1)
                return fn

            def evac_qk(base, l):
                def fn(t, par):
                    act.wait_ge(S["proj_ready"], ATT[base] + t + 1)
                    seen(act, S["scores_ready"], ATT[base] + t - 1)
                    seen(act, S["kbd_ready"], ATT[base] + t - 1)
                    for g in range(SPT):
                        rows_ = slice(64 * g, 64 * g + 64)
                        cols_ = slice(SEQ * g, SEQ * g + SEQ)
                        if l is None:
                            nc.scalar.copy(qbd[rows_, par, :, cols_], ps_a[rows_, 0:P].rearrange("p (r k) -> p r k", r=2))
                        else:
                            for r in range(2):
                                nc.scalar.activation(qbd[rows_, par, r, cols_], ps_a[rows_, r * SEQ:(r + 1) * SEQ],
                                                     ACT.Identity, bias=qkbias(0, l, r, rows_))
                    if l is None:
                        i = nc.scalar.copy(kts[:, par, :, :], ps_a[:, P:2 * P].rearrange("p (r k) -> p r k", r=2))
                    else:
                        for r in range(2):
                            i = nc.scalar.activation(kts[:, par, r, :], ps_a[:, P + r * SEQ:P + (r + 1) * SEQ],
                                                     ACT.Identity, bias=qkbias(1, l, r, slice(0, P)))
                    i.then_inc(S["qk_ready"], 1)
                return fn

            def exp_step(base):
                def fn(t, par):
                    act.wait_ge(S["shifted_ready"], ATT[base] + t + 1)
                    seen(act, S["pt_ready"], ATT[base] + t - 1)
                    nc.scalar.activation(probs[:, par, :], shifted[:, par, :], ACT.Exp, scale=HD ** -0.5
                                         ).then_inc(S["probs_ready"], 1)
                return fn

            def evac_pt(base, width):
                def fn(t, par):
                    act.wait_ge(S["pt_ready"], ATT[base] + t + 1)
                    seen(act, S["o_ready"], ATT[base] + t - 1)
                    nc.scalar.copy(probs_t[:, par, 0:width], ps_t[:, 0:width]).then_inc(S["pts_ready"], 1)
                return fn

            def evac_yt(base, l):
                def fn(t, par):
                    act.wait_ge(S["yt_ready"], ATT[base] + t + 1)
                    seen(act, S["outp_ready"], ATT[base] + t - 1)
                    if l is None:
                        i = nc.scalar.copy(yts[:, par, :], ps_a[:, 0:P])
                    else:
                        i = nc.scalar.activation(yts[:, par, :], ps_a[:, 0:P], ACT.Identity, bias=vec(6, l))
                    i.then_inc(S["yts_ready"], 1)
                return fn

            def attention(base, l):
                pipeline(act, [(L_OUT, evac_yt(base, l)), (L_WEIGH, evac_pt(base, 1024)), (L_SCORES, exp_step(base)),
                               (1, evac_t(base, l, None if l is None else 0, l is None)), (2, evac_qk(base, l))])

            def gelu_block(l):
                def fn(b, par):
                    for e in range(NE):
                        for c in range(CH):
                            k = c + 1 + e * CH
                            act.wait_ge(S["hid_ready"], l * NB * NE * CH + b * (NE * CH) + k)
                            if c == 0:
                                seen(act, S["yexp_ready"], l * NB * NE + b * NE + (e - 1))
                            nc.scalar.activation(gel[:, e % 2, c, :], (ps_s, ps_t)[c // 2][:, (c % 2) * BLK:(c % 2 + 1) * BLK],
                                                 ACT.Gelu, bias=b1col(l, e, c)).then_inc(S["gelu_ready"], 1)
                return fn

            attention("x", None)
            for l in range(LAYERS):
                attention(l, l)
                pipeline(act, [(1, evac_t(f"p{l}", l, 2, False))])
                act.wait_ge(S["route_link"], ROUTE_AT(l, ROUTE_EXP))
                nr = (P, NSEQ)[l]
                nt = (NT, 1)[l]
                nc.scalar.activation(e21[0:nr, 0:nt], e21[0:nr, 0:nt], ACT.Exp).then_inc(S["route_exp"], 1)
                if l == 0:
                    fn = gelu_block(l)
                    fn(0, 0)
                    with act.Fori(1, NB, 1) as b:
                        fn(b, 0)

            def pair_rows(t, par):
                seen(act, S["pair_hid"], t - 1)
                for g in range(2):
                    q = act.value_load(col_of[0:1, bass.ds(2 * t + g, 1)], min_val=0, max_val=TOK - SEQ)
                    i = nc.scalar.copy(hs[:, par, g * SEQ:(g + 1) * SEQ], h_t[:, bass.ds(q, SEQ)])
                i.then_inc(S["hs_ready"], 1)

            def pair_gelu(t, par):
                act.wait_ge(S["pair_hid"], t + 1)
                seen(act, S["pair_out"], t - 1)
                for c in range(CH):
                    i = nc.scalar.activation(gels[:, par, c * P:(c + 1) * P], ps_s3[:, par, c * P:(c + 1) * P],
                                             ACT.Gelu, bias=b1s[:, par, c:c + 1])
                i.then_inc(S["pair_gelu"], 1)
            act.wait_ge(S["tables_ready"], 1)
            act.wait_ge(S["ht_stored"], 2 * NT)
            pipeline(act, [(2, pair_gelu), (1, pair_rows)], NPAIR)

            pipeline(act, [(1, evac_t("m", None, None, True))])
            act.wait_ge(S["gate_link"], 1)
            nc.scalar.activation(gtmp[:, :, :], gtmp[:, :, :], ACT.Exp).then_inc(S["gexp_ready"], 1)
            act.wait_ge(S["gexp_ready"], 1)
            nc.scalar.activation(gtmp[:, :, :], gtmp[:, :, :], ACT.Ln, bias=1.0).then_inc(S["gln_ready"], 1)

            def query_copy(t, par):
                if isinstance(t, int) and t == 0:
                    act.wait_ge(S["xct_stored"], NT)
                seen(act, S["scores_ready"], ATT["m"] + t - 1)
                nc.scalar.copy(xts[:, par, :], tile(h_t, t)).then_inc(S["qcopy_ready"], 1)

            def decay_exp(t, par):
                act.wait_ge(S["shifted_ready"], ATT["m"] + t + 1)
                seen(act, S["ctil_ready"], t - 1)
                nc.scalar.activation(probs[:, par, 0:512], shifted[:, par, 0:512], ACT.Exp).then_inc(S["d_ready"], 1)

            def evac_ctil(t, par):
                act.wait_ge(S["pt_ready"], ATT["m"] + t + 1)
                seen(act, S["o_ready"], ATT["m"] + t - 1)
                nc.scalar.copy(probs_t[:, par, 0:512], (ps_a, ps_x)[par][:, :]).then_inc(S["pts_ready"], 1)

            def store_o(t, par):
                act.wait_ge(S["o_ready"], ATT["m"] + t + 1)
                bank = (ps_o, ps_v)[par]
                for s_ in range(SPT):
                    r_ = slice(64 * s_, 64 * s_ + 64)
                    at = s_ * MH * (MHD + 1)
                    i = nc.scalar.copy(w12[r_, bass.ds(t * (MH * (MHD + 1)), MH * (MHD + 1))],
                                       bank[r_, at:at + MH * (MHD + 1)])
                i.then_inc(S["o_stored"], 1)
            pipeline(act, [(8, store_o), (6, evac_ctil), (3, decay_exp), (2, query_copy)])
            act.wait_ge(S["negmd_ready"], 1)
            nc.scalar.activation(csum[:, :, :], csum[:, :, :], ACT.Exp, scale=-1.0).then_inc(S["emd_ready"], 1)
            act.wait_ge(S["gn_link"], GN_CENTRED)
            nc.scalar.activation(inner[:, :], h_t[:, :], ACT.Square).then_inc(S["square_ready"], 1)

            act.wait_ge(S["amrow_ps"], 1)
            nc.scalar.copy(amrow[:, :], ps_a[0:1, 0:P]).then_inc(S["amrow_done"], 1)

            def evac_q8(t, par):
                act.wait_ge(S["q8t_ps"], t + 1)
                seen(act, S["acc8_ready"], t - 1)
                nc.scalar.copy(q8t[:, par, :], q8ps[:, :]).then_inc(S["q8t_ready"], 1)
            pipeline(act, [(1, evac_q8)])

        @block.tensor
        def _(pe):
            pe.wait_ge(S["pool_const"], CONSTS[0])
            pe.wait_ge(S["weights_loaded"], 16 * N_WLOADS)

            def mm(o, a, b, start=True, stop=True):
                return nc.tensor.matmul(o, a, b, start=start, stop=stop, skip_group_check=True)

            for k in range(4):
                i = nc.tensor.transpose(ps_s[:, k * D:(k + 1) * D], wraw[:, k, :], ident[:, :])
            i.then_inc(S["setup_t"], 1)
            nc.tensor.transpose(ps_t[:, 0:78], vecs[:, :], ident[0:78, 0:78]).then_inc(S["setup_t"], 1)
            nc.tensor.transpose(ps_t[:, 512:520], vecs2[:, :], ident[0:8, 0:8]).then_inc(S["setup_t"], 1)
            for k in range(3):
                i = nc.tensor.transpose(ps_o[:, k * 16:(k + 1) * 16], wg_raw[:, k, :], ident[0:16, 0:16])
            i.then_inc(S["setup_t"], 1)
            mm(ps_a[:, 0:512], ones_row[:, :], rows[:, 0:512]).then_inc(S["setup_t"], 1)
            mm(ps_v[:, 0:12], ones_row[:, :], rows[:, 512:524]).then_inc(S["setup_t"], 1)
            pe.wait_ge(S["dve_setup"], 1)
            nc.tensor.transpose(ps_x[:, 0:P], w8f[:, :], ident[:, :]).then_inc(S["setup_t"], 1)
            pe.wait_ge(S["setup_copied"], 8)

            def ctx_transpose(base, before=None):
                def fn(t, par):
                    seen(pe, S["xts_ready"], TB[base] + t)
                    pe.wait_ge(ctx_loaded[par], (8 * NT if base == "m" else 0) + arrived(t, par, 16))
                    if before and not isinstance(t, int):
                        before(t)
                    nc.tensor.transpose(ps_x[:, P:2 * P], ctx_in[:, par, :], ident[:, :]).then_inc(S["ctx_used"], 1)
                return fn

            def transposes(base, nbase):
                def fn(t, par):
                    pe.wait_ge(S["xn_ready"], nbase + t + 1)
                    seen(pe, S["xts_ready"], TB[base] + t)
                    nc.tensor.transpose(ps_x[:, 0:P], xn[:, par, :], ident[:, :]).then_inc(S["xt_ready"], 1)
                return fn

            def project(base, l):
                w = (lambda k: wx[:, k, :]) if l is None else (lambda k: wself[:, l, k, :])

                def fn(t, par):
                    pe.wait_ge(S["xts_ready"], TB[base] + t + 1)
                    seen(pe, S["yts_ready"], ATT[base] + t + 3 - L_OUT)
                    seen(pe, S["qk_ready"], ATT[base] + t)
                    for k in range(2):
                        for g in range(SPT):
                            src = xts[:, par, g * SEQ:(g + 1) * SEQ] if k == 0 and l is None else kvt[:, par, g, 0, :]
                            for r in range(2):
                                at = k * P + r * SEQ
                                mm(ps_a[g * 64:(g + 1) * 64, at:at + SEQ], w(k)[:, r * 64:(r + 1) * 64], src)
                    seen(pe, S["x_updated"], UPD[base] + t + 3 - L_OUT)
                    seen(pe, S["vbd_ready"], ATT[base] + t)
                    for g in range(SPT):
                        i = mm(ps_v[:, g * D:(g + 1) * D], kvt[:, par, g, :, :].rearrange("p a k -> p (a k)"), w(2))
                    i.then_inc(S["proj_ready"], 1)
                return fn

            def scores(base, masked):
                def fn(t, par):
                    pe.wait_ge(S["qk_ready"], ATT[base] + t + 1)
                    pe.wait_ge(S["kbd_ready"], ATT[base] + t + 1)
                    seen(pe, S["shifted_ready"], ATT[base] + t)
                    if masked:
                        for r in range(2):
                            mm(ps_s3[:, r, :], identb[:, :], causal[:, :, :].rearrange("p a b -> p (a b)"),
                               True, False)
                    for r in range(2):
                        i = mm(ps_s3[:, r, :], qbd[:, par, r, :],
                               kbd[:, par, r * 4:(r + 1) * 4, :].rearrange("p a k -> p (a k)"), not masked, True)
                    i.then_inc(S["scores_ready"], 1)
                return fn

            def transpose_probs(base, n, src):
                def fn(t, par):
                    if base == "m":
                        pe.wait_ge(S["ctil_ready"], t + 1)
                    else:
                        pe.wait_ge(S["probs_ready"], ATT[base] + t + 1)
                    seen(pe, S["pts_ready"], ATT[base] + t)
                    for j in range(n):
                        i = nc.tensor.transpose(ps_t[:, j * P:(j + 1) * P], src[:, par, j * P:(j + 1) * P], ident[:, :])
                    i.then_inc(S["pt_ready"], 1)
                return fn

            def weigh(base):
                def fn(t, par, slot):
                    pe.wait_ge(S["pts_ready"], ATT[base] + t + 1)
                    pe.wait_ge(S["vbd_ready"], ATT[base] + t + 1)
                    seen(pe, S["y_ready"], ATT[base] + t)
                    o = ps_o[:, 0:SPT * HEADS * (HD + 1)].rearrange("p (s n) -> p s n", s=SPT)
                    for j in range(HEADS // 2):
                        a = 2 * j * (HD + 1)
                        i = mm(o[:, :, a:a + 2 * (HD + 1)], probs_t[:, par, j * P:(j + 1) * P],
                               vbd[:, slot, :, 2 * j:2 * j + 2, :].rearrange("p s h d -> p s (h d)"))
                    i.then_inc(S["o_ready"], 1)
                return fn

            def transpose_y(base):
                def fn(t, par):
                    pe.wait_ge(S["y_ready"], ATT[base] + t + 1)
                    pe.wait_ge(S["qk_ready"], ATT[base] + capped(t + L_OUT - 2, NT))
                    seen(pe, S["yts_ready"], ATT[base] + t)
                    nc.tensor.transpose(ps_a[:, 0:P], y[:, par, :], ident[:, :]).then_inc(S["yt_ready"], 1)
                return fn

            def out_project(base, l):
                def fn(t, par):
                    pe.wait_ge(S["yts_ready"], ATT[base] + t + 1)
                    pe.wait_ge(S["vbd_ready"], ATT[base] + capped(t + L_OUT - 2, NT))
                    seen(pe, S["x_updated"], UPD[base] + t)
                    if l is None:
                        i = mm(ps_v[:, 0:D], yts[:, par, :], wx[:, 3, :])
                    else:
                        mm(ps_v[:, 0:D], yts[:, par, :], wself[:, l, 3, :], True, False)
                        i = mm(ps_v[:, 0:D], ones_row[:, :], rows[:, R_BO + l * D:R_BO + (l + 1) * D], False, True)
                    i.then_inc(S["outp_ready"], 1)
                return fn

            def attention(base, l, nbase):
                early = [] if l is not None else [(1, ctx_transpose(base))]
                pipeline(pe, [(L_SCORES, scores(base, l is not None)), (L_OUT, transpose_y(base)),
                              (L_WEIGH, transpose_probs(base, HEADS // 2, probs)), (L_OUT, out_project(base, l))]
                             + early + [(1, transposes(base, nbase)), (2, project(base, l)),
                                        (L_WEIGH, weigh(base), VBUFS)])

            def logits_step(t, par):
                pe.wait_ge(S["xts_ready"], TB["p0"] + t + 1)
                seen(pe, S["logits_sb"], t)
                mm(ps_a[:, 0:NE], xts[:, par, :], gatew[:, 0, :], True, False)
                mm(ps_a[:, 0:NE], ones_row[:, :], rows[:, R_GB0:R_GB0 + NE], False, True
                   ).then_inc(S["logits_ps"], 1)

            def expert_block(l):
                def hidden(b, e):
                    for c in range(CH):
                        seen(pe, S["gelu_ready"], l * NB * NE * CH + b * (NE * CH) + (e - 1) * CH + c + 1)
                        mm((ps_s, ps_t)[c // 2][:, (c % 2) * BLK:(c % 2 + 1) * BLK], w1[:, e, c * P:(c + 1) * P],
                           h_t[:, bass.ds(b * BLK, BLK)]).then_inc(S["hid_ready"], 1)

                def second(b, e):
                    bank = (ps_o, ps_v)[e % 2]
                    seen(pe, S["acc_ready"], l * NB * NE + b * NE + (e - 1))
                    mm(bank[:, :], ones3[:, :], b2rows[:, e, :, :].rearrange("p s d -> p (s d)"), True, False)
                    for c in range(CH):
                        pe.wait_ge(S["gelu_ready"], l * NB * NE * CH + b * (NE * CH) + e * CH + c + 1)
                        for s in range(SUB):
                            i = mm(bank[:, s * D:(s + 1) * D], gel[:, e % 2, c, s * P:(s + 1) * P],
                                   w2[:, e, c, :], False, c == CH - 1)
                    i.then_inc(S["yexp_ready"], 1)

                def fn(b, par):
                    hidden(b, 0)
                    for e in range(NE):
                        if e + 1 < NE:
                            hidden(b, e + 1)
                        second(b, e)
                return fn

            attention("x", None, CROSS)
            for l in range(LAYERS):
                attention(l, l, (SELF0, SELF1)[l])
                steps = [(1, transposes(f"p{l}", (PRE0, PRE1)[l]))]
                if l == 0:
                    steps.append((1, logits_step))
                pipeline(pe, steps)
                if l == 1:
                    pe.wait_ge(S["hmean_ready"], 1)
                    mm(ps_a[0:NSEQ, 0:NE], hmean[:, :], gatew[:, 1, :]).then_inc(S["seqlog_ready"], 1)
                    pe.wait_ge(S["route_link"], ROUTE_AT(1, ROUTE_COUNTS))
                    mm(ps_a[0:NSEQ, 0:NE], before[:, :], counts[:, :])
                    mm(ps_a[:, NE:2 * NE], ones_seq[:, :], counts[:, :]).then_inc(S["place_ps"], 1)
                    pe.wait_ge(S["route_link"], ROUTE_AT(1, ROUTE_LINKS[1]))
                    nc.tensor.transpose(ps_o[0:NE, 0:NSEQ], cw[0:NSEQ, 0, :], ident[0:NSEQ, 0:NSEQ]
                                        ).then_inc(S["place_ps"], 1)
                    pe.wait_ge(S["place_link"], 1)
                    mm(ps_v[:, 0:NSEQ], b2w[:, :], cw_t[:, :]).then_inc(S["place_ps"], 1)
                    pe.wait_ge(S["place_link"], PLACE_TABLES)
                    for v in range(2):
                        for k in range(2):
                            i = mm(ps_x[:, v * PLACES:(v + 1) * PLACES], ones_seq[:, :], at_place[:, v, k, :],
                                   k == 0, k == 1)
                    i.then_inc(S["place_ps"], 1)
                    break
                pe.wait_ge(S["ffn_w_loaded"], 16 * 5)
                pe.wait_ge(S["route_done"], 1)
                pe.wait_ge(S["ht_stored"], NT)
                fn = expert_block(l)
                fn(0, 0)
                with pe.Fori(1, NB, 1) as b:
                    fn(b, 0)
                pe.wait_ge(S["acc_ready"], NB * NE)

            def pair_hidden(t, par):
                pe.wait_ge(S["hs_ready"], t + 1)
                pe.wait_ge(S["w1s_ready"], t + 1)
                seen(pe, S["pair_gelu"], t - 1)
                for c in range(CH):
                    i = mm(ps_s3[:, par, c * P:(c + 1) * P], w1s[:, par, c * P:(c + 1) * P], hs[:, par, :])
                i.then_inc(S["pair_hid"], 1)

            def pair_second(t, par):
                pe.wait_ge(S["pair_gelu"], t + 1)
                pe.wait_ge(S["w2s_ready"], t + 1)
                seen(pe, S["pair_added"], 2 * (t - 1))
                for c in range(CH):
                    i = mm((ps_o, ps_v)[par][:, 0:P], w2s[:, par, c * D:(c + 1) * D], gels[:, par, c * P:(c + 1) * P],
                           c == 0, c == CH - 1)
                i.then_inc(S["pair_out"], 1)
            pe.wait_ge(S["tables_ready"], 1)
            pipeline(pe, [(1, pair_hidden), (2, pair_second)], NPAIR)
            pe.wait_ge(S["pair_added"], 2 * NPAIR)
            for b in range(NB):
                seen(pe, S["rows_added"], b - 1)
                for k in range(SUB):
                    c = (b * SUB + k) * P
                    i = nc.tensor.transpose(ps_s3[:, b % 2, k * P:(k + 1) * P], inner[:, c:c + P], ident[:, :])
                i.then_inc(S["rows_ps"], 1)

            def gates_step(t, par):
                pe.wait_ge(S["xts_ready"], TB["m"] + t + 1)
                seen(pe, S["gates_sb"], t)
                for k, a in enumerate((xts, cts, cts)):
                    mm(ps_a[:, 0:16], a[:, par, :], wg_t[:, k, :], k == 0, False)
                mm(ps_a[:, 0:16], ones_row[:, :], rows[:, R_GI:R_GI + 16], False, True).then_inc(S["gates_ps"], 1)
            pipeline(pe, [(2, gates_step), (1, ctx_transpose("m")), (1, transposes("m", MLSTM))])
            pe.wait_ge(S["gate_link"], 2)
            mm(ps_v[:, 0:NT * MH], block_tri[:, :], lsig[:, :, :].rearrange("p t h -> p (t h)")
               ).then_inc(S["csum_ps"], 1)
            pe.wait_ge(S["avec_ready"], 1)

            def decay_step(t, par):
                pe.wait_ge(S["adiag_ready"], t + 1)
                seen(pe, S["shifted_ready"], ATT["m"] + t - 1)
                a = ps_t[:, par * 512:(par + 1) * 512]
                mm(a, identb[:, :], causal[:, :, :].rearrange("p a b -> p (a b)"), True, False)
                mm(a, block_ones[:, :], adiag[:, par, :, :].rearrange("p a b -> p (a b)"), False, True
                   ).then_inc(S["a_ready"], 1)

            def scores16(t, par):
                for s_ in range(SPT):
                    for r_ in range(2):
                        i = mm(ps_s3[s_ * 64:(s_ + 1) * 64, r_, 0:4 * SEQ],
                               xts[r_ * 64:(r_ + 1) * 64, par, s_ * SEQ:(s_ + 1) * SEQ],
                               kbd[r_ * 64:(r_ + 1) * 64, par, 0:4, s_ * SEQ:(s_ + 1) * SEQ])
                i.then_inc(S["scores_ready"], 1)

            def scores16_need(t, par):
                pe.wait_ge(S["qcopy_ready"], t + 1)
                pe.wait_ge(S["kbd_ready"], ATT["m"] + t + 1)
                seen(pe, S["ctil_ready"], t)

            def transpose_ctil(t, par):
                pe.wait_ge(S["ctil_ready"], t + 1)
                seen(pe, S["pts_ready"], ATT["m"] + t - 1)
                for j in range(MH // 2):
                    i = nc.tensor.transpose((ps_a, ps_x)[par][:, j * P:(j + 1) * P], ctil[:, par, j * P:(j + 1) * P],
                                            ident[:, :])
                i.then_inc(S["pt_ready"], 1)

            def weigh16(t, par):
                pe.wait_ge(S["pts_ready"], ATT["m"] + t + 1)
                pe.wait_ge(S["vb16_ready"], t + 1)
                seen(pe, S["o_stored"], t - 1)
                o = (ps_o, ps_v)[par][:, 0:SPT * MH * (MHD + 1)].rearrange("p (s n) -> p s n", s=SPT)
                for j in range(MH // 2):
                    a = 2 * j * (MHD + 1)
                    i = mm(o[:, :, a:a + 2 * (MHD + 1)], probs_t[:, par, j * P:(j + 1) * P],
                           vbd16[:, par, :, 2 * j:2 * j + 2, :].rearrange("p s h d -> p s (h d)"))
                i.then_inc(S["o_ready"], 1)
            pipeline(pe, [(7, weigh16), (5, transpose_ctil), (3, scores16_need), (1, decay_step), (3, scores16)])

            pe.wait_ge(S["amax_ready"], 1)
            nc.tensor.transpose(ps_a[0:1, 0:P], amax[:, :], ident[:, :]).then_inc(S["amrow_ps"], 1)
            pe.wait_ge(S["scale_ready"], 1)
            mm(ps_v[:, 0:1], ones_row[:, :], am1[:, 0:1]).then_inc(S["scale_ps"], 1)

            def q8_transpose(t, par):
                pe.wait_ge(S["q8_ready"], t + 1)
                seen(pe, S["q8t_ready"], t)
                nc.tensor.transpose(q8ps[:, :], q8[:, par, :], identb[:, :]).then_inc(S["q8t_ps"], 1)

            def q8_product(t, par):
                pe.wait_ge(S["q8t_ready"], t + 1)
                seen(pe, S["o1_ready"], t)
                mm(ps_o[:, 0:D], q8t[:, par, :], w8t[:, :]).then_inc(S["acc8_ready"], 1)
            pipeline(pe, [(1, q8_transpose), (2, q8_product)])

        @block.vector
        def _(dve):
            V = nc.vector
            dve.wait_ge(S["weights_loaded"], 16 * N_WLOADS)
            V.tensor_copy(w8f[:, :], w8[:, :].bitcast(I8)).then_inc(S["dve_setup"], 1)
            dve.wait_ge(S["setup_copied"], 8)
            V.tensor_scalar(coef[:, 0:1], tg[:, 0:1], ROW0_PAIRS, None, ALU.mult).then_inc(S["dve_setup"], 1)
            V.tensor_scalar(rowb[:, 0:2 * D], rowb[:, 0:2 * D], tg[:, 1:2], None, ALU.mult).then_inc(S["dve_setup"], 1)
            dve.wait_ge(S["dve_setup"], 3)
            dve.wait_ge(S["x_loaded"], 16)
            dve.wait_ge(S["pool_const"], CONSTS[0])

            def row_stats(src, k):
                def sums(t, par):
                    V.bn_stats(stats[:, bass.ds(t, 1), :].rearrange("p a s -> p (a s)"), tile(src, t)
                               ).then_inc(S["bn_done"], 1)
                pipeline(dve, [(0, sums)], unroll=8)
                n = [STAT_LINKS * k]

                def link(i):
                    n[0] += 1
                    i.then_inc(S["stat_link"], 1)
                    dve.wait_ge(S["stat_link"], n[0])
                dve.wait_ge(S["bn_done"], NT * (k + 1))
                even, odd = stats[:, :, 1], stats[:, :, 4]
                link(V.tensor_tensor(half_gap[:, :], even, odd, ALU.subtract))
                link(V.tensor_tensor(mean[:, :], even, odd, ALU.add))
                link(V.tensor_scalar(mean[:, :], mean[:, :], 0.5, None, ALU.mult))
                link(V.scalar_tensor_tensor(half_gap[:, :], half_gap[:, :], 0.25, half_gap[:, :], ALU.mult, ALU.mult))
                link(V.tensor_tensor(var[:, :], stats[:, :, 2], stats[:, :, 5], ALU.add))
                link(V.scalar_tensor_tensor(var[:, :], var[:, :], 1.0 / D, half_gap[:, :], ALU.mult, ALU.add))
                V.tensor_scalar(vare[:, :], var[:, :], EPS, None, ALU.add).then_inc(S["vare_ready"], 1)
                assert n[0] == STAT_LINKS * (k + 1)
                dve.wait_ge(S["rstd_ready"], k + 1)

            def norm_step(src, base, tb):
                def fn(t, par):
                    seen(dve, S["xt_ready"], TB[tb] + t - 1)
                    V.tensor_scalar(xn[:, par, :], tile(src, t), mean[:, bass.ds(t, 1)], rstd[:, bass.ds(t, 1)],
                                    ALU.subtract, ALU.mult).then_inc(S["xn_ready"], 1)
                return fn

            def vbd_step(base):
                def fn(t, par, slot):
                    dve.wait_ge(S["proj_ready"], ATT[base] + t + 1)
                    seen(dve, S["o_ready"], ATT[base] + t + 1 - VBUFS)
                    V.tensor_tensor(vbd[:, slot, :, :, 0:HD].rearrange("p s h d -> p (s h) d"),
                                    ps_v[:, 0:2 * D].rearrange("p (n d) -> p n d", d=HD), vmask[:, :, :],
                                    ALU.mult).then_inc(S["vbd_ready"], 1)
                return fn

            def shift_step(base):
                def fn(t, par):
                    dve.wait_ge(S["scores_ready"], ATT[base] + t + 1)
                    s3 = ps_s[:, :].rearrange("p (h k) -> p h k", k=SEQ)
                    V.tensor_reduce(rowmax[:, par, :], s3, AXX, ALU.max).then_inc(S["max_ready"], 1)
                    dve.wait_ge(S["max_ready"], ATT[base] + t + 1)
                    seen(dve, S["probs_ready"], ATT[base] + t - 1)
                    V.tensor_tensor(shifted[:, par, :].rearrange("p (h k) -> p h k", k=SEQ), s3,
                                    rowmax[:, par, :].unsqueeze(2).to_broadcast([P, HEADS, SEQ]), ALU.subtract
                                    ).then_inc(S["shifted_ready"], 1)
                return fn

            def y_step(base):
                def fn(t, par):
                    dve.wait_ge(S["o_ready"], ATT[base] + t + 1)
                    seen(dve, S["yt_ready"], ATT[base] + t - 1)
                    o = ps_o[:, 0:SPT * HEADS * (HD + 1)].rearrange("p (s h d) -> p s h d", s=SPT, h=HEADS)
                    for s in range(SPT):
                        r = slice(64 * s, 64 * s + 64)
                        i = V.reciprocal(recip[r, par, :].unsqueeze(2), o[r, s, :, HD:HD + 1])
                    i.then_inc(S["recip_ready"], 1)
                    dve.wait_ge(S["recip_ready"], ATT[base] + t + 1)
                    for s in range(SPT):
                        r = slice(64 * s, 64 * s + 64)
                        i = V.tensor_tensor(y[r, par, :].rearrange("p (h d) -> p h d", d=HD), o[r, s, :, 0:HD],
                                            recip[r, par, :].unsqueeze(2).to_broadcast([64, HEADS, HD]), ALU.mult)
                    i.then_inc(S["y_ready"], 1)
                return fn

            def add_step(base, dst, scale):
                def fn(t, par):
                    dve.wait_ge(S["outp_ready"], ATT[base] + t + 1)
                    V.scalar_tensor_tensor(tile(dst, t), ps_v[:, 0:D], scale, tile(dst, t), ALU.mult, ALU.add
                                           ).then_inc(S["x_updated"], 1)
                return fn

            def attention(base, src, nbase, scale):
                row_stats(src, nbase // NT)
                pipeline(dve, [(L_OUT, y_step(base)), (1, norm_step(src, nbase, base)), (L_SCORES, shift_step(base)),
                               (L_OUT, add_step(base, src, scale)), (2, vbd_step(base), VBUFS)])

            def plain_norm(src, dst, base, upd):
                def fn(t, par):
                    V.tensor_scalar(tile(dst, t), tile(src, t), mean[:, bass.ds(t, 1)], rstd[:, bass.ds(t, 1)],
                                    ALU.subtract, ALU.mult).then_inc(S["xn_ready"], 1)
                dve.wait_ge(S["x_updated"], upd)
                row_stats(src, base // NT)
                pipeline(dve, [(0, fn)], unroll=8)
                dve.wait_ge(S["xn_ready"], base + NT)

            def best_two(rows_, n, l):
                k = [ROUTE_AT(l, 0)]

                def link(i):
                    k[0] += 1
                    i.then_inc(S["route_link"], 1)
                    dve.wait_ge(S["route_link"], k[0])
                r = slice(0, rows_)
                lg, c1, c2 = logits[r, 0:n, :], cw[r, 0:n, :], oneh[r, 0:n, :]

                def wide(v):
                    return v[r, 0:n].unsqueeze(2).to_broadcast([rows_, n, NE])

                def first_best(best, hot):
                    link(V.tensor_reduce(best[r, 0:n], lg, AXX, ALU.max))
                    link(V.tensor_tensor(hot, lg, wide(best), ALU.is_equal))
                    link(V.scalar_tensor_tensor(cand[r, 0:n, :], hot, -float(NE), iota8[r, 0:n, :], ALU.mult, ALU.add))
                    link(V.tensor_reduce(first[r, 0:n], cand[r, 0:n, :], AXX, ALU.min))
                    link(V.tensor_tensor(hot, cand[r, 0:n, :], wide(first), ALU.is_equal))

                first_best(best1, c1)
                link(V.scalar_tensor_tensor(lg, c1, NEG, lg, ALU.mult, ALU.add))
                first_best(best2, c2)
                link(V.tensor_tensor(e21[r, 0:n], best2[r, 0:n], best1[r, 0:n], ALU.subtract))
                if l == 1:
                    link(V.tensor_copy(chosen[:, 0:1, :], c1))
                    link(V.tensor_copy(chosen[:, 1:2, :], c2))
                    link(V.tensor_tensor(counts[:, :].unsqueeze(1), c1, c2, ALU.add))
                dve.wait_ge(S["route_exp"], l + 1)
                link(V.tensor_scalar(tw2[r, 0:n], e21[r, 0:n], 1.0, None, ALU.add))
                link(V.reciprocal(tw1[r, 0:n], tw2[r, 0:n]))
                link(V.tensor_tensor(tw2[r, 0:n], e21[r, 0:n], tw1[r, 0:n], ALU.mult))
                link(V.tensor_tensor(c1, c1, wide(tw1), ALU.mult))
                link(V.tensor_tensor(c2, c2, wide(tw2), ALU.mult))
                i = V.tensor_tensor(c1, c1, c2, ALU.add)
                if l == 0:
                    i.then_inc(S["route_done"], 1)
                else:
                    link(i)
                assert k[0] == ROUTE_AT(l, ROUTE_LINKS[l])

            def top_step(t, par):
                dve.wait_ge(S["logits_ps"], t + 1)
                V.tensor_copy(logits[:, bass.ds(t, 1), :], ps_a[:, 0:NE].unsqueeze(1)).then_inc(S["logits_sb"], 1)

            def split_b2(l):
                k = [B2_LINKS * l]

                def link(i):
                    k[0] += 1
                    i.then_inc(S["rs_link"], 1)
                    dve.wait_ge(S["rs_link"], k[0])
                dve.wait_ge(S["ffn_w_loaded"], 16 * 5 * (l + 1))
                link(V.tensor_copy(b2hi[:, :, :], b2src[:, :, :]))
                link(V.tensor_tensor(b2a[:, :, :], b2src[:, :, :], b2hi[:, :, :], ALU.subtract))
                link(V.tensor_copy(b2mid[:, :, :], b2a[:, :, :]))
                link(V.tensor_tensor(b2lo[:, :, :], b2a[:, :, :], b2mid[:, :, :], ALU.subtract))
                link(V.tensor_scalar(b2a[:, :, :], b2hi[:, :, :], row3[:, 0:1], None, ALU.mult))
                link(V.scalar_tensor_tensor(b2a[:, :, :], b2mid[:, :, :], row3[:, 1:2], b2a[:, :, :], ALU.mult, ALU.add))
                link(V.scalar_tensor_tensor(b2a[:, :, :], b2lo[:, :, :], row3[:, 2:3], b2a[:, :, :], ALU.mult, ALU.add))
                for s in range(SUB):
                    link(V.tensor_copy(b2rows[:, :, s, :], b2a[:, :, :]))
                assert k[0] == B2_LINKS * (l + 1)

            def weigh_experts(l):
                def fn(b, par):
                    for e in range(NE):
                        bank = (ps_o, ps_v)[e % 2]
                        dve.wait_ge(S["yexp_ready"], l * NB * NE + b * NE + (e + 1))
                        seen(dve, S["acc_ready"], l * NB * NE + b * NE + e)
                        for s in range(SUB):
                            t = b * SUB + s
                            i = V.scalar_tensor_tensor(tile(inner, t), bank[:, s * D:(s + 1) * D],
                                                       cw[:, bass.ds(t, 1), e], tile(inner, t), ALU.mult, ALU.add)
                        i.then_inc(S["acc_ready"], 1)
                return fn

            attention("x", x_res, CROSS, coef[:, 0:1])
            plain_norm(x_res, inner, NORM0, UPD["x"] + NT)
            for l in range(LAYERS):
                attention(l, inner, (SELF0, SELF1)[l], 1.0)
                dve.wait_ge(S["x_updated"], UPD[l] + NT)
                nb_ = (PRE0, PRE1)[l]
                row_stats(inner, nb_ // NT)
                steps = [(0, norm_step(inner, nb_, f"p{l}"))]
                if l == 0:
                    steps.append((1, top_step))
                pipeline(dve, steps)
                if l == 0:
                    dve.wait_ge(S["logits_sb"], NT)
                    split_b2(0)
                    best_two(P, NT, 0)
                    dve.wait_ge(S["route_done"], 1)
                else:
                    dve.wait_ge(S["ht_stored"], 2 * NT)
                    V.tensor_reduce(hmean[:, :], h_t[:, :].rearrange("p (q i) -> p q i", i=SEQ), AXX, ALU.add
                                    ).then_inc(S["hmean_ready"], 1)
                    dve.wait_ge(S["seqlog_ready"], 1)
                    V.scalar_tensor_tensor(logits[0:NSEQ, 0, :], ps_a[0:NSEQ, 0:NE], 1.0 / SEQ,
                                           rowb[0:NSEQ, R_GB1:R_GB1 + NE], ALU.mult, ALU.add).then_inc(S["logits_sb"], 1)
                    dve.wait_ge(S["logits_sb"], NT + 1)
                    best_two(NSEQ, 1, 1)
                    break
                fn = weigh_experts(l)
                fn(0, 0)
                with dve.Fori(1, NB, 1) as b:
                    fn(b, 0)
                dve.wait_ge(S["acc_ready"], NB * NE)

            def make_tables():
                k = [0]

                def link(i):
                    k[0] += 1
                    i.then_inc(S["place_link"], 1)
                    dve.wait_ge(S["place_link"], k[0])
                dve.wait_ge(S["place_ps"], 2)
                link(V.tensor_copy(cw_t[:, :], ps_o[0:NE, 0:NSEQ]))
                link(V.tensor_scalar(tiles_of[:, :], ps_a[:, NE:2 * NE], 0.5, 0.25, ALU.mult, ALU.add))
                link(V.tensor_scalar(tiles_of[:, :], tiles_of[:, :], MAGIC, None, ALU.add))
                link(V.tensor_scalar(upto_a[:, NE:2 * NE], tiles_of[:, :], MAGIC, None, ALU.subtract))
                for src, dst, d in ((upto_a, upto_b, 1), (upto_b, upto_a, 2), (upto_a, upto_b, 4)):
                    link(V.tensor_tensor(dst[:, NE:2 * NE], src[:, NE:2 * NE], src[:, NE - d:2 * NE - d], ALU.add))
                link(V.scalar_tensor_tensor(place_base[:, :], upto_b[0:NSEQ, NE - 1:2 * NE - 1], 2.0,
                                            ps_a[0:NSEQ, 0:NE], ALU.mult, ALU.add))
                link(V.tensor_tensor(chosen_place[:, :, :], chosen[:, :, :],
                                     place_base[:, :].unsqueeze(1).to_broadcast([NSEQ, 2, NE]), ALU.mult))
                link(V.tensor_reduce(place[:, :], chosen_place[:, :, :], AXX, ALU.add))
                for c, w in enumerate((tw1, tw2)):
                    link(V.tensor_scalar(at_place[:, 0, c, :], place_no[:, :], place[:, c:c + 1], w[0:NSEQ, 0:1],
                                         ALU.is_equal, ALU.mult))
                    link(V.tensor_scalar(at_place[:, 1, c, :], place_no[:, :], place[:, c:c + 1], seq_col[:, :],
                                         ALU.is_equal, ALU.mult))
                assert k[0] == PLACE_TABLES
                link(V.tensor_tensor(past[:, :, :], pair_no[:, :, :],
                                     upto_b[0:1, NE:2 * NE].unsqueeze(1).to_broadcast([1, NPAIR, NE]), ALU.is_ge))
                link(V.tensor_reduce(expert_f[:, :], past[:, :, 0:NE - 1], AXX, ALU.add))
                link(V.tensor_copy(expert_of[:, :], expert_f[:, :]))
                link(V.scalar_tensor_tensor(x_res[:, :], inner[:, :], tg[:, 2:3], x_res[:, :], ALU.mult, ALU.add))
                dve.wait_ge(S["place_ps"], 3)
                link(V.tensor_copy(inner[:, :].rearrange("p (q i) -> p q i", i=SEQ),
                                   ps_v[:, 0:NSEQ].unsqueeze(2).to_broadcast([P, NSEQ, SEQ])))
                dve.wait_ge(S["place_ps"], 4)
                link(V.tensor_copy(place_w[:, :], ps_x[:, 0:PLACES]))
                V.tensor_copy(col_of[:, :], ps_x[0:1, PLACES:2 * PLACES]).then_inc(S["tables_ready"], 1)
                dve.wait_ge(S["tables_ready"], 1)
            make_tables()

            def first_weights(t, par):
                seen(dve, S["pair_gelu"], t - 1)
                e = dve.value_load(expert_of[0:1, bass.ds(t, 1)], min_val=0, max_val=NE - 1)
                V.tensor_copy(b1s[:, par, :], vec_t[:, bass.ds(e * CH + (14 + NE * CH), CH)])
                V.tensor_copy(w1s[:, par, :].unsqueeze(1), w1[:, bass.ds(e, 1), :]).then_inc(S["w1s_ready"], 1)

            def add_pair(t, par):
                dve.wait_ge(S["pair_out"], t + 1)
                for g in range(2):
                    q = dve.value_load(col_of[0:1, bass.ds(2 * t + g, 1)], min_val=0, max_val=TOK - SEQ)
                    seen(dve, S["pair_added"], 2 * t + g)
                    V.scalar_tensor_tensor(inner[:, bass.ds(q, SEQ)], (ps_o, ps_v)[par][:, g * SEQ:(g + 1) * SEQ],
                                           place_w[:, bass.ds(2 * t + g, 1)], inner[:, bass.ds(q, SEQ)], ALU.mult,
                                           ALU.add).then_inc(S["pair_added"], 1)
            dve.wait_ge(S["ffn_w_loaded"], 16 * 7)
            pipeline(dve, [(0, first_weights), (3, add_pair)], NPAIR)
            for b in range(NB):
                dve.wait_ge(S["rows_ps"], b + 1)
                c = slice(b * BLK, (b + 1) * BLK)
                V.scalar_tensor_tensor(x_res[:, c], ps_s3[:, b % 2, :], tg[:, 2:3], x_res[:, c], ALU.mult, ALU.add
                                       ).then_inc(S["rows_added"], 1)
            dve.wait_ge(S["rows_added"], NB)

            def gates_copy(t, par):
                dve.wait_ge(S["gates_ps"], t + 1)
                V.tensor_copy(gates[:, bass.ds(t, 1), :], ps_a[:, 0:16].unsqueeze(1)).then_inc(S["gates_sb"], 1)
            row_stats(x_res, MLSTM // NT)
            pipeline(dve, [(0, norm_step(x_res, MLSTM, "m")), (2, gates_copy)])
            dve.wait_ge(S["gates_sb"], NT)
            gi, gf = gates[:, :, 0:MH], gates[:, :, MH:2 * MH]
            V.scalar_tensor_tensor(gtmp[:, :, :], gf, -1.0, gf, ALU.mult, ALU.min).then_inc(S["gate_link"], 1)
            dve.wait_ge(S["gln_ready"], 1)
            V.scalar_tensor_tensor(lsig[:, :, :], gf, 0.0, gtmp[:, :, :], ALU.min, ALU.subtract
                                   ).then_inc(S["gate_link"], 1)
            dve.wait_ge(S["csum_ps"], 1)
            V.tensor_copy(csum[:, :, :].rearrange("p t h -> p (t h)"), ps_v[:, 0:NT * MH]).then_inc(S["gate_link"], 1)
            dve.wait_ge(S["gate_link"], 3)
            V.tensor_tensor(avec[:, :, :], gi, csum[:, :, :], ALU.subtract).then_inc(S["avec_ready"], 1)

            def decay_shift(t, par):
                dve.wait_ge(S["a_ready"], t + 1)
                a3 = ps_t[:, par * 512:(par + 1) * 512].rearrange("p (h k) -> p h k", k=SEQ)
                V.tensor_reduce(rowmax[:, par, 0:MH], a3, AXX, ALU.max).then_inc(S["max_ready"], 1)
                dve.wait_ge(S["max_ready"], ATT["m"] + t + 1)
                seen(dve, S["d_ready"], t - 1)
                V.tensor_copy(maxes[:, bass.ds(t, 1), :], rowmax[:, par:par + 1, 0:MH])
                V.tensor_tensor(shifted[:, par, 0:512].rearrange("p (h k) -> p h k", k=SEQ), a3,
                                rowmax[:, par, 0:MH].unsqueeze(2).to_broadcast([P, MH, SEQ]), ALU.subtract
                                ).then_inc(S["shifted_ready"], 1)

            def ctil_step(t, par):
                dve.wait_ge(S["d_ready"], t + 1)
                dve.wait_ge(S["scores_ready"], ATT["m"] + t + 1)
                seen(dve, S["pt_ready"], ATT["m"] + t - 1)
                V.tensor_tensor(ctil[:, par, :].rearrange("p (r n) -> p r n", r=2), ps_s3[:, :, 0:4 * SEQ],
                                probs[:, par, 0:512].rearrange("p (r n) -> p r n", r=2), ALU.mult
                                ).then_inc(S["ctil_ready"], 1)
            pipeline(dve, [(4, ctil_step), (2, decay_shift)])

            def head_norms():
                k = [0]

                def link(i):
                    k[0] += 1
                    i.then_inc(S["gn_link"], 1)
                    dve.wait_ge(S["gn_link"], k[0])

                def flat(a):
                    return a[:, :, :].rearrange("p t h -> p (t h)")

                def wide(a):
                    return flat(a).unsqueeze(2).to_broadcast([P, NT * MH, MHD])
                y3 = h_t[:, :].rearrange("p (n d) -> p n d", d=MHD)
                dve.wait_ge(S["shifted_ready"], ATT["m"] + NT)
                V.tensor_tensor(csum[:, :, :], csum[:, :, :], maxes[:, :, :], ALU.add).then_inc(S["negmd_ready"], 1)
                dve.wait_ge(S["o_stored"], NT)
                o3d = w12[:, 0:NT * MH * (MHD + 1)].rearrange("p (n d) -> p n d", d=MHD + 1)
                link(V.tensor_scalar(flat(avec).unsqueeze(2), o3d[:, :, MHD:MHD + 1], 0.25, None, ALU.mult))
                link(V.scalar_tensor_tensor(flat(avec), flat(avec), -1.0, flat(avec), ALU.mult, ALU.max))
                dve.wait_ge(S["emd_ready"], 1)
                link(V.tensor_tensor(flat(avec), flat(avec), flat(csum), ALU.max))
                link(V.tensor_scalar(flat(avec), flat(avec), 1e-6, 4.0, ALU.add, ALU.mult))
                link(V.reciprocal(flat(maxes), flat(avec)))
                link(V.tensor_tensor(y3, o3d[:, :, 0:MHD], wide(maxes), ALU.mult))
                V.tensor_reduce(flat(lsig), y3, AXX, ALU.add).then_inc(S["gate_link"], 1)
                dve.wait_ge(S["gate_link"], 4)
                link(V.scalar_tensor_tensor(y3, wide(lsig), -1.0 / MHD, y3, ALU.mult, ALU.add))
                assert k[0] == GN_CENTRED
                dve.wait_ge(S["square_ready"], 1)
                link(V.tensor_reduce(flat(lsig), inner[:, :].rearrange("p (n d) -> p n d", d=MHD), AXX, ALU.add))
                V.tensor_scalar(flat(lsig), flat(lsig), 1.0 / MHD, EPS, ALU.mult, ALU.add).then_inc(S["gve_ready"], 1)
                dve.wait_ge(S["grstd_ready"], 1)
                link(V.tensor_tensor(y3, y3, wide(gtmp), ALU.mult))
                yt = h_t[:, :].rearrange("p (t d) -> p t d", d=D)
                x3 = x_res[:, :].rearrange("p (t d) -> p t d", d=D)
                link(V.tensor_tensor(yt, yt, rowb[:, R_GNW:R_GNW + D].unsqueeze(1).to_broadcast([P, NT, D]), ALU.mult))
                link(V.tensor_tensor(x3, x3, rowb[:, R_GNB:R_GNB + D].unsqueeze(1).to_broadcast([P, NT, D]), ALU.add))
                V.tensor_tensor(x3, x3, yt, ALU.add).then_inc(S["x_updated"], 1)
            head_norms()

            plain_norm(x_res, inner, NORM1, UPD["m"] + 1)
            V.tensor_reduce(xscale[:, 0:1], inner[:, :], AXX, ALU.min).then_inc(S["fin_link"], 1)
            V.tensor_reduce(xscale[:, 1:2], inner[:, :], AXX, ALU.max).then_inc(S["fin_link"], 1)
            dve.wait_ge(S["fin_link"], 2)
            V.scalar_tensor_tensor(amax[:, :], xscale[:, 0:1], -1.0, xscale[:, 1:2], ALU.mult, ALU.max
                                   ).then_inc(S["amax_ready"], 1)
            dve.wait_ge(S["amrow_done"], 1)
            V.tensor_reduce(am1[:, 1:2], amrow[:, :], AXX, ALU.max).then_inc(S["fin_link"], 1)
            dve.wait_ge(S["fin_link"], 3)
            V.tensor_scalar(am1[:, 0:1], am1[:, 1:2], 1.0 / 127.0, EPS, ALU.mult, ALU.max).then_inc(S["scale_ready"], 1)
            dve.wait_ge(S["scale_ps"], 1)
            V.tensor_copy(xscale[:, 0:1], ps_v[:, 0:1]).then_inc(S["fin_link"], 1)
            dve.wait_ge(S["fin_link"], 4)
            V.reciprocal(xscale[:, 1:2], xscale[:, 0:1]).then_inc(S["fin_link"], 1)
            dve.wait_ge(S["fin_link"], 5)

            def quantise(t, par):
                V.tensor_scalar(qa[:, par, :], tile(inner, t), xscale[:, 1:2], -128.0, ALU.mult, ALU.max
                                ).then_inc(S["fin_link"], 1)
                dve.wait_ge(S["fin_link"], 5 + 2 * t + 1)
                V.tensor_scalar(qb[:, par, :], qa[:, par, :], 127.0, MAGIC, ALU.min, ALU.add).then_inc(S["fin_link"], 1)
                dve.wait_ge(S["fin_link"], 5 + 2 * t + 2)
                seen(dve, S["q8t_ps"], t - 1)
                V.tensor_scalar(q8[:, par, :], qb[:, par, :], MAGIC, None, ALU.subtract).then_inc(S["q8_ready"], 1)

            def dequantise(t, par):
                dve.wait_ge(S["acc8_ready"], t + 1)
                seen(dve, S["o2_ready"], t - 1)
                V.scalar_tensor_tensor(o1[:, par, :], ps_o[:, 0:D], xscale[:, 0:1], rowb[:, R_WS:R_WS + D], ALU.mult,
                                       ALU.mult).then_inc(S["o1_ready"], 1)

            def finish(t, par):
                dve.wait_ge(S["o2_ready"], t + 1)
                seen(dve, out_stored[par], arrived(t, par, 16) - 16)
                V.scalar_tensor_tensor(o3[:, par, :], o2[:, par, :], tg[:, 3:4], tile(x_res, t), ALU.mult, ALU.add
                                       ).then_inc(S["o3_ready"], 1)
            pipeline(dve, [(0, quantise), (2, dequantise), (3, finish)])


_INS = ['x', 'ctx_1024', 'g_xattn', 'g_ffn', 'L0_xattn_Wq', 'L0_xattn_Wk', 'L0_xattn_Wv', 'L0_xattn_Wo',
        'L0_ffn_ln1_w', 'L0_ffn_ln1_b', 'L0_ffn_ln2_w', 'L0_ffn_ln2_b', 'L0_ffn_wq', 'L0_ffn_wk', 'L0_ffn_wv',
        'L0_ffn_wo', 'L0_ffn_bq', 'L0_ffn_bk', 'L0_ffn_bv', 'L0_ffn_bo', 'L0_ffn_gate_w', 'L0_ffn_gate_b',
        'L0_ffn_e_w1', 'L0_ffn_e_b1', 'L0_ffn_e_w2', 'L0_ffn_e_b2', 'L1_xattn_Wi_w', 'L1_xattn_Wi_b',
        'L1_xattn_Wf_w', 'L1_xattn_Wf_b', 'L1_xattn_gn_w', 'L1_xattn_gn_b', 'L1_ffn_weight_int8',
        'L1_ffn_weight_scale', 'L1_ffn_bias']


def kernel(**inputs):
    import numpy as _np
    import concourse.bacc as _bacc
    from concourse import mybir as _mybir
    from concourse.bass_utils import run_bass_kernel_spmd as _run

    nc = _bacc.Bacc("TRN2", target_bir_lowering=False, num_devices=1)
    arrays, args = {}, {}
    for name in _INS:
        a = _np.ascontiguousarray(inputs[name])
        if a.dtype == _np.int8:
            a = a.view(_np.int32)
        arrays[f"in_{name}_dram"] = a
        args[name] = nc.dram_tensor(f"in_{name}_dram", a.shape, _mybir.dt.from_np(a.dtype), kind="ExternalInput").ap()
    out = nc.dram_tensor("out_0_dram", (NSEQ, SEQ, D), _mybir.dt.float32, kind="ExternalOutput").ap()
    build(nc, args, out)
    r = _run(nc, [arrays], core_ids=[0])
    return r.results[0]["out_0_dram"]
```

```python
from contextlib import ExitStack

import concourse.bass as bass
from concourse import mybir

P = 128
NSEQ, SEQ, D = 64, 64, 128
TOK = NSEQ * SEQ
NT = TOK // P
SPT = P // SEQ
HEADS, HD = 16, 8
MH, MHD = 8, 16
NE, DFF = 8, 512
CH = DFF // P
BLK = 512
NB = TOK // BLK
SUB = BLK // P
LAYERS = 2
L_SCORES, L_WEIGH, L_OUT = 4, 5, 7
VBUFS = 4
QT = 2
QW = QT * P
ITEMS = 2 * NSEQ
NPAIR = (ITEMS + NE) // 2
PLACES = 2 * NPAIR
EPS = 1e-5
NEG = -1e30
MAGIC = 12582912.0
ROW0_PAIRS = 3.0

F32 = mybir.dt.float32
BF16 = mybir.dt.bfloat16
I8 = mybir.dt.int8
U32 = mybir.dt.uint32
I32 = mybir.dt.int32
ALU = mybir.AluOpType
ACT = mybir.ActivationFunctionType
AXX = mybir.AxisListType.X


def seen(eng, sem, value):
    if isinstance(value, int) and value <= 0:
        return
    eng.wait_ge(sem, value)


def capped(value, most):
    return min(value, most) if isinstance(value, int) else value


def arrived(t, par, each):
    return (t - par) * (each // 2) + each


def pipeline(eng, steps, n=NT, unroll=4):
    last = max(step[0] for step in steps)
    head = (last + unroll) // unroll * unroll

    def call(step, t, k):
        step[1](t, k % 2, *(k % buffers for buffers in step[2:]))
    for i in range(head):
        for step in steps:
            if i >= step[0]:
                call(step, i - step[0], i - step[0])
    with eng.Fori(head // unroll, n // unroll, 1) as turn:
        i0 = turn * unroll
        for u in range(unroll):
            for step in steps:
                call(step, i0 + (u - step[0]), u - step[0])
    for i in range(n, n + last):
        for step in steps:
            if i - step[0] < n:
                call(step, i - step[0], i - step[0])


def build(nc, A, out):
    with ExitStack() as ctx:
        def sb(name, shape, dt=F32):
            return ctx.enter_context(nc.sbuf_tensor(name, shape, dt))

        def psum(name, cols):
            return ctx.enter_context(nc.psum_tensor(name, [P, cols], F32))

        def sem(name):
            return ctx.enter_context(nc.semaphore(name))

        def tile(buf, t):
            return buf[:, bass.ds(t * P, P)]

        x_res = sb("x_res", [P, NT * D])
        inner = sb("inner", [P, NT * D])
        h_t = sb("h_t", [P, TOK])
        w12 = sb("w12", [P, 2 * NE * DFF])
        w1 = w12[:, 0:NE * DFF].rearrange("p (e n) -> p e n", e=NE)
        w2 = w12[:, NE * DFF:2 * NE * DFF].rearrange("p (e c d) -> p e c d", e=NE, c=CH)
        o_all = w12[:, 0:NT * MH * (MHD + 1)].rearrange("p (t h d) -> p t h d", t=NT, h=MH)
        wraw = sb("wraw", [P, 4, D])
        wx = sb("wx", [P, 4, D])
        wself = sb("wself", [P, LAYERS, 4, D])
        gatew = sb("gatew", [P, LAYERS, NE])
        vecs = sb("vecs", [78, D])
        vec_t = sb("vec_t", [P, 78])
        wg_raw = sb("wg_raw", [2 * MH, 3, D])
        wg_t = sb("wg_t", [P, 3, 2 * MH])
        w8 = sb("w8", [P, D // 4], I32)
        w8f = sb("w8f", [P, D])
        w8t = sb("w8t", [P, D], BF16)
        rows = sb("rows", [1, 1024])
        rowb = sb("rowb", [P, 5 * D + 16])
        tg = sb("tg", [P, 4])
        coef = sb("coef", [P, 4])
        b2src = sb("b2src", [3, NE, D])
        b2a = sb("b2a", [3, NE, D])
        b2hi = sb("b2hi", [3, NE, D], BF16)
        b2mid = sb("b2mid", [3, NE, D], BF16)
        b2lo = sb("b2lo", [3, NE, D], BF16)
        b2rows = sb("b2rows", [3, NE, SUB, D], BF16)
        ident = sb("ident", [P, P])
        identb = sb("identb", [P, P], BF16)
        ones_row = sb("ones_row", [1, P])
        ones3 = sb("ones3", [3, P], BF16)
        kmask = sb("kmask", [P, 8, SEQ])
        kmask4 = sb("kmask4", [P, 4, SEQ])
        vmask = sb("vmask", [P, SPT * HEADS, HD])
        vmask16 = sb("vmask16", [P, SPT * MH, MHD])
        causal = sb("causal", [P, 8, SEQ], BF16)
        block_ones = sb("block_ones", [P, P])
        block_tri = sb("block_tri", [P, P])
        delta = sb("delta", [P, MH, SEQ])
        row3 = sb("row3", [3, 3])
        iota8 = sb("iota8", [P, NT, NE])
        before = sb("before", [NSEQ, NSEQ])
        ones_seq = sb("ones_seq", [NSEQ, P])
        place_no = sb("place_no", [NSEQ, PLACES])
        pair_no = sb("pair_no", [1, NPAIR, NE])
        seq_col = sb("seq_col", [NSEQ, 1])
        b2w = sb("b2w", [NE, D])
        stats = sb("stats", [P, NT, 6])
        mean = sb("mean", [P, NT])
        half_gap = sb("half_gap", [P, NT])
        var = sb("var", [P, NT])
        vare = sb("vare", [P, NT])
        std = sb("std", [P, NT])
        rstd = sb("rstd", [P, NT])
        xn = sb("xn", [P, 2, D])
        xts = sb("xts", [P, 2, P])
        cts = sb("cts", [P, 2, P])
        ctx_in = sb("ctx_in", [P, 2, D])
        ctx_dup = sb("ctx_dup", [P, 2, SPT, D])
        kvt = sb("kvt", [P, 2, SPT, 2, SEQ])
        qbd = sb("qbd", [P, 2, 2, P])
        kts = sb("kts", [P, 2, 2, SEQ])
        vecs2 = sb("vecs2", [8, P])
        vec2_t = sb("vec2_t", [P, 8])
        kbd = sb("kbd", [P, 2, 8, P])
        vbd = sb("vbd", [P, VBUFS, SPT, HEADS, HD + 1])
        vbd16 = sb("vbd16", [P, 2, SPT, MH, MHD + 1])
        rowmax = sb("rowmax", [P, 2, HEADS])
        work = sb("work", [P, 2 * CH * BLK])
        shifted = work[:, 0:2048].rearrange("p (b n) -> p b n", b=2)
        probs = work[:, 2048:4096].rearrange("p (b n) -> p b n", b=2)
        gel = work[:, :].rearrange("p (b c n) -> p b c n", b=2, c=CH)
        w1s = work[:, 0:2 * DFF].rearrange("p (b n) -> p b n", b=2)
        w2s = work[:, 2 * DFF:4 * DFF].rearrange("p (b n) -> p b n", b=2)
        gels = work[:, 4 * DFF:6 * DFF].rearrange("p (b n) -> p b n", b=2)
        hs = work[:, 6 * DFF:6 * DFF + 2 * P].rearrange("p (b n) -> p b n", b=2)
        probs_t = sb("probs_t", [P, 2, 1024])
        recip = sb("recip", [P, 2, HEADS])
        y = sb("y", [P, 2, D])
        yts = sb("yts", [P, 2, P])
        logits = sb("logits", [P, NT, NE])
        cand = sb("cand", [P, NT, NE])
        first = sb("first", [P, NT])
        best1 = sb("best1", [P, NT])
        best2 = sb("best2", [P, NT])
        e21 = sb("e21", [P, NT])
        tw1 = sb("tw1", [P, NT])
        tw2 = sb("tw2", [P, NT])
        oneh = sb("oneh", [P, NT, NE])
        cw = sb("cw", [P, NT, NE])
        hmean = sb("hmean", [P, NSEQ])
        chosen = sb("chosen", [NSEQ, 2, NE])
        counts = sb("counts", [NSEQ, NE])
        tiles_of = sb("tiles_of", [P, NE])
        upto_a = sb("upto_a", [P, 2 * NE])
        upto_b = sb("upto_b", [P, 2 * NE])
        place_base = sb("place_base", [NSEQ, NE])
        chosen_place = sb("chosen_place", [NSEQ, 2, NE])
        place = sb("place", [NSEQ, 2])
        at_place = sb("at_place", [NSEQ, 2, 2, PLACES])
        past = sb("past", [1, NPAIR, NE])
        expert_f = sb("expert_f", [1, NPAIR])
        expert_of = sb("expert_of", [1, NPAIR], I32)
        col_of = sb("col_of", [1, PLACES], I32)
        place_w = sb("place_w", [P, PLACES])
        cw_t = sb("cw_t", [NE, NSEQ])
        b1s = sb("b1s", [P, 2, CH])
        gates = sb("gates", [P, NT, 2 * MH])
        gtmp = oneh
        lsig = logits
        csum = sb("csum", [P, NT, MH])
        avec = cw
        maxes = cand
        adiag = shifted[:, :, 512:1024].rearrange("p b (h k) -> p b h k", k=SEQ)
        ctil = probs[:, :, 512:1024]
        amax = sb("amax", [P, 1])
        amrow = sb("amrow", [1, P])
        am1 = sb("am1", [1, 2])
        xscale = sb("xscale", [P, 2])
        magic = sb("magic", [P, 1])
        q8 = sb("q8", [P, 2, QW], BF16)
        q8t = sb("q8t", [P, 2, QW], BF16)
        qa, qb, o1, o3 = (work[:, k * 2 * QW:(k + 1) * 2 * QW].rearrange("p (b n) -> p b n", b=2) for k in range(4))

        ps_s = psum("ps_s", 1024)
        ps_t = psum("ps_t", 1024)
        ps_o = psum("ps_o", 512)
        ps_x = psum("ps_x", 512)
        ps_a = psum("ps_a", 512)
        ps_v = psum("ps_v", 512)
        ps_s3 = ps_s[:, :].rearrange("p (r n) -> p r n", r=2)

        names = """x_loaded weights_loaded ffn_w_loaded pool_const setup_t setup_copied dve_setup
        bn_done stat_link vare_ready std_ready rstd_ready xn_ready xt_ready xts_ready ctx_used
        proj_ready qk_ready kbd_ready vbd_ready scores_ready max_ready shifted_ready probs_ready
        pt_ready pts_ready o_ready recip_ready y_ready yt_ready yts_ready outp_ready x_updated
        ht_stored logits_ps logits_sb route_link route_exp route_done hmean_ready seqlog_ready
        place_ps place_link tables_ready w1s_ready w2s_ready hs_ready pair_hid pair_gelu pair_out pair_added
        rows_ps rows_added
        hid_ready gelu_ready yexp_ready acc_ready gates_ps gates_sb xct_stored gate_link gexp_ready gln_ready
        csum_ps avec_ready adiag_ready a_ready d_ready ctil_ready qcopy_ready o_stored negmd_ready emd_ready
        vb16_ready rs_link gn_link square_ready gve_ready gstd_ready fin_link qb_ready amax_ready amrow_ps
        amrow_done scale_ps scale_ready q8_ready q8t_ps q8t_ready acc8_ready o1_ready o3_ready xb_ready
        ctx0_loaded ctx1_loaded dup0_loaded dup1_loaded out0_stored out1_stored """
        S = {n: sem(n) for n in names.split()}
        ctx_loaded = [S["ctx0_loaded"], S["ctx1_loaded"]]
        dup_loaded = [S["dup0_loaded"], S["dup1_loaded"]]
        out_stored = [S["out0_stored"], S["out1_stored"]]

        CROSS, NORM0, SELF0, PRE0, SELF1, PRE1, MLSTM, NORM1 = (k * NT for k in range(8))
        ATT = {"x": 0, 0: NT, 1: 2 * NT, "m": 3 * NT}
        TB = {"x": 0, 0: NT, "p0": 2 * NT, 1: 3 * NT, "p1": 4 * NT, "m": 5 * NT}
        UPD = {"x": 0, 0: NT, 1: 2 * NT, "m": 3 * NT}

        x_v = A["x"].rearrange("(t s) i d -> (s i) t d", s=SPT)
        ctx_v = A["ctx_1024"].rearrange("(t s) i d -> t (s i) d", s=SPT)
        ctxd_v = A["ctx_1024"].rearrange("(t s) i d -> t i s d", s=SPT)
        out_v = out.rearrange("(u v s) i d -> u (s i) v d", v=QT, s=SPT)

        CONSTS = []
        block = ctx.enter_context(nc.Block())

        ROUTE_EXP = 12
        ROUTE_COUNTS = ROUTE_EXP + 3
        ROUTE_LINKS = (ROUTE_EXP + 5, ROUTE_COUNTS + 6)
        B2_LINKS = 7 + SUB
        STAT_LINKS = 6
        PLACE_TABLES = 14
        GN_CENTRED = 7

        def ROUTE_AT(l, k):
            return sum(ROUTE_LINKS[:l]) + k

        q8ps = [bank[:, :].bitcast(BF16)[:, 0:QW] for bank in (ps_x, ps_a)]

        def vec(kind, l):
            c = 2 * kind + l
            return vec_t[:, c:c + 1]

        def b1col(l, e, c):
            k = 14 + (l * NE + e) * CH + c
            return vec_t[:, k:k + 1]

        def qkbias(kind, l, r, rows_):
            c = kind * 4 + l * 2 + r
            return vec2_t[rows_, c:c + 1]

        R_GNW, R_GNB, R_WS, R_B1, R_GB1, R_G = 0, D, 2 * D, 3 * D, 4 * D, 4 * D + 8
        R_BO, R_GI, R_GB0 = 4 * D + 16, 6 * D + 16, 6 * D + 32
        row_loads = [("L1_xattn_gn_w", R_GNW), ("L1_xattn_gn_b", R_GNB), ("L1_ffn_weight_scale", R_WS),
                     ("L1_ffn_bias", R_B1), ("g_xattn", R_G), ("g_ffn", R_G + 2), ("L1_xattn_Wi_b", R_GI),
                     ("L1_xattn_Wf_b", R_GI + 8)]
        small_loads = []
        for name, at in row_loads:
            ap = A[name]
            n = 1
            for s_ in ap.shape:
                n *= s_
            flat = ap.rearrange("a b -> (b a)") if len(ap.shape) == 2 else ap
            small_loads.append((rows[0:1, at:at + n], flat.rearrange("(a n) -> a n", a=1)))
        small_loads.append((rows[0:1, R_GB1:R_GB1 + 8], A["L0_ffn_gate_b"][1:2, :]))
        small_loads.append((rows[0:1, R_GB0:R_GB0 + 8], A["L0_ffn_gate_b"][0:1, :]))
        for l in range(LAYERS):
            small_loads.append((rows[0:1, R_BO + l * D:R_BO + (l + 1) * D], A["L0_ffn_bo"][l:l + 1, :]))
        for k, name in enumerate(("ln1_w", "ln1_b", "ln2_w", "ln2_b", "bq", "bk", "bv")):
            small_loads.append((vecs[2 * k:2 * k + 2, :], A["L0_ffn_" + name]))
        for k, name in enumerate(("bq", "bk")):
            for half in range(2):
                small_loads.append((vecs2[4 * k:4 * k + 4, half * 64:(half + 1) * 64],
                                    A["L0_ffn_" + name].rearrange("l (r c) -> (l r) c", r=2)))
        small_loads.append((vecs[14:78, :], A["L0_ffn_e_b1"].rearrange("l e (c p) -> (l e c) p", p=P)))
        for k, name in enumerate(("Wq", "Wk", "Wv", "Wo")):
            small_loads.append((wraw[:, k, :], A["L0_xattn_" + name]))
            for l in range(LAYERS):
                small_loads.append((wself[:, l, k, :], A["L0_ffn_" + name.lower()][l, :, :]))
        for l in range(LAYERS):
            small_loads.append((gatew[:, l, :], A["L0_ffn_gate_w"][l, :, :]))
        small_loads.append((wg_raw[0:MH, :, :], A["L1_xattn_Wi_w"].rearrange("h (k d) -> h k d", k=3)))
        small_loads.append((wg_raw[MH:2 * MH, :, :], A["L1_xattn_Wf_w"].rearrange("h (k d) -> h k d", k=3)))
        small_loads.append((w8[:, :], A["L1_ffn_weight_int8"]))
        small_loads.append((b2w[:, :], A["L0_ffn_e_b2"][1, :, :]))
        for row in range(3):
            small_loads.append((b2src[row:row + 1, :, :], A["L0_ffn_e_b2"][0:1, :, :]))
        N_WLOADS = len(small_loads)

        @block.sync
        def _(sp):
            sp.dma_start(x_res[:, :].rearrange("p (t d) -> p t d", d=D), x_v).then_inc(S["x_loaded"], 16)
            for dst, src in small_loads[:N_WLOADS // 2]:
                sp.dma_start(dst, src).then_inc(S["weights_loaded"], 16)

            def ctx_load(base):
                def fn(t, par):
                    seen(sp, S["ctx_used"], base + t - 1)
                    sp.dma_start(ctx_in[:, par, :], ctx_v[bass.ds(t, 1), :, :].rearrange("a p d -> p (a d)")
                                 ).then_inc(ctx_loaded[par], 16)
                return fn

            def dup_load(t, par):
                seen(sp, S["vb16_ready"], t - 1)
                for g in range(2):
                    sp.dma_start(ctx_dup[g * SEQ:(g + 1) * SEQ, par, :, :],
                                 ctxd_v[bass.ds(t, 1), :, :, :].rearrange("a i s d -> i (a s) d")
                                 ).then_inc(dup_loaded[par], 16)

            def expert_load(l):
                if l:
                    sp.wait_ge(S["yexp_ready"], NB * NE)
                sp.dma_start(w1[:, :, :], A["L0_ffn_e_w1"][l, :, :, :].rearrange("e d f -> d e f")
                             ).then_inc(S["ffn_w_loaded"], 16)
                sp.dma_start(w2[:, :, :, :], A["L0_ffn_e_w2"][l, :, :, :].rearrange("e (c p) d -> p e c d", p=P)
                             ).then_inc(S["ffn_w_loaded"], 16)

            pipeline(sp, [(0, ctx_load(0))])
            expert_load(0)
            expert_load(1)
            pipeline(sp, [(0, ctx_load(NT))])
            pipeline(sp, [(0, dup_load)])

            def store(t, par):
                sp.wait_ge(S["o3_ready"], t + 1)
                sp.dma_start(out_v[bass.ds(t, 1), :, :, :].rearrange("a p v d -> p (a v) d"),
                             o3[:, par, :].rearrange("p (v d) -> p v d", v=QT)
                             ).then_inc(out_stored[par], 16)
            pipeline(sp, [(0, store)], NT // QT)
            for par in range(2):
                sp.wait_ge(out_stored[par], 16 * (NT // QT // 2))

        @block.gpsimd
        def _(pool):
            n = [0]

            def fresh(ins):
                n[0] += 1
                ins.then_inc(S["pool_const"], 1)
                pool.wait_ge(S["pool_const"], n[0])

            def select(ap, pattern, base, mult, cmp=ALU.is_ge, fill=0.0):
                fresh(pool.affine_select(out=ap, in_=ap, compare_op=cmp, fill=fill, base=base,
                                         pattern=pattern, channel_multiplier=mult))

            fresh(pool.memset(ident[:, :], 0.0))
            select(ident[:, :], [[-1, P]], 0, 1, ALU.not_equal, 1.0)
            fresh(pool.memset(identb[:, :], 0.0))
            select(identb[:, :], [[-1, P]], 0, 1, ALU.not_equal, 1.0)
            fresh(pool.memset(ones_row[:, :], 1.0))
            fresh(pool.memset(magic[:, :], -MAGIC))
            fresh(pool.memset(ones3[:, :], 1.0))
            for buf, hh, hd, width in ((kmask, 8, HD, SEQ), (kmask4, 4, MHD, SEQ)):
                for half in range(2):
                    part = buf[half * 64:(half + 1) * 64, :, :]
                    fresh(pool.memset(part, 1.0))
                    select(part, [[-hd, hh], [0, width]], 0, 1)
                    select(part, [[hd, hh], [0, width]], hd - 1, -1)
            for buf, hd in ((vmask, HD), (vmask16, MHD)):
                v = buf[:, :, :].rearrange("p (n g) d -> p n g d", g=2)
                fresh(pool.memset(buf[:, :, :], 0.0))
                for half in range(2):
                    fresh(pool.memset(v[half * 64:(half + 1) * 64, :, half, :], 1.0))
            fresh(pool.memset(vbd[:, :, :, :, :], 1.0))
            fresh(pool.memset(qbd[:, :, :, :], 0.0))
            fresh(pool.memset(vbd16[:, :, :, :, :], 1.0))
            for buf, nh, hd in ((vbd, HEADS, HD), (vbd16, MH, MHD)):
                for half in range(2):
                    for par in range(buf.shape[1]):
                        v = buf[half * 64:(half + 1) * 64, par, :, :, hd:hd + 1].rearrange(
                            "p s (n g) o -> p s n g o", g=2)[:, :, :, 1 - half, :]
                        fresh(pool.memset(v, 0.0))
            fresh(pool.memset(causal[:, :, :], 0.0))
            for half in range(2):
                part = causal[half * 64:(half + 1) * 64, :, :]
                select(part, [[0, 8], [-1, SEQ]], 0, 1, ALU.is_ge, NEG)
            fresh(pool.memset(block_ones[:, :], 0.0))
            fresh(pool.memset(block_tri[:, :], 0.0))
            fresh(pool.memset(delta[:, :, :], 0.0))
            for half in range(2):
                a, b = half * 64, (half + 1) * 64
                fresh(pool.memset(block_ones[a:b, a:b], 1.0))
                fresh(pool.memset(block_tri[a:b, a:b], 1.0))
                select(block_tri[a:b, a:b], [[1, 64]], 0, -1)
                select(delta[a:b, :, :], [[0, MH], [-1, SEQ]], 0, 1, ALU.not_equal, 1.0)
            fresh(pool.memset(row3[:, :], 0.0))
            select(row3[:, :], [[-1, 3]], 0, 1, ALU.not_equal, 1.0)
            fresh(pool.iota(iota8[:, :, :], pattern=[[0, NT], [1, NE]], base=0, channel_multiplier=0,
                            allow_small_or_imprecise_dtypes=True))
            fresh(pool.memset(before[:, :], 1.0))
            select(before[:, :], [[1, NSEQ]], -1, -1)
            fresh(pool.memset(ones_seq[:, :], 1.0))
            fresh(pool.iota(place_no[:, :], pattern=[[1, PLACES]], base=0, channel_multiplier=0,
                            allow_small_or_imprecise_dtypes=True))
            fresh(pool.iota(pair_no[:, :, :], pattern=[[1, NPAIR], [0, NE]], base=0, channel_multiplier=0,
                            allow_small_or_imprecise_dtypes=True))
            fresh(pool.iota(seq_col[:, :], pattern=[[0, 1]], base=0, channel_multiplier=SEQ,
                            allow_small_or_imprecise_dtypes=True))
            fresh(pool.memset(upto_a[:, :], 0.0))
            fresh(pool.memset(upto_b[:, :], 0.0))
            CONSTS.append(n[0])

            def kbd_step(base):
                def fn(t, par):
                    pool.wait_ge(S["qk_ready"], base + t + 1)
                    seen(pool, S["scores_ready"], base + t - 1)
                    for r in range(2):
                        i = pool.tensor_tensor(kbd[:, par, r * 4:(r + 1) * 4, :].rearrange("p a (b k) -> p (a b) k", k=SEQ),
                                               kts[:, par, r:r + 1, :].to_broadcast([P, 8, SEQ]),
                                               kmask[:, :, :], ALU.mult)
                    i.then_inc(S["kbd_ready"], 1)
                return fn

            def ht_step(base):
                def fn(t, par):
                    pool.wait_ge(S["xts_ready"], TB[base] + t + 1)
                    pool.tensor_copy(tile(h_t, t), xts[:, par, :]).then_inc(S["ht_stored"], 1)
                return fn

            pipeline(pool, [(2, kbd_step(ATT["x"]))])
            for l in range(LAYERS):
                pipeline(pool, [(2, kbd_step(ATT[l]))])
                if l:
                    pool.wait_ge(S["yexp_ready"], NB * NE)
                pipeline(pool, [(3, ht_step(f"p{l}"))])

            def second_weights(t, par):
                seen(pool, S["pair_out"], t - 1)
                e = pool.value_load(expert_of[0:1, bass.ds(t, 1)], min_val=0, max_val=NE - 1)
                pool.tensor_copy(w2s[:, par, :].unsqueeze(1), w2[:, bass.ds(e, 1), :, :].rearrange("p e c d -> p e (c d)")
                                 ).then_inc(S["w2s_ready"], 1)
            pool.wait_ge(S["ffn_w_loaded"], 16 * 4)
            pool.wait_ge(S["tables_ready"], 1)
            pipeline(pool, [(0, second_weights)], NPAIR)

            def store_xct(t, par):
                pool.wait_ge(S["xts_ready"], TB["m"] + t + 1)
                for g in range(SPT):
                    for r in range(2):
                        to, at = slice(64 * g, 64 * g + 64), slice(64 * r, 64 * r + 64)
                        pool.tensor_copy(h_t[to, bass.ds(t * P + r * SEQ, SEQ)], xts[at, par, g * SEQ:(g + 1) * SEQ])
                        i = pool.tensor_copy(inner[to, bass.ds(t * P + r * SEQ, SEQ)],
                                             cts[at, par, g * SEQ:(g + 1) * SEQ])
                i.then_inc(S["xct_stored"], 1)

            def kbd16_step(t, par):
                seen(pool, S["scores_ready"], ATT["m"] + t - 1)
                for r in range(2):
                    i = pool.tensor_tensor(kbd[:, par, 2 * r:2 * r + 2, :].rearrange("p a (b k) -> p (a b) k", k=SEQ),
                                           inner[:, bass.ds(t * P + r * SEQ, SEQ)].unsqueeze(1).to_broadcast([P, 4, SEQ]),
                                           kmask4[:, :, :], ALU.mult)
                i.then_inc(S["kbd_ready"], 1)

            def vbd16_step(t, par):
                pool.wait_ge(dup_loaded[par], arrived(t, par, 32))
                seen(pool, S["o_ready"], ATT["m"] + t - 1)
                pool.tensor_tensor(vbd16[:, par, :, :, 0:MHD].rearrange("p s h d -> p (s h) d"),
                                   ctx_dup[:, par, :, :].rearrange("p s (h d) -> p (s h) d", d=MHD),
                                   vmask16[:, :, :], ALU.mult).then_inc(S["vb16_ready"], 1)

            def adiag_step(t, par):
                seen(pool, S["a_ready"], t - 1)
                pool.tensor_tensor(adiag[:, par, :, :],
                                   avec[:, bass.ds(t, 1), :].rearrange("p a h -> p (a h)").unsqueeze(2).to_broadcast([P, MH, SEQ]),
                                   delta[:, :, :], ALU.mult).then_inc(S["adiag_ready"], 1)

            pipeline(pool, [(2, store_xct)])
            pool.wait_ge(S["xct_stored"], NT)
            pool.wait_ge(S["avec_ready"], 1)
            pipeline(pool, [(6, vbd16_step), (2, kbd16_step), (0, adiag_step)])
            x3 = x_res[:, :].rearrange("p (t d) -> p t d", d=D)
            pool.wait_ge(S["xn_ready"], MLSTM + NT)
            pool.tensor_tensor(x3, x3, rowb[:, R_GNB:R_GNB + D].unsqueeze(1).to_broadcast([P, NT, D]), ALU.add
                               ).then_inc(S["xb_ready"], 1)
            pool.wait_ge(S["xn_ready"], NORM1 + NT)
            pool.tensor_tensor(x3, x3, rowb[:, R_B1:R_B1 + D].unsqueeze(1).to_broadcast([P, NT, D]), ALU.add
                               ).then_inc(S["xb_ready"], 1)
            pool.wait_ge(S["xb_ready"], 2)

            def finish(t, par):
                pool.wait_ge(S["o1_ready"], t + 1)
                seen(pool, out_stored[par], arrived(t, par, 16) - 16)
                pool.tensor_tensor(o3[:, par, :], o1[:, par, :], x_res[:, bass.ds(t * QW, QW)], ALU.add
                                   ).then_inc(S["o3_ready"], 1)
            pipeline(pool, [(0, finish)], NT // QT)

        @block.scalar
        def _(act):
            for dst, src in small_loads[N_WLOADS // 2:]:
                act.dma_start(dst, src).then_inc(S["weights_loaded"], 16)
            k = [0]

            def copied(dst, src):
                k[0] += 1
                act.wait_ge(S["setup_t"], k[0])
                nc.scalar.copy(dst, src).then_inc(S["setup_copied"], 1)
            copied(wx[:, :, :].rearrange("p a d -> p (a d)"), ps_s[:, 0:4 * D])
            copied(vec_t[:, :], ps_t[:, 0:78])
            copied(vec2_t[:, :], ps_t[:, 512:520])
            copied(wg_t[:, :, :].rearrange("p a d -> p (a d)"), ps_o[:, 0:48])
            copied(rowb[:, 0:512], ps_a[:, 0:512])
            copied(rowb[:, 512:524], ps_v[:, 0:12])
            copied(w8t[:, :], ps_x[:, 0:P])
            act.wait_ge(S["setup_copied"], 6)
            nc.scalar.activation(tg[:, :], rowb[:, R_G:R_G + 4], ACT.Tanh).then_inc(S["setup_copied"], 1)

            def evac_t(base, l, vk, both):
                def fn(t, par):
                    act.wait_ge(S["xt_ready"], TB[base] + t + 1)
                    if base in ("x", 0, 1):
                        seen(act, S["proj_ready"], ATT[base] + t - 1)
                    elif base == "m":
                        seen(act, S["gates_ps"], t - 1)
                        seen(act, S["xct_stored"], t - 1)
                    else:
                        seen(act, S["ht_stored"], int(base[1]) * NT + t - 1)
                        if base == "p0":
                            seen(act, S["logits_ps"], t - 1)
                    if base in (0, 1):
                        src = ps_x[:, 0:P].rearrange("p (s k) -> p s k", s=SPT)
                        for g in range(2):
                            i = nc.scalar.activation(kvt[:, par, :, g, :], src, ACT.Identity, bias=vec(vk + 1, l),
                                                     scale=vec(vk, l))
                    elif vk is None:
                        i = nc.scalar.copy(xts[:, par, :], ps_x[:, 0:P])
                    else:
                        i = nc.scalar.activation(xts[:, par, :], ps_x[:, 0:P], ACT.Identity,
                                                 bias=vec(vk + 1, l), scale=vec(vk, l))
                    if base == "x":
                        src = ps_x[:, P:2 * P].rearrange("p (s k) -> p s k", s=SPT)
                        for g in range(2):
                            i = nc.scalar.copy(kvt[:, par, :, g, :], src)
                    elif both:
                        i = nc.scalar.copy(cts[:, par, :], ps_x[:, P:2 * P])
                    i.then_inc(S["xts_ready"], 1)
                return fn

            def evac_qk(base, l):
                def fn(t, par):
                    act.wait_ge(S["proj_ready"], ATT[base] + t + 1)
                    seen(act, S["scores_ready"], ATT[base] + t - 1)
                    seen(act, S["kbd_ready"], ATT[base] + t - 1)
                    for g in range(SPT):
                        rows_ = slice(64 * g, 64 * g + 64)
                        cols_ = slice(SEQ * g, SEQ * g + SEQ)
                        if l is None:
                            nc.scalar.copy(qbd[rows_, par, :, cols_], ps_a[rows_, 0:P].rearrange("p (r k) -> p r k", r=2))
                        else:
                            for r in range(2):
                                nc.scalar.activation(qbd[rows_, par, r, cols_], ps_a[rows_, r * SEQ:(r + 1) * SEQ],
                                                     ACT.Identity, bias=qkbias(0, l, r, rows_))
                    if l is None:
                        i = nc.scalar.copy(kts[:, par, :, :], ps_a[:, P:2 * P].rearrange("p (r k) -> p r k", r=2))
                    else:
                        for r in range(2):
                            i = nc.scalar.activation(kts[:, par, r, :], ps_a[:, P + r * SEQ:P + (r + 1) * SEQ],
                                                     ACT.Identity, bias=qkbias(1, l, r, slice(0, P)))
                    i.then_inc(S["qk_ready"], 1)
                return fn

            def exp_step(base):
                def fn(t, par):
                    act.wait_ge(S["shifted_ready"], ATT[base] + t + 1)
                    seen(act, S["pt_ready"], ATT[base] + t - 1)
                    nc.scalar.activation(probs[:, par, :], shifted[:, par, :], ACT.Exp, scale=HD ** -0.5
                                         ).then_inc(S["probs_ready"], 1)
                return fn

            def evac_pt(base):
                def fn(t, par):
                    act.wait_ge(S["pt_ready"], ATT[base] + t + 1)
                    seen(act, S["o_ready"], ATT[base] + t - 1)
                    nc.scalar.copy(probs_t[:, par, :], ps_t[:, :]).then_inc(S["pts_ready"], 1)
                return fn

            def evac_yt(base, l):
                def fn(t, par):
                    act.wait_ge(S["yt_ready"], ATT[base] + t + 1)
                    seen(act, S["outp_ready"], ATT[base] + t - 1)
                    if l is None:
                        i = nc.scalar.copy(yts[:, par, :], ps_a[:, 0:P])
                    else:
                        i = nc.scalar.activation(yts[:, par, :], ps_a[:, 0:P], ACT.Identity, bias=vec(6, l))
                    i.then_inc(S["yts_ready"], 1)
                return fn

            def attention(base, l):
                pipeline(act, [(L_OUT, evac_yt(base, l)), (L_WEIGH, evac_pt(base)), (2, evac_qk(base, l)),
                               (1, evac_t(base, l, None if l is None else 0, l is None)),
                               (L_SCORES, exp_step(base))])

            def gelu_block(l):
                def fn(b, par):
                    for e in range(NE):
                        for c in range(CH):
                            k = c + 1 + e * CH
                            act.wait_ge(S["hid_ready"], l * NB * NE * CH + b * (NE * CH) + k)
                            if c == 0:
                                seen(act, S["yexp_ready"], l * NB * NE + b * NE + (e - 1))
                            nc.scalar.activation(gel[:, e % 2, c, :], (ps_s, ps_t)[c // 2][:, (c % 2) * BLK:(c % 2 + 1) * BLK],
                                                 ACT.Gelu, bias=b1col(l, e, c)).then_inc(S["gelu_ready"], 1)
                return fn

            def row_std(k):
                act.wait_ge(S["vare_ready"], k + 1)
                nc.scalar.activation(std[:, :], vare[:, :], ACT.Sqrt).then_inc(S["std_ready"], 1)

            row_std(0)
            attention("x", None)
            row_std(1)
            for l in range(LAYERS):
                row_std(2 + 2 * l)
                attention(l, l)
                row_std(3 + 2 * l)
                pipeline(act, [(2, evac_t(f"p{l}", l, 2, False))])
                act.wait_ge(S["route_link"], ROUTE_AT(l, ROUTE_EXP))
                nr = (P, NSEQ)[l]
                nt = (NT, 1)[l]
                nc.scalar.activation(e21[0:nr, 0:nt], e21[0:nr, 0:nt], ACT.Exp).then_inc(S["route_exp"], 1)
                if l == 0:
                    fn = gelu_block(l)
                    fn(0, 0)
                    with act.Fori(1, NB, 1) as b:
                        fn(b, 0)

            def pair_rows(t, par):
                seen(act, S["pair_hid"], t - 1)
                for g in range(2):
                    q = act.value_load(col_of[0:1, bass.ds(2 * t + g, 1)], min_val=0, max_val=TOK - SEQ)
                    i = nc.scalar.copy(hs[:, par, g * SEQ:(g + 1) * SEQ], h_t[:, bass.ds(q, SEQ)])
                i.then_inc(S["hs_ready"], 1)

            def pair_gelu(t, par):
                act.wait_ge(S["pair_hid"], t + 1)
                seen(act, S["pair_out"], t - 1)
                for c in range(CH):
                    i = nc.scalar.activation(gels[:, par, c * P:(c + 1) * P], ps_s3[:, par, c * P:(c + 1) * P],
                                             ACT.Gelu, bias=b1s[:, par, c:c + 1])
                i.then_inc(S["pair_gelu"], 1)
            act.wait_ge(S["tables_ready"], 1)
            act.wait_ge(S["ht_stored"], 2 * NT)
            pipeline(act, [(2, pair_gelu), (0, pair_rows)], NPAIR)

            row_std(6)
            pipeline(act, [(1, evac_t("m", None, None, True))])
            act.wait_ge(S["gate_link"], 1)
            nc.scalar.activation(gtmp[:, :, :], gtmp[:, :, :], ACT.Exp).then_inc(S["gexp_ready"], 1)
            act.wait_ge(S["gexp_ready"], 1)
            nc.scalar.activation(gtmp[:, :, :], gtmp[:, :, :], ACT.Ln, bias=1.0).then_inc(S["gln_ready"], 1)

            def query_copy(t, par):
                if isinstance(t, int) and t == 0:
                    act.wait_ge(S["xct_stored"], NT)
                seen(act, S["scores_ready"], ATT["m"] + t - 1)
                for g in range(SPT):
                    rows_ = slice(64 * g, 64 * g + 64)
                    i = nc.scalar.copy(qbd[rows_, par, :, SEQ * g:SEQ * g + SEQ],
                                       h_t[rows_, bass.ds(t * P, P)].rearrange("p (r k) -> p r k", r=2))
                i.then_inc(S["qcopy_ready"], 1)

            def decay_exp(t, par):
                act.wait_ge(S["shifted_ready"], ATT["m"] + t + 1)
                seen(act, S["ctil_ready"], t - 1)
                nc.scalar.activation(probs[:, par, 0:512], shifted[:, par, 0:512], ACT.Exp).then_inc(S["d_ready"], 1)

            def evac_ctil(t, par):
                act.wait_ge(S["pt_ready"], ATT["m"] + t + 1)
                seen(act, S["o_ready"], ATT["m"] + t - 1)
                nc.scalar.copy(probs_t[:, par, 0:512], (ps_a, ps_x)[par][:, :]).then_inc(S["pts_ready"], 1)

            def store_o(t, par):
                act.wait_ge(S["o_ready"], ATT["m"] + t + 1)
                bank = (ps_o, ps_v)[par]
                for s_ in range(SPT):
                    r_ = slice(64 * s_, 64 * s_ + 64)
                    at = s_ * MH * (MHD + 1)
                    i = nc.scalar.copy(w12[r_, bass.ds(t * (MH * (MHD + 1)), MH * (MHD + 1))],
                                       bank[r_, at:at + MH * (MHD + 1)])
                i.then_inc(S["o_stored"], 1)
            pipeline(act, [(8, store_o), (6, evac_ctil), (3, decay_exp), (2, query_copy)])
            act.wait_ge(S["negmd_ready"], 1)
            nc.scalar.activation(csum[:, :, :], csum[:, :, :], ACT.Exp, scale=-1.0).then_inc(S["emd_ready"], 1)
            act.wait_ge(S["gn_link"], GN_CENTRED)
            nc.scalar.activation(inner[:, :], h_t[:, :], ACT.Square).then_inc(S["square_ready"], 1)
            act.wait_ge(S["gve_ready"], 1)
            nc.scalar.activation(gtmp[:, :, :], lsig[:, :, :], ACT.Sqrt).then_inc(S["gstd_ready"], 1)
            row_std(7)

            act.wait_ge(S["amrow_ps"], 1)
            nc.scalar.copy(amrow[:, :], ps_a[0:1, 0:P]).then_inc(S["amrow_done"], 1)

            def unshift(t, par):
                act.wait_ge(S["qb_ready"], t + 1)
                seen(act, S["q8t_ps"], t - 1)
                nc.scalar.activation(q8[:, par, :], qb[:, par, :], ACT.Identity, bias=magic[:, :]
                                     ).then_inc(S["q8_ready"], 1)

            def evac_q8(t, par):
                act.wait_ge(S["q8t_ps"], t + 1)
                seen(act, S["acc8_ready"], t - 1)
                nc.scalar.copy(q8t[:, par, :], q8ps[par]).then_inc(S["q8t_ready"], 1)
            pipeline(act, [(3, evac_q8), (1, unshift)], NT // QT)

        @block.tensor
        def _(pe):
            pe.wait_ge(S["pool_const"], CONSTS[0])
            pe.wait_ge(S["weights_loaded"], 16 * N_WLOADS)

            def mm(o, a, b, start=True, stop=True):
                return nc.tensor.matmul(o, a, b, start=start, stop=stop, skip_group_check=True)

            for k in range(4):
                i = nc.tensor.transpose(ps_s[:, k * D:(k + 1) * D], wraw[:, k, :], ident[:, :])
            i.then_inc(S["setup_t"], 1)
            nc.tensor.transpose(ps_t[:, 0:78], vecs[:, :], ident[0:78, 0:78]).then_inc(S["setup_t"], 1)
            nc.tensor.transpose(ps_t[:, 512:520], vecs2[:, :], ident[0:8, 0:8]).then_inc(S["setup_t"], 1)
            for k in range(3):
                i = nc.tensor.transpose(ps_o[:, k * 16:(k + 1) * 16], wg_raw[:, k, :], ident[0:16, 0:16])
            i.then_inc(S["setup_t"], 1)
            mm(ps_a[:, 0:512], ones_row[:, :], rows[:, 0:512]).then_inc(S["setup_t"], 1)
            mm(ps_v[:, 0:12], ones_row[:, :], rows[:, 512:524]).then_inc(S["setup_t"], 1)
            pe.wait_ge(S["dve_setup"], 1)
            nc.tensor.transpose(ps_x[:, 0:P], w8f[:, :], ident[:, :]).then_inc(S["setup_t"], 1)
            pe.wait_ge(S["setup_copied"], 8)

            def ctx_transpose(base):
                def fn(t, par):
                    seen(pe, S["xts_ready"], TB[base] + t)
                    pe.wait_ge(ctx_loaded[par], (8 * NT if base == "m" else 0) + arrived(t, par, 16))
                    nc.tensor.transpose(ps_x[:, P:2 * P], ctx_in[:, par, :], ident[:, :]).then_inc(S["ctx_used"], 1)
                return fn

            def transposes(base, nbase):
                def fn(t, par):
                    pe.wait_ge(S["xn_ready"], nbase + t + 1)
                    seen(pe, S["xts_ready"], TB[base] + t)
                    nc.tensor.transpose(ps_x[:, 0:P], xn[:, par, :], ident[:, :]).then_inc(S["xt_ready"], 1)
                return fn

            def project(base, l):
                w = (lambda k: wx[:, k, :]) if l is None else (lambda k: wself[:, l, k, :])

                def fn(t, par):
                    pe.wait_ge(S["xts_ready"], TB[base] + t + 1)
                    seen(pe, S["yts_ready"], ATT[base] + t + 3 - L_OUT)
                    seen(pe, S["qk_ready"], ATT[base] + t)
                    for k in range(2):
                        for g in range(SPT):
                            src = xts[:, par, g * SEQ:(g + 1) * SEQ] if k == 0 and l is None else kvt[:, par, g, 0, :]
                            for r in range(2):
                                at = k * P + r * SEQ
                                mm(ps_a[g * 64:(g + 1) * 64, at:at + SEQ], w(k)[:, r * 64:(r + 1) * 64], src)
                    seen(pe, S["x_updated"], UPD[base] + t + 3 - L_OUT)
                    seen(pe, S["vbd_ready"], ATT[base] + t)
                    for g in range(SPT):
                        i = mm(ps_v[:, g * D:(g + 1) * D], kvt[:, par, g, :, :].rearrange("p a k -> p (a k)"), w(2))
                    i.then_inc(S["proj_ready"], 1)
                return fn

            def scores(base, masked):
                def fn(t, par):
                    pe.wait_ge(S["qk_ready"], ATT[base] + t + 1)
                    pe.wait_ge(S["kbd_ready"], ATT[base] + t + 1)
                    seen(pe, S["shifted_ready"], ATT[base] + t)
                    if masked:
                        for r in range(2):
                            mm(ps_s3[:, r, :], identb[:, :], causal[:, :, :].rearrange("p a b -> p (a b)"),
                               True, False)
                    for r in range(2):
                        i = mm(ps_s3[:, r, :], qbd[:, par, r, :],
                               kbd[:, par, r * 4:(r + 1) * 4, :].rearrange("p a k -> p (a k)"), not masked, True)
                    i.then_inc(S["scores_ready"], 1)
                return fn

            def transpose_probs(base):
                def fn(t, par):
                    pe.wait_ge(S["probs_ready"], ATT[base] + t + 1)
                    seen(pe, S["pts_ready"], ATT[base] + t)
                    for j in range(HEADS // 2):
                        i = nc.tensor.transpose(ps_t[:, j * P:(j + 1) * P], probs[:, par, j * P:(j + 1) * P], ident[:, :])
                    i.then_inc(S["pt_ready"], 1)
                return fn

            def weigh(base):
                def fn(t, par, slot):
                    pe.wait_ge(S["pts_ready"], ATT[base] + t + 1)
                    pe.wait_ge(S["vbd_ready"], ATT[base] + t + 1)
                    seen(pe, S["y_ready"], ATT[base] + t)
                    o = ps_o[:, 0:SPT * HEADS * (HD + 1)].rearrange("p (s n) -> p s n", s=SPT)
                    for j in range(HEADS // 2):
                        a = 2 * j * (HD + 1)
                        i = mm(o[:, :, a:a + 2 * (HD + 1)], probs_t[:, par, j * P:(j + 1) * P],
                               vbd[:, slot, :, 2 * j:2 * j + 2, :].rearrange("p s h d -> p s (h d)"))
                    i.then_inc(S["o_ready"], 1)
                return fn

            def transpose_y(base):
                def fn(t, par):
                    pe.wait_ge(S["y_ready"], ATT[base] + t + 1)
                    pe.wait_ge(S["qk_ready"], ATT[base] + capped(t + L_OUT - 2, NT))
                    seen(pe, S["yts_ready"], ATT[base] + t)
                    nc.tensor.transpose(ps_a[:, 0:P], y[:, par, :], ident[:, :]).then_inc(S["yt_ready"], 1)
                return fn

            def out_project(base, l):
                def fn(t, par):
                    pe.wait_ge(S["yts_ready"], ATT[base] + t + 1)
                    pe.wait_ge(S["vbd_ready"], ATT[base] + capped(t + L_OUT - 2, NT))
                    seen(pe, S["x_updated"], UPD[base] + t)
                    if l is None:
                        i = mm(ps_v[:, 0:D], yts[:, par, :], wx[:, 3, :])
                    else:
                        mm(ps_v[:, 0:D], yts[:, par, :], wself[:, l, 3, :], True, False)
                        i = mm(ps_v[:, 0:D], ones_row[:, :], rows[:, R_BO + l * D:R_BO + (l + 1) * D], False, True)
                    i.then_inc(S["outp_ready"], 1)
                return fn

            def attention(base, l, nbase):
                early = [] if l is not None else [(1, ctx_transpose(base))]
                pipeline(pe, [(L_OUT, transpose_y(base)), (L_SCORES, scores(base, l is not None)),
                              (L_OUT, out_project(base, l)), (L_WEIGH, transpose_probs(base)),
                              (2, project(base, l))]
                             + early + [(1, transposes(base, nbase)), (L_WEIGH, weigh(base), VBUFS)])

            def logits_step(t, par):
                pe.wait_ge(S["xts_ready"], TB["p0"] + t + 1)
                seen(pe, S["logits_sb"], t)
                mm(ps_a[:, 0:NE], xts[:, par, :], gatew[:, 0, :], True, False)
                mm(ps_a[:, 0:NE], ones_row[:, :], rows[:, R_GB0:R_GB0 + NE], False, True
                   ).then_inc(S["logits_ps"], 1)

            def expert_block(l):
                def hidden(b, e):
                    for c in range(CH):
                        seen(pe, S["gelu_ready"], l * NB * NE * CH + b * (NE * CH) + (e - 1) * CH + c + 1)
                        mm((ps_s, ps_t)[c // 2][:, (c % 2) * BLK:(c % 2 + 1) * BLK], w1[:, e, c * P:(c + 1) * P],
                           h_t[:, bass.ds(b * BLK, BLK)]).then_inc(S["hid_ready"], 1)

                def second(b, e):
                    bank = (ps_o, ps_v)[e % 2]
                    seen(pe, S["acc_ready"], l * NB * NE + b * NE + (e - 1))
                    mm(bank[:, :], ones3[:, :], b2rows[:, e, :, :].rearrange("p s d -> p (s d)"), True, False)
                    for c in range(CH):
                        pe.wait_ge(S["gelu_ready"], l * NB * NE * CH + b * (NE * CH) + e * CH + c + 1)
                        for s in range(SUB):
                            i = mm(bank[:, s * D:(s + 1) * D], gel[:, e % 2, c, s * P:(s + 1) * P],
                                   w2[:, e, c, :], False, c == CH - 1)
                    i.then_inc(S["yexp_ready"], 1)

                def fn(b, par):
                    hidden(b, 0)
                    for e in range(NE):
                        if e + 1 < NE:
                            hidden(b, e + 1)
                        second(b, e)
                return fn

            attention("x", None, CROSS)
            for l in range(LAYERS):
                attention(l, l, (SELF0, SELF1)[l])
                steps = [(1, transposes(f"p{l}", (PRE0, PRE1)[l]))]
                if l == 0:
                    steps.insert(0, (3, logits_step))
                pipeline(pe, steps)
                if l == 1:
                    pe.wait_ge(S["hmean_ready"], 1)
                    mm(ps_a[0:NSEQ, 0:NE], hmean[:, :], gatew[:, 1, :]).then_inc(S["seqlog_ready"], 1)
                    pe.wait_ge(S["route_link"], ROUTE_AT(1, ROUTE_COUNTS))
                    mm(ps_a[0:NSEQ, 0:NE], before[:, :], counts[:, :])
                    mm(ps_a[:, NE:2 * NE], ones_seq[:, :], counts[:, :]).then_inc(S["place_ps"], 1)
                    pe.wait_ge(S["route_link"], ROUTE_AT(1, ROUTE_LINKS[1]))
                    nc.tensor.transpose(ps_o[0:NE, 0:NSEQ], cw[0:NSEQ, 0, :], ident[0:NSEQ, 0:NSEQ]
                                        ).then_inc(S["place_ps"], 1)
                    pe.wait_ge(S["place_link"], 1)
                    mm(ps_v[:, 0:NSEQ], b2w[:, :], cw_t[:, :]).then_inc(S["place_ps"], 1)
                    pe.wait_ge(S["place_link"], PLACE_TABLES)
                    for v in range(2):
                        for k in range(2):
                            i = mm(ps_x[:, v * PLACES:(v + 1) * PLACES], ones_seq[:, :], at_place[:, v, k, :],
                                   k == 0, k == 1)
                    i.then_inc(S["place_ps"], 1)
                    break
                pe.wait_ge(S["ffn_w_loaded"], 16 * 2)
                pe.wait_ge(S["route_done"], 1)
                pe.wait_ge(S["ht_stored"], NT)
                fn = expert_block(l)
                fn(0, 0)
                with pe.Fori(1, NB, 1) as b:
                    fn(b, 0)
                pe.wait_ge(S["acc_ready"], NB * NE)

            def pair_hidden(t, par):
                pe.wait_ge(S["hs_ready"], t + 1)
                pe.wait_ge(S["w1s_ready"], t + 1)
                seen(pe, S["pair_gelu"], t - 1)
                for c in range(CH):
                    i = mm(ps_s3[:, par, c * P:(c + 1) * P], w1s[:, par, c * P:(c + 1) * P], hs[:, par, :])
                i.then_inc(S["pair_hid"], 1)

            def pair_second(t, par):
                pe.wait_ge(S["pair_gelu"], t + 1)
                pe.wait_ge(S["w2s_ready"], t + 1)
                seen(pe, S["pair_added"], 2 * (t - 1))
                for c in range(CH):
                    i = mm((ps_o, ps_v)[par][:, 0:P], w2s[:, par, c * D:(c + 1) * D], gels[:, par, c * P:(c + 1) * P],
                           c == 0, c == CH - 1)
                i.then_inc(S["pair_out"], 1)
            pe.wait_ge(S["tables_ready"], 1)
            pipeline(pe, [(3, pair_second), (1, pair_hidden)], NPAIR)
            pe.wait_ge(S["pair_added"], 2 * NPAIR)
            for b in range(NB):
                seen(pe, S["rows_added"], b - 1)
                for k in range(SUB):
                    c = (b * SUB + k) * P
                    i = nc.tensor.transpose(ps_s3[:, b % 2, k * P:(k + 1) * P], inner[:, c:c + P], ident[:, :])
                i.then_inc(S["rows_ps"], 1)

            def gates_step(t, par):
                pe.wait_ge(S["xts_ready"], TB["m"] + t + 1)
                seen(pe, S["gates_sb"], t)
                for k, a in enumerate((xts, cts, cts)):
                    mm(ps_a[:, 0:16], a[:, par, :], wg_t[:, k, :], k == 0, False)
                mm(ps_a[:, 0:16], ones_row[:, :], rows[:, R_GI:R_GI + 16], False, True).then_inc(S["gates_ps"], 1)
            pipeline(pe, [(2, gates_step), (1, ctx_transpose("m")), (1, transposes("m", MLSTM))])
            pe.wait_ge(S["gate_link"], 2)
            mm(ps_v[:, 0:NT * MH], block_tri[:, :], lsig[:, :, :].rearrange("p t h -> p (t h)")
               ).then_inc(S["csum_ps"], 1)
            pe.wait_ge(S["avec_ready"], 1)

            def decay_step(t, par):
                pe.wait_ge(S["adiag_ready"], t + 1)
                seen(pe, S["shifted_ready"], ATT["m"] + t - 1)
                a = ps_t[:, par * 512:(par + 1) * 512]
                mm(a, identb[:, :], causal[:, :, :].rearrange("p a b -> p (a b)"), True, False)
                mm(a, block_ones[:, :], adiag[:, par, :, :].rearrange("p a b -> p (a b)"), False, True
                   ).then_inc(S["a_ready"], 1)

            def scores16(t, par):
                pe.wait_ge(S["qcopy_ready"], t + 1)
                pe.wait_ge(S["kbd_ready"], ATT["m"] + t + 1)
                seen(pe, S["ctil_ready"], t)
                for r_ in range(2):
                    i = mm(ps_s3[:, r_, 0:4 * SEQ], qbd[:, par, r_, :],
                           kbd[:, par, 2 * r_:2 * r_ + 2, :].rearrange("p a k -> p (a k)"))
                i.then_inc(S["scores_ready"], 1)

            def transpose_ctil(t, par):
                pe.wait_ge(S["ctil_ready"], t + 1)
                seen(pe, S["pts_ready"], ATT["m"] + t - 1)
                for j in range(MH // 2):
                    i = nc.tensor.transpose((ps_a, ps_x)[par][:, j * P:(j + 1) * P], ctil[:, par, j * P:(j + 1) * P],
                                            ident[:, :])
                i.then_inc(S["pt_ready"], 1)

            def weigh16(t, par):
                pe.wait_ge(S["pts_ready"], ATT["m"] + t + 1)
                pe.wait_ge(S["vb16_ready"], t + 1)
                seen(pe, S["o_stored"], t - 1)
                o = (ps_o, ps_v)[par][:, 0:SPT * MH * (MHD + 1)].rearrange("p (s n) -> p s n", s=SPT)
                for j in range(MH // 2):
                    a = 2 * j * (MHD + 1)
                    i = mm(o[:, :, a:a + 2 * (MHD + 1)], probs_t[:, par, j * P:(j + 1) * P],
                           vbd16[:, par, :, 2 * j:2 * j + 2, :].rearrange("p s h d -> p s (h d)"))
                i.then_inc(S["o_ready"], 1)
            pipeline(pe, [(7, weigh16), (5, transpose_ctil), (1, decay_step), (3, scores16)])

            pe.wait_ge(S["amax_ready"], 1)
            nc.tensor.transpose(ps_a[0:1, 0:P], amax[:, :], ident[:, :]).then_inc(S["amrow_ps"], 1)
            pe.wait_ge(S["scale_ready"], 1)
            mm(ps_v[:, 0:1], ones_row[:, :], am1[:, 0:1]).then_inc(S["scale_ps"], 1)

            def q8_transpose(t, par):
                pe.wait_ge(S["q8_ready"], t + 1)
                seen(pe, S["q8t_ready"], t - 1)
                for v in range(QT):
                    i = nc.tensor.transpose(q8ps[par][:, v * P:(v + 1) * P], q8[:, par, v * P:(v + 1) * P], identb[:, :])
                i.then_inc(S["q8t_ps"], 1)

            def q8_product(t, par):
                pe.wait_ge(S["q8t_ready"], t + 1)
                seen(pe, S["o1_ready"], t - 1)
                for v in range(QT):
                    i = mm((ps_o, ps_v)[par][:, v * D:(v + 1) * D], q8t[:, par, v * P:(v + 1) * P], w8t[:, :])
                i.then_inc(S["acc8_ready"], 1)
            pe.wait_ge(S["fin_link"], 4)
            pipeline(pe, [(4, q8_product), (2, q8_transpose)], NT // QT)

        @block.vector
        def _(dve):
            V = nc.vector
            dve.wait_ge(S["weights_loaded"], 16 * N_WLOADS)
            V.tensor_copy(w8f[:, :], w8[:, :].bitcast(I8)).then_inc(S["dve_setup"], 1)

            def split_b2():
                k = [0]

                def link(i):
                    k[0] += 1
                    i.then_inc(S["rs_link"], 1)
                    dve.wait_ge(S["rs_link"], k[0])
                link(V.tensor_copy(b2hi[:, :, :], b2src[:, :, :]))
                link(V.tensor_tensor(b2a[:, :, :], b2src[:, :, :], b2hi[:, :, :], ALU.subtract))
                link(V.tensor_copy(b2mid[:, :, :], b2a[:, :, :]))
                link(V.tensor_tensor(b2lo[:, :, :], b2a[:, :, :], b2mid[:, :, :], ALU.subtract))
                link(V.tensor_scalar(b2a[:, :, :], b2hi[:, :, :], row3[:, 0:1], None, ALU.mult))
                link(V.scalar_tensor_tensor(b2a[:, :, :], b2mid[:, :, :], row3[:, 1:2], b2a[:, :, :], ALU.mult, ALU.add))
                link(V.scalar_tensor_tensor(b2a[:, :, :], b2lo[:, :, :], row3[:, 2:3], b2a[:, :, :], ALU.mult, ALU.add))
                for s in range(SUB):
                    link(V.tensor_copy(b2rows[:, :, s, :], b2a[:, :, :]))
                assert k[0] == B2_LINKS
            dve.wait_ge(S["pool_const"], CONSTS[0])
            split_b2()
            dve.wait_ge(S["setup_copied"], 8)
            V.tensor_scalar(coef[:, 0:1], tg[:, 0:1], ROW0_PAIRS, None, ALU.mult).then_inc(S["dve_setup"], 1)
            V.tensor_scalar(rowb[:, 0:2 * D], rowb[:, 0:2 * D], tg[:, 1:2], None, ALU.mult).then_inc(S["dve_setup"], 1)
            V.tensor_scalar(rowb[:, 2 * D:4 * D], rowb[:, 2 * D:4 * D], tg[:, 3:4], None, ALU.mult
                            ).then_inc(S["dve_setup"], 1)
            dve.wait_ge(S["dve_setup"], 4)
            dve.wait_ge(S["x_loaded"], 16)
            dve.wait_ge(S["pool_const"], CONSTS[0])

            def sums_step(src, need=None, base=0):
                def sums(t, par):
                    if need:
                        dve.wait_ge(S[need], base + t + 1)
                    V.bn_stats(stats[:, bass.ds(t, 1), :].rearrange("p a s -> p (a s)"), tile(src, t)
                               ).then_inc(S["bn_done"], 1)
                return sums

            def row_stats(k):
                n = [STAT_LINKS * k]

                def link(i):
                    n[0] += 1
                    i.then_inc(S["stat_link"], 1)
                    dve.wait_ge(S["stat_link"], n[0])
                dve.wait_ge(S["bn_done"], NT * (k + 1))
                even, odd = stats[:, :, 1], stats[:, :, 4]
                link(V.tensor_tensor(half_gap[:, :], even, odd, ALU.subtract))
                link(V.tensor_tensor(mean[:, :], even, odd, ALU.add))
                link(V.tensor_scalar(mean[:, :], mean[:, :], 0.5, None, ALU.mult))
                link(V.scalar_tensor_tensor(half_gap[:, :], half_gap[:, :], 0.25, half_gap[:, :], ALU.mult, ALU.mult))
                link(V.tensor_tensor(var[:, :], stats[:, :, 2], stats[:, :, 5], ALU.add))
                link(V.scalar_tensor_tensor(var[:, :], var[:, :], 1.0 / D, half_gap[:, :], ALU.mult, ALU.add))
                V.tensor_scalar(vare[:, :], var[:, :], EPS, None, ALU.add).then_inc(S["vare_ready"], 1)
                assert n[0] == STAT_LINKS * (k + 1)
                dve.wait_ge(S["std_ready"], k + 1)
                V.reciprocal(rstd[:, :], std[:, :]).then_inc(S["rstd_ready"], 1)
                dve.wait_ge(S["rstd_ready"], k + 1)

            def norm_step(src, base, tb):
                def fn(t, par):
                    seen(dve, S["xt_ready"], TB[tb] + t - 1)
                    V.tensor_scalar(xn[:, par, :], tile(src, t), mean[:, bass.ds(t, 1)], rstd[:, bass.ds(t, 1)],
                                    ALU.subtract, ALU.mult).then_inc(S["xn_ready"], 1)
                return fn

            def vbd_step(base):
                def fn(t, par, slot):
                    dve.wait_ge(S["proj_ready"], ATT[base] + t + 1)
                    seen(dve, S["o_ready"], ATT[base] + t + 1 - VBUFS)
                    V.tensor_tensor(vbd[:, slot, :, :, 0:HD].rearrange("p s h d -> p (s h) d"),
                                    ps_v[:, 0:2 * D].rearrange("p (n d) -> p n d", d=HD), vmask[:, :, :],
                                    ALU.mult).then_inc(S["vbd_ready"], 1)
                return fn

            def shift_step(base):
                def fn(t, par):
                    dve.wait_ge(S["scores_ready"], ATT[base] + t + 1)
                    s3 = ps_s[:, :].rearrange("p (h k) -> p h k", k=SEQ)
                    V.tensor_reduce(rowmax[:, par, :], s3, AXX, ALU.max).then_inc(S["max_ready"], 1)
                    dve.wait_ge(S["max_ready"], ATT[base] + t + 1)
                    seen(dve, S["probs_ready"], ATT[base] + t - 1)
                    V.tensor_tensor(shifted[:, par, :].rearrange("p (h k) -> p h k", k=SEQ), s3,
                                    rowmax[:, par, :].unsqueeze(2).to_broadcast([P, HEADS, SEQ]), ALU.subtract
                                    ).then_inc(S["shifted_ready"], 1)
                return fn

            def y_step(base):
                def fn(t, par):
                    dve.wait_ge(S["o_ready"], ATT[base] + t + 1)
                    seen(dve, S["yt_ready"], ATT[base] + t - 1)
                    o = ps_o[:, 0:SPT * HEADS * (HD + 1)].rearrange("p (s h d) -> p s h d", s=SPT, h=HEADS)
                    for s in range(SPT):
                        r = slice(64 * s, 64 * s + 64)
                        i = V.reciprocal(recip[r, par, :].unsqueeze(2), o[r, s, :, HD:HD + 1])
                    i.then_inc(S["recip_ready"], 1)
                    dve.wait_ge(S["recip_ready"], ATT[base] + t + 1)
                    for s in range(SPT):
                        r = slice(64 * s, 64 * s + 64)
                        i = V.tensor_tensor(y[r, par, :].rearrange("p (h d) -> p h d", d=HD), o[r, s, :, 0:HD],
                                            recip[r, par, :].unsqueeze(2).to_broadcast([64, HEADS, HD]), ALU.mult)
                    i.then_inc(S["y_ready"], 1)
                return fn

            def add_step(base, dst, scale):
                def fn(t, par):
                    dve.wait_ge(S["outp_ready"], ATT[base] + t + 1)
                    V.scalar_tensor_tensor(tile(dst, t), ps_v[:, 0:D], scale, tile(dst, t), ALU.mult, ALU.add
                                           ).then_inc(S["x_updated"], 1)
                return fn

            def attention(base, src, nbase, scale):
                row_stats(nbase // NT)
                pipeline(dve, [(L_OUT - 1, y_step(base)), (3, vbd_step(base), VBUFS), (1, norm_step(src, nbase, base)),
                               (L_OUT, add_step(base, src, scale)), (L_SCORES, shift_step(base)),
                               (L_OUT + 1, sums_step(src, "x_updated", UPD[base]))])

            def plain_norm(src, dst, base, sums_too):
                def fn(t, par):
                    V.tensor_scalar(tile(dst, t), tile(src, t), mean[:, bass.ds(t, 1)], rstd[:, bass.ds(t, 1)],
                                    ALU.subtract, ALU.mult).then_inc(S["xn_ready"], 1)
                row_stats(base // NT)
                if sums_too:
                    pipeline(dve, [(0, fn), (1, sums_step(dst, "xn_ready", base))], unroll=8)
                else:
                    pipeline(dve, [(0, fn)], unroll=8)
                dve.wait_ge(S["xn_ready"], base + NT)

            def best_two(rows_, n, l):
                k = [ROUTE_AT(l, 0)]

                def link(i):
                    k[0] += 1
                    i.then_inc(S["route_link"], 1)
                    dve.wait_ge(S["route_link"], k[0])
                r = slice(0, rows_)
                lg, c1, c2 = logits[r, 0:n, :], cw[r, 0:n, :], oneh[r, 0:n, :]

                def wide(v):
                    return v[r, 0:n].unsqueeze(2).to_broadcast([rows_, n, NE])

                def first_best(best, hot):
                    link(V.tensor_reduce(best[r, 0:n], lg, AXX, ALU.max))
                    link(V.tensor_tensor(hot, lg, wide(best), ALU.is_equal))
                    link(V.scalar_tensor_tensor(cand[r, 0:n, :], hot, -float(NE), iota8[r, 0:n, :], ALU.mult, ALU.add))
                    link(V.tensor_reduce(first[r, 0:n], cand[r, 0:n, :], AXX, ALU.min))
                    link(V.tensor_tensor(hot, cand[r, 0:n, :], wide(first), ALU.is_equal))

                first_best(best1, c1)
                link(V.scalar_tensor_tensor(lg, c1, NEG, lg, ALU.mult, ALU.add))
                first_best(best2, c2)
                link(V.tensor_tensor(e21[r, 0:n], best2[r, 0:n], best1[r, 0:n], ALU.subtract))
                if l == 1:
                    link(V.tensor_copy(chosen[:, 0:1, :], c1))
                    link(V.tensor_copy(chosen[:, 1:2, :], c2))
                    link(V.tensor_tensor(counts[:, :].unsqueeze(1), c1, c2, ALU.add))
                dve.wait_ge(S["route_exp"], l + 1)
                link(V.tensor_scalar(tw2[r, 0:n], e21[r, 0:n], 1.0, None, ALU.add))
                link(V.reciprocal(tw1[r, 0:n], tw2[r, 0:n]))
                link(V.tensor_tensor(tw2[r, 0:n], e21[r, 0:n], tw1[r, 0:n], ALU.mult))
                link(V.tensor_tensor(c1, c1, wide(tw1), ALU.mult))
                link(V.tensor_tensor(c2, c2, wide(tw2), ALU.mult))
                i = V.tensor_tensor(c1, c1, c2, ALU.add)
                if l == 0:
                    i.then_inc(S["route_done"], 1)
                else:
                    link(i)
                assert k[0] == ROUTE_AT(l, ROUTE_LINKS[l])

            def top_step(t, par):
                dve.wait_ge(S["logits_ps"], t + 1)
                V.tensor_copy(logits[:, bass.ds(t, 1), :], ps_a[:, 0:NE].unsqueeze(1)).then_inc(S["logits_sb"], 1)

            def weigh_experts(l):
                def fn(b, par):
                    for e in range(NE):
                        bank = (ps_o, ps_v)[e % 2]
                        dve.wait_ge(S["yexp_ready"], l * NB * NE + b * NE + (e + 1))
                        seen(dve, S["acc_ready"], l * NB * NE + b * NE + e)
                        for s in range(SUB):
                            t = b * SUB + s
                            i = V.scalar_tensor_tensor(tile(inner, t), bank[:, s * D:(s + 1) * D],
                                                       cw[:, bass.ds(t, 1), e], tile(inner, t), ALU.mult, ALU.add)
                        i.then_inc(S["acc_ready"], 1)
                    dve.wait_ge(S["acc_ready"], b * NE + NE)
                    for s in range(SUB):
                        sums_step(inner)(b * SUB + s, 0)
                return fn

            pipeline(dve, [(0, sums_step(x_res))], unroll=8)
            attention("x", x_res, CROSS, coef[:, 0:1])
            plain_norm(x_res, inner, NORM0, True)
            for l in range(LAYERS):
                attention(l, inner, (SELF0, SELF1)[l], 1.0)
                dve.wait_ge(S["x_updated"], UPD[l] + NT)
                nb_ = (PRE0, PRE1)[l]
                row_stats(nb_ // NT)
                steps = [(0, norm_step(inner, nb_, f"p{l}"))]
                if l == 0:
                    steps.append((4, top_step))
                pipeline(dve, steps)
                if l == 0:
                    dve.wait_ge(S["logits_sb"], NT)
                    best_two(P, NT, 0)
                    dve.wait_ge(S["route_done"], 1)
                else:
                    dve.wait_ge(S["ht_stored"], 2 * NT)
                    V.tensor_reduce(hmean[:, :], h_t[:, :].rearrange("p (q i) -> p q i", i=SEQ), AXX, ALU.add
                                    ).then_inc(S["hmean_ready"], 1)
                    dve.wait_ge(S["seqlog_ready"], 1)
                    V.scalar_tensor_tensor(logits[0:NSEQ, 0, :], ps_a[0:NSEQ, 0:NE], 1.0 / SEQ,
                                           rowb[0:NSEQ, R_GB1:R_GB1 + NE], ALU.mult, ALU.add).then_inc(S["logits_sb"], 1)
                    dve.wait_ge(S["logits_sb"], NT + 1)
                    best_two(NSEQ, 1, 1)
                    break
                fn = weigh_experts(l)
                fn(0, 0)
                with dve.Fori(1, NB, 1) as b:
                    fn(b, 0)
                dve.wait_ge(S["acc_ready"], NB * NE)

            def make_tables():
                k = [0]

                def link(i):
                    k[0] += 1
                    i.then_inc(S["place_link"], 1)
                    dve.wait_ge(S["place_link"], k[0])
                dve.wait_ge(S["place_ps"], 2)
                link(V.tensor_copy(cw_t[:, :], ps_o[0:NE, 0:NSEQ]))
                link(V.tensor_scalar(tiles_of[:, :], ps_a[:, NE:2 * NE], 0.5, 0.25, ALU.mult, ALU.add))
                link(V.tensor_scalar(tiles_of[:, :], tiles_of[:, :], MAGIC, None, ALU.add))
                link(V.tensor_scalar(upto_a[:, NE:2 * NE], tiles_of[:, :], MAGIC, None, ALU.subtract))
                for src, dst, d in ((upto_a, upto_b, 1), (upto_b, upto_a, 2), (upto_a, upto_b, 4)):
                    link(V.tensor_tensor(dst[:, NE:2 * NE], src[:, NE:2 * NE], src[:, NE - d:2 * NE - d], ALU.add))
                link(V.scalar_tensor_tensor(place_base[:, :], upto_b[0:NSEQ, NE - 1:2 * NE - 1], 2.0,
                                            ps_a[0:NSEQ, 0:NE], ALU.mult, ALU.add))
                link(V.tensor_tensor(chosen_place[:, :, :], chosen[:, :, :],
                                     place_base[:, :].unsqueeze(1).to_broadcast([NSEQ, 2, NE]), ALU.mult))
                link(V.tensor_reduce(place[:, :], chosen_place[:, :, :], AXX, ALU.add))
                for c, w in enumerate((tw1, tw2)):
                    link(V.tensor_scalar(at_place[:, 0, c, :], place_no[:, :], place[:, c:c + 1], w[0:NSEQ, 0:1],
                                         ALU.is_equal, ALU.mult))
                    link(V.tensor_scalar(at_place[:, 1, c, :], place_no[:, :], place[:, c:c + 1], seq_col[:, :],
                                         ALU.is_equal, ALU.mult))
                assert k[0] == PLACE_TABLES
                link(V.tensor_tensor(past[:, :, :], pair_no[:, :, :],
                                     upto_b[0:1, NE:2 * NE].unsqueeze(1).to_broadcast([1, NPAIR, NE]), ALU.is_ge))
                link(V.tensor_reduce(expert_f[:, :], past[:, :, 0:NE - 1], AXX, ALU.add))
                link(V.tensor_copy(expert_of[:, :], expert_f[:, :]))
                link(V.scalar_tensor_tensor(x_res[:, :], inner[:, :], tg[:, 2:3], x_res[:, :], ALU.mult, ALU.add))
                dve.wait_ge(S["place_ps"], 3)
                link(V.tensor_copy(inner[:, :].rearrange("p (q i) -> p q i", i=SEQ),
                                   ps_v[:, 0:NSEQ].unsqueeze(2).to_broadcast([P, NSEQ, SEQ])))
                dve.wait_ge(S["place_ps"], 4)
                link(V.tensor_copy(place_w[:, :], ps_x[:, 0:PLACES]))
                V.tensor_copy(col_of[:, :], ps_x[0:1, PLACES:2 * PLACES]).then_inc(S["tables_ready"], 1)
                dve.wait_ge(S["tables_ready"], 1)
            make_tables()

            def first_weights(t, par):
                seen(dve, S["pair_gelu"], t - 1)
                e = dve.value_load(expert_of[0:1, bass.ds(t, 1)], min_val=0, max_val=NE - 1)
                V.tensor_copy(b1s[:, par, :], vec_t[:, bass.ds(e * CH + (14 + NE * CH), CH)])
                V.tensor_copy(w1s[:, par, :].unsqueeze(1), w1[:, bass.ds(e, 1), :]).then_inc(S["w1s_ready"], 1)

            def add_pair(t, par):
                dve.wait_ge(S["pair_out"], t + 1)
                for g in range(2):
                    q = dve.value_load(col_of[0:1, bass.ds(2 * t + g, 1)], min_val=0, max_val=TOK - SEQ)
                    seen(dve, S["pair_added"], 2 * t + g)
                    V.scalar_tensor_tensor(inner[:, bass.ds(q, SEQ)], (ps_o, ps_v)[par][:, g * SEQ:(g + 1) * SEQ],
                                           place_w[:, bass.ds(2 * t + g, 1)], inner[:, bass.ds(q, SEQ)], ALU.mult,
                                           ALU.add).then_inc(S["pair_added"], 1)
            dve.wait_ge(S["ffn_w_loaded"], 16 * 4)
            pipeline(dve, [(4, add_pair), (0, first_weights)], NPAIR)
            for b in range(NB):
                dve.wait_ge(S["rows_ps"], b + 1)
                c = slice(b * BLK, (b + 1) * BLK)
                V.scalar_tensor_tensor(x_res[:, c], ps_s3[:, b % 2, :], tg[:, 2:3], x_res[:, c], ALU.mult, ALU.add
                                       ).then_inc(S["rows_added"], 1)
            dve.wait_ge(S["rows_added"], NB)
            pipeline(dve, [(0, sums_step(x_res))], unroll=8)

            def gates_copy(t, par):
                dve.wait_ge(S["gates_ps"], t + 1)
                V.tensor_copy(gates[:, bass.ds(t, 1), :], ps_a[:, 0:16].unsqueeze(1)).then_inc(S["gates_sb"], 1)
            row_stats(MLSTM // NT)
            pipeline(dve, [(0, norm_step(x_res, MLSTM, "m")), (2, gates_copy)])
            dve.wait_ge(S["gates_sb"], NT)
            gi, gf = gates[:, :, 0:MH], gates[:, :, MH:2 * MH]
            V.scalar_tensor_tensor(gtmp[:, :, :], gf, -1.0, gf, ALU.mult, ALU.min).then_inc(S["gate_link"], 1)
            dve.wait_ge(S["gln_ready"], 1)
            V.scalar_tensor_tensor(lsig[:, :, :], gf, 0.0, gtmp[:, :, :], ALU.min, ALU.subtract
                                   ).then_inc(S["gate_link"], 1)
            dve.wait_ge(S["csum_ps"], 1)
            V.tensor_copy(csum[:, :, :].rearrange("p t h -> p (t h)"), ps_v[:, 0:NT * MH]).then_inc(S["gate_link"], 1)
            dve.wait_ge(S["gate_link"], 3)
            V.tensor_tensor(avec[:, :, :], gi, csum[:, :, :], ALU.subtract).then_inc(S["avec_ready"], 1)

            def decay_shift(t, par):
                dve.wait_ge(S["a_ready"], t + 1)
                a3 = ps_t[:, par * 512:(par + 1) * 512].rearrange("p (h k) -> p h k", k=SEQ)
                V.tensor_reduce(rowmax[:, par, 0:MH], a3, AXX, ALU.max).then_inc(S["max_ready"], 1)
                dve.wait_ge(S["max_ready"], ATT["m"] + t + 1)
                seen(dve, S["d_ready"], t - 1)
                V.tensor_copy(maxes[:, bass.ds(t, 1), :], rowmax[:, par:par + 1, 0:MH])
                V.tensor_tensor(shifted[:, par, 0:512].rearrange("p (h k) -> p h k", k=SEQ), a3,
                                rowmax[:, par, 0:MH].unsqueeze(2).to_broadcast([P, MH, SEQ]), ALU.subtract
                                ).then_inc(S["shifted_ready"], 1)

            def ctil_step(t, par):
                dve.wait_ge(S["d_ready"], t + 1)
                dve.wait_ge(S["scores_ready"], ATT["m"] + t + 1)
                seen(dve, S["pt_ready"], ATT["m"] + t - 1)
                V.tensor_tensor(ctil[:, par, :].rearrange("p (r n) -> p r n", r=2), ps_s3[:, :, 0:4 * SEQ],
                                probs[:, par, 0:512].rearrange("p (r n) -> p r n", r=2), ALU.mult
                                ).then_inc(S["ctil_ready"], 1)
            pipeline(dve, [(4, ctil_step), (2, decay_shift)])

            def head_norms():
                k = [0]

                def link(i):
                    k[0] += 1
                    i.then_inc(S["gn_link"], 1)
                    dve.wait_ge(S["gn_link"], k[0])

                def flat(a):
                    return a[:, :, :].rearrange("p t h -> p (t h)")

                def wide(a):
                    return flat(a).unsqueeze(2).to_broadcast([P, NT * MH, MHD])
                y3 = h_t[:, :].rearrange("p (n d) -> p n d", d=MHD)
                dve.wait_ge(S["shifted_ready"], ATT["m"] + NT)
                V.tensor_tensor(csum[:, :, :], csum[:, :, :], maxes[:, :, :], ALU.add).then_inc(S["negmd_ready"], 1)
                dve.wait_ge(S["o_stored"], NT)
                o3d = w12[:, 0:NT * MH * (MHD + 1)].rearrange("p (n d) -> p n d", d=MHD + 1)
                link(V.tensor_scalar(flat(avec).unsqueeze(2), o3d[:, :, MHD:MHD + 1], 0.25, None, ALU.mult))
                link(V.scalar_tensor_tensor(flat(avec), flat(avec), -1.0, flat(avec), ALU.mult, ALU.max))
                dve.wait_ge(S["emd_ready"], 1)
                link(V.tensor_tensor(flat(avec), flat(avec), flat(csum), ALU.max))
                link(V.tensor_scalar(flat(avec), flat(avec), 1e-6, 4.0, ALU.add, ALU.mult))
                link(V.reciprocal(flat(maxes), flat(avec)))
                link(V.tensor_tensor(y3, o3d[:, :, 0:MHD], wide(maxes), ALU.mult))
                V.tensor_reduce(flat(lsig), y3, AXX, ALU.add).then_inc(S["gate_link"], 1)
                dve.wait_ge(S["gate_link"], 4)
                link(V.scalar_tensor_tensor(y3, wide(lsig), -1.0 / MHD, y3, ALU.mult, ALU.add))
                assert k[0] == GN_CENTRED
                dve.wait_ge(S["square_ready"], 1)
                link(V.tensor_reduce(flat(lsig), inner[:, :].rearrange("p (n d) -> p n d", d=MHD), AXX, ALU.add))
                V.tensor_scalar(flat(lsig), flat(lsig), 1.0 / MHD, EPS, ALU.mult, ALU.add).then_inc(S["gve_ready"], 1)
                dve.wait_ge(S["gstd_ready"], 1)
                link(V.reciprocal(flat(gtmp), flat(gtmp)))
                link(V.tensor_tensor(y3, y3, wide(gtmp), ALU.mult))
                yt = h_t[:, :].rearrange("p (t d) -> p t d", d=D)
                x3 = x_res[:, :].rearrange("p (t d) -> p t d", d=D)
                link(V.tensor_tensor(yt, yt, rowb[:, R_GNW:R_GNW + D].unsqueeze(1).to_broadcast([P, NT, D]), ALU.mult))
                dve.wait_ge(S["xb_ready"], 1)
                V.tensor_tensor(x3, x3, yt, ALU.add).then_inc(S["x_updated"], 1)
            head_norms()

            dve.wait_ge(S["x_updated"], UPD["m"] + 1)
            pipeline(dve, [(0, sums_step(x_res))], unroll=8)
            plain_norm(x_res, inner, NORM1, False)
            V.tensor_reduce(xscale[:, 0:1], inner[:, :], AXX, ALU.min).then_inc(S["fin_link"], 1)
            V.tensor_reduce(xscale[:, 1:2], inner[:, :], AXX, ALU.max).then_inc(S["fin_link"], 1)
            dve.wait_ge(S["fin_link"], 2)
            V.scalar_tensor_tensor(amax[:, :], xscale[:, 0:1], -1.0, xscale[:, 1:2], ALU.mult, ALU.max
                                   ).then_inc(S["amax_ready"], 1)
            dve.wait_ge(S["amrow_done"], 1)
            V.tensor_reduce(am1[:, 1:2], amrow[:, :], AXX, ALU.max).then_inc(S["fin_link"], 1)
            dve.wait_ge(S["fin_link"], 3)
            V.tensor_scalar(am1[:, 0:1], am1[:, 1:2], 1.0 / 127.0, EPS, ALU.mult, ALU.max).then_inc(S["scale_ready"], 1)
            dve.wait_ge(S["scale_ps"], 1)
            V.tensor_copy(xscale[:, 0:1], ps_v[:, 0:1]).then_inc(S["fin_link"], 1)
            dve.wait_ge(S["fin_link"], 4)
            V.reciprocal(xscale[:, 1:2], xscale[:, 0:1]).then_inc(S["fin_link"], 1)
            dve.wait_ge(S["fin_link"], 5)

            def quantise(t, par):
                seen(dve, S["q8_ready"], t - 1)
                V.tensor_scalar(qa[:, par, :], inner[:, bass.ds(t * QW, QW)], xscale[:, 1:2], -128.0, ALU.mult, ALU.max
                                ).then_inc(S["fin_link"], 1)
                dve.wait_ge(S["fin_link"], 5 + t + 1)
                V.tensor_scalar(qb[:, par, :], qa[:, par, :], 127.0, MAGIC, ALU.min, ALU.add).then_inc(S["qb_ready"], 1)

            def dequantise(t, par):
                dve.wait_ge(S["acc8_ready"], t + 1)
                seen(dve, S["o3_ready"], t - 1)
                V.scalar_tensor_tensor(o1[:, par, :].rearrange("p (v d) -> p v d", v=QT),
                                       (ps_o, ps_v)[par][:, 0:QW].rearrange("p (v d) -> p v d", v=QT), xscale[:, 0:1],
                                       rowb[:, R_WS:R_WS + D].unsqueeze(1).to_broadcast([P, QT, D]), ALU.mult, ALU.mult
                                       ).then_inc(S["o1_ready"], 1)
            pipeline(dve, [(5, dequantise), (0, quantise)], NT // QT)


_INS = ['x', 'ctx_1024', 'g_xattn', 'g_ffn', 'L0_xattn_Wq', 'L0_xattn_Wk', 'L0_xattn_Wv', 'L0_xattn_Wo',
        'L0_ffn_ln1_w', 'L0_ffn_ln1_b', 'L0_ffn_ln2_w', 'L0_ffn_ln2_b', 'L0_ffn_wq', 'L0_ffn_wk', 'L0_ffn_wv',
        'L0_ffn_wo', 'L0_ffn_bq', 'L0_ffn_bk', 'L0_ffn_bv', 'L0_ffn_bo', 'L0_ffn_gate_w', 'L0_ffn_gate_b',
        'L0_ffn_e_w1', 'L0_ffn_e_b1', 'L0_ffn_e_w2', 'L0_ffn_e_b2', 'L1_xattn_Wi_w', 'L1_xattn_Wi_b',
        'L1_xattn_Wf_w', 'L1_xattn_Wf_b', 'L1_xattn_gn_w', 'L1_xattn_gn_b', 'L1_ffn_weight_int8',
        'L1_ffn_weight_scale', 'L1_ffn_bias']


def kernel(**inputs):
    import numpy as _np
    import concourse.bacc as _bacc
    from concourse import mybir as _mybir
    from concourse.bass_utils import run_bass_kernel_spmd as _run

    nc = _bacc.Bacc("TRN2", target_bir_lowering=False, num_devices=1)
    arrays, args = {}, {}
    for name in _INS:
        a = _np.ascontiguousarray(inputs[name])
        if a.dtype == _np.int8:
            a = a.view(_np.int32)
        arrays[f"in_{name}_dram"] = a
        args[name] = nc.dram_tensor(f"in_{name}_dram", a.shape, _mybir.dt.from_np(a.dtype), kind="ExternalInput").ap()
    out = nc.dram_tensor("out_0_dram", (NSEQ, SEQ, D), _mybir.dt.float32, kind="ExternalOutput").ap()
    build(nc, args, out)
    r = _run(nc, [arrays], core_ids=[0])
    return r.results[0]["out_0_dram"]
```
